# Optimizing a Trainium2 kernel written in Bass

```python
import numpy as np
import jax
import jax.numpy as jnp

def _softmax(x, axis=-1):
    return jax.nn.softmax(x, axis=axis)

def _gelu(x):
    return jax.nn.gelu(x, approximate=True)

def _silu(x):
    return jax.nn.silu(x)

def _sigmoid(x):
    return jax.nn.sigmoid(x)

def _layernorm(x, axis=-1, eps=1e-05):
    m = jnp.mean(x, axis=axis, keepdims=True)
    v = jnp.var(x, axis=axis, keepdims=True)
    return (x - m) / jnp.sqrt(v + eps)

def _scatter_add(tgt, idx, src, axis=0):
    return tgt.at[idx].add(src)

def _segment_sum(src, seg, n):
    return jax.ops.segment_sum(src, seg, n)
kernel_name = 'mk_flamingo_gated_d2_seqx_r4_5cc3b9'

def setup_inputs(seed: int=0):
    np.random.seed(seed)
    _w = jnp.asarray

    def _rec_inputs():
        import jax
        import jax.numpy as jnp
        _rk = jax.random.key(seed)
        x = -0.0002928 + 1 * jax.random.normal(jax.random.fold_in(_rk, 1), (2, 1024, 256), jnp.float32)
        _lenS = 1024 - jax.random.randint(jax.random.fold_in(_rk, 7), (2,), 0, max(1, 1024 // 4) + 1, jnp.int32)
        _lenS2 = 77 - jax.random.randint(jax.random.fold_in(_rk, 8), (2,), 0, max(1, 77 // 4) + 1, jnp.int32)
        _ctx_1024P = jax.random.normal(jax.random.fold_in(_rk, 11), (2, 16, 256), jnp.float32)
        _ctx_1024c = jax.random.dirichlet(jax.random.fold_in(_rk, 511), 0.3 * jnp.ones((16,), jnp.float32), (2, 77))
        _ctx_1024t = jnp.einsum('bsk,bkd->bsd', _ctx_1024c, _ctx_1024P)
        _ctx_1024t = _ctx_1024t * jax.lax.rsqrt(jnp.mean(jnp.square(_ctx_1024t)) + 1e-12) * 0.953939
        ctx_1024 = -1.39393e-06 + 0.999914 * (_ctx_1024t + 0.3 * jax.random.normal(jax.random.fold_in(_rk, 611), (2, 77, 256), jnp.float32))
        fside_Bx16xSxS2_0 = 9.80324e-05 + 1.00009 * jax.random.normal(jax.random.fold_in(_rk, 12), (2, 16, 1024, 77), jnp.float32)
        _validS = jnp.arange(1024)[None, :] < _lenS[:, None]
        _validS2 = jnp.arange(77)[None, :] < _lenS2[:, None]
        _causal = jnp.tril(jnp.ones((1024, 1024), dtype=bool))
        mask_BxS2_bf0 = jnp.logical_not(jnp.ones((2, 77), dtype=bool))
        _g = jax.random.normal(jax.random.fold_in(_rk, 9001), (2, 2), jnp.float32)
        _g = jnp.sign(_g) * jnp.maximum(jnp.abs(_g), 1.0) + (_g == 0) * 1.0
        g_xattn = _g[0]
        g_ffn = _g[1]
        return (x, ctx_1024, fside_Bx16xSxS2_0, mask_BxS2_bf0, g_xattn, g_ffn)
    x, ctx_1024, fside_Bx16xSxS2_0, mask_BxS2_bf0, g_xattn, g_ffn = _rec_inputs()

    def _L0_xattn_setup():
        import jax, jax.numpy as jnp
        import numpy as np
        B, T, D, H = (2, 512, 256, 16)
        HD = D // H
        key = jax.random.key(seed)
        ks = jax.random.split(key, 12)
        s = D ** (-0.5)
        return {'query': jax.random.normal(ks[0], (B, T, D), jnp.float32), 'key': jax.random.normal(ks[1], (B, T, D), jnp.float32), 'value': jax.random.normal(ks[2], (B, T, D), jnp.float32), 'attn_bias': jax.random.normal(ks[3], (B, H, T, T), jnp.float32), 'key_padding_mask': jnp.zeros((B, T), dtype=bool), 'wq': jax.random.normal(ks[4], (D, D), jnp.float32) * s, 'bq': jnp.zeros((D,), jnp.float32), 'wk': jax.random.normal(ks[5], (D, D), jnp.float32) * s, 'bk': jnp.zeros((D,), jnp.float32), 'wv': jax.random.normal(ks[6], (D, D), jnp.float32) * s, 'bv': jnp.zeros((D,), jnp.float32), 'wo': jax.random.normal(ks[7], (D, D), jnp.float32) * s, 'bo': jnp.zeros((D,), jnp.float32)}
    _L0_xattn_all = _L0_xattn_setup()
    _L0_xattn_in = {k: v for k, v in _L0_xattn_all.items() if k in ('wq', 'bq', 'wk', 'bk', 'wv', 'bv', 'wo', 'bo')}
    del _L0_xattn_all

    def _L0_ffn_setup():
        import jax, jax.numpy as jnp
        import numpy as np
        D_MODEL = 256
        D_FF = 1024
        NUM_EXPERTS = 8
        key = jax.random.key(seed)
        ks = jax.random.split(key, 8)
        scale_in = 1.0 / np.sqrt(D_MODEL)
        scale_ff = 1.0 / np.sqrt(D_FF)
        x = jax.random.normal(ks[0], (4, 512, D_MODEL), dtype=jnp.float32)
        gate_w = jax.random.uniform(ks[1], (NUM_EXPERTS, D_MODEL), jnp.float32, -scale_in, scale_in)
        gate_b = jax.random.uniform(ks[2], (NUM_EXPERTS,), jnp.float32, -scale_in, scale_in)
        expert_bias = jnp.zeros((NUM_EXPERTS,), dtype=jnp.float32)
        w1 = jax.random.uniform(ks[3], (NUM_EXPERTS, D_MODEL, D_FF), jnp.float32, -scale_in, scale_in)
        b1 = jax.random.uniform(ks[4], (NUM_EXPERTS, D_FF), jnp.float32, -scale_in, scale_in)
        w2 = jax.random.uniform(ks[5], (NUM_EXPERTS, D_FF, D_MODEL), jnp.float32, -scale_ff, scale_ff)
        b2 = jax.random.uniform(ks[6], (NUM_EXPERTS, D_MODEL), jnp.float32, -scale_ff, scale_ff)
        return {'x': x, 'gate_w': gate_w, 'gate_b': gate_b, 'expert_bias': expert_bias, 'w1': w1, 'b1': b1, 'w2': w2, 'b2': b2}
    _L0_ffn_all = _L0_ffn_setup()
    _L0_ffn_in = {k: v for k, v in _L0_ffn_all.items() if k in ('gate_w', 'gate_b', 'expert_bias', 'w1', 'b1', 'w2', 'b2')}
    del _L0_ffn_all

    def _L1_xattn_setup():
        import jax, jax.numpy as jnp
        import numpy as np
        D_MODEL = 256
        NUM_HEADS = 16
        HEAD_DIM = D_MODEL // NUM_HEADS
        B, S = (2, 512)

        def _split_heads(x):
            b, s, _ = x.shape
            return x.reshape(b, s, NUM_HEADS, HEAD_DIM).transpose(0, 2, 1, 3)
        key = jax.random.key(seed)
        ks = jax.random.split(key, 11)
        scale = 1.0 / np.sqrt(D_MODEL)
        inp = {'Q': jax.random.normal(ks[0], (B, S, D_MODEL), jnp.float32), 'K': jax.random.normal(ks[1], (B, S, D_MODEL), jnp.float32), 'V': jax.random.normal(ks[2], (B, S, D_MODEL), jnp.float32), 'Wq': jax.random.normal(ks[3], (D_MODEL, D_MODEL), jnp.float32) * scale, 'bq': jax.random.normal(ks[4], (D_MODEL,), jnp.float32) * scale, 'Wk': jax.random.normal(ks[5], (D_MODEL, D_MODEL), jnp.float32) * scale, 'bk': jax.random.normal(ks[6], (D_MODEL,), jnp.float32) * scale, 'Wv': jax.random.normal(ks[7], (D_MODEL, D_MODEL), jnp.float32) * scale, 'bv': jax.random.normal(ks[8], (D_MODEL,), jnp.float32) * scale, 'Wo': jax.random.normal(ks[9], (D_MODEL, D_MODEL), jnp.float32) * scale, 'bo': jax.random.normal(ks[10], (D_MODEL,), jnp.float32) * scale}
        return inp
    _L1_xattn_all = _L1_xattn_setup()
    _L1_xattn_in = {k: v for k, v in _L1_xattn_all.items() if k in ('Wq', 'bq', 'Wk', 'bk', 'Wv', 'bv', 'Wo', 'bo')}
    del _L1_xattn_all

    def _L1_ffn_setup():
        import jax, jax.numpy as jnp
        import numpy as np
        B, N, D = (4, 512, 256)
        SPARSITY = 0.01
        key = jax.random.key(seed)
        k1, k2, k3 = jax.random.split(key, 3)
        x = jax.random.normal(k1, (B, N, D), dtype=jnp.float32)
        spatial = jax.random.normal(k2, (D, D), dtype=jnp.float32) * 0.02
        freq = jnp.fft.fft(spatial, axis=-1)
        k = int(D * SPARSITY)
        mag = jnp.abs(freq)
        kth = jax.lax.top_k(mag, k)[0][:, -1:]
        w_sparse = jnp.where(mag >= kth, freq, 0.0 + 0j)
        bias = jax.random.normal(k3, (D,), dtype=jnp.float32) * 0.01
        return {'x': x, 'w_freq_real': jnp.real(w_sparse).astype(jnp.float32), 'w_freq_imag': jnp.imag(w_sparse).astype(jnp.float32), 'bias': bias}
    _L1_ffn_all = _L1_ffn_setup()
    _L1_ffn_in = {k: v for k, v in _L1_ffn_all.items() if k in ('w_freq_real', 'w_freq_imag', 'bias')}
    del _L1_ffn_all
    return {'x': x, 'ctx_1024': ctx_1024, 'fside_Bx16xSxS2_0': fside_Bx16xSxS2_0, 'mask_BxS2_bf0': mask_BxS2_bf0, 'g_xattn': g_xattn, 'g_ffn': g_ffn, 'L0_xattn_wq': _L0_xattn_in['wq'], 'L0_xattn_bq': _L0_xattn_in['bq'], 'L0_xattn_wk': _L0_xattn_in['wk'], 'L0_xattn_bk': _L0_xattn_in['bk'], 'L0_xattn_wv': _L0_xattn_in['wv'], 'L0_xattn_bv': _L0_xattn_in['bv'], 'L0_xattn_wo': _L0_xattn_in['wo'], 'L0_xattn_bo': _L0_xattn_in['bo'], 'L0_ffn_gate_w': _L0_ffn_in['gate_w'], 'L0_ffn_gate_b': _L0_ffn_in['gate_b'], 'L0_ffn_expert_bias': _L0_ffn_in['expert_bias'], 'L0_ffn_w1': _L0_ffn_in['w1'], 'L0_ffn_b1': _L0_ffn_in['b1'], 'L0_ffn_w2': _L0_ffn_in['w2'], 'L0_ffn_b2': _L0_ffn_in['b2'], 'L1_xattn_Wq': _L1_xattn_in['Wq'], 'L1_xattn_bq': _L1_xattn_in['bq'], 'L1_xattn_Wk': _L1_xattn_in['Wk'], 'L1_xattn_bk': _L1_xattn_in['bk'], 'L1_xattn_Wv': _L1_xattn_in['Wv'], 'L1_xattn_bv': _L1_xattn_in['bv'], 'L1_xattn_Wo': _L1_xattn_in['Wo'], 'L1_xattn_bo': _L1_xattn_in['bo'], 'L1_ffn_w_freq_real': _L1_ffn_in['w_freq_real'], 'L1_ffn_w_freq_imag': _L1_ffn_in['w_freq_imag'], 'L1_ffn_bias': _L1_ffn_in['bias']}

def reference(x, ctx_1024, fside_Bx16xSxS2_0, mask_BxS2_bf0, g_xattn, g_ffn, L0_xattn_wq, L0_xattn_bq, L0_xattn_wk, L0_xattn_bk, L0_xattn_wv, L0_xattn_bv, L0_xattn_wo, L0_xattn_bo, L0_ffn_gate_w, L0_ffn_gate_b, L0_ffn_expert_bias, L0_ffn_w1, L0_ffn_b1, L0_ffn_w2, L0_ffn_b2, L1_xattn_Wq, L1_xattn_bq, L1_xattn_Wk, L1_xattn_bk, L1_xattn_Wv, L1_xattn_bv, L1_xattn_Wo, L1_xattn_bo, L1_ffn_w_freq_real, L1_ffn_w_freq_imag, L1_ffn_bias):
    import jax
    import jax.numpy as jnp

    def _L0_xattn_ref(query, key, value, attn_bias, key_padding_mask, wq, bq, wk, bk, wv, bv, wo, bo):
        import jax, jax.numpy as jnp
        import numpy as np
        B, T, D, H = (2, 512, 256, 16)
        HD = D // H
        b, t, d = query.shape
        q = (query @ wq.T + bq).reshape(b, t, H, HD).transpose(0, 2, 1, 3)
        k = (key @ wk.T + bk).reshape(b, -1, H, HD).transpose(0, 2, 1, 3)
        v = (value @ wv.T + bv).reshape(b, -1, H, HD).transpose(0, 2, 1, 3)
        q = q * HD ** (-0.5)
        scores = jnp.einsum('bhqd,bhkd->bhqk', q, k) + attn_bias
        s = scores.shape[-1]
        causal = jnp.triu(jnp.ones((t, s), dtype=bool), k=1)
        neg_inf = jnp.float32(-jnp.inf)
        scores = jnp.where(causal, neg_inf, scores)
        scores = jnp.where(key_padding_mask[:, None, None, :], neg_inf, scores)
        attn = jax.nn.softmax(scores, axis=-1)
        out = jnp.einsum('bhqk,bhkd->bhqd', attn, v)
        out = out.transpose(0, 2, 1, 3).reshape(b, t, d)
        return out @ wo.T + bo

    def _L0_ffn_ref(x, gate_w, gate_b, expert_bias, w1, b1, w2, b2):
        import jax, jax.numpy as jnp
        import numpy as np
        D_MODEL = 256
        D_FF = 1024
        NUM_EXPERTS = 8
        gate_logits = jnp.einsum('bsd,ed->bse', x, gate_w) + gate_b + expert_bias
        top_idx = jnp.argmax(gate_logits, axis=-1)
        out = jnp.zeros_like(x)
        for e in range(NUM_EXPERTS):
            mask = (top_idx == e)[..., None].astype(x.dtype)
            h = jax.nn.relu(jnp.einsum('bsd,df->bsf', x, w1[e]) + b1[e])
            y = jnp.einsum('bsf,fd->bsd', h, w2[e]) + b2[e]
            out = out + mask * y
        return out

    def _L1_xattn_ref(Q, K, V, Wq, bq, Wk, bk, Wv, bv, Wo, bo):
        import jax, jax.numpy as jnp
        import numpy as np
        D_MODEL = 256
        NUM_HEADS = 16
        HEAD_DIM = D_MODEL // NUM_HEADS
        B, S = (2, 512)

        def _split_heads(x):
            b, s, _ = x.shape
            return x.reshape(b, s, NUM_HEADS, HEAD_DIM).transpose(0, 2, 1, 3)
        q = _split_heads(Q @ Wq + bq)
        k = _split_heads(K @ Wk + bk)
        v = _split_heads(V @ Wv + bv)
        scores = jnp.einsum('bhqd,bhkd->bhqk', q, k) / jnp.sqrt(jnp.asarray(HEAD_DIM, q.dtype))
        attn = jax.nn.softmax(scores, axis=-1)
        out = jnp.einsum('bhqk,bhkd->bhqd', attn, v)
        out = out.transpose(0, 2, 1, 3).reshape(Q.shape[0], -1, D_MODEL)
        return out @ Wo + bo

    def _L1_ffn_ref(x, w_freq_real, w_freq_imag, bias):
        import jax, jax.numpy as jnp
        import numpy as np
        B, N, D = (4, 512, 256)
        SPARSITY = 0.01
        w = jax.lax.complex(w_freq_real, w_freq_imag)
        x_freq = jnp.fft.fft(x, axis=-1)
        y_freq = jnp.einsum('bnd,do->bno', x_freq, w)
        y = jnp.real(jnp.fft.ifft(y_freq, axis=-1))
        return y + bias
    x = x + jnp.tanh(g_xattn[0]) * _L0_xattn_ref(_layernorm(x, axis=-1), ctx_1024, ctx_1024, fside_Bx16xSxS2_0, mask_BxS2_bf0, L0_xattn_wq, L0_xattn_bq, L0_xattn_wk, L0_xattn_bk, L0_xattn_wv, L0_xattn_bv, L0_xattn_wo, L0_xattn_bo)
    x = x + jnp.tanh(g_ffn[0]) * _L0_ffn_ref(_layernorm(x, axis=-1), L0_ffn_gate_w, L0_ffn_gate_b, L0_ffn_expert_bias, L0_ffn_w1, L0_ffn_b1, L0_ffn_w2, L0_ffn_b2)
    x = x + jnp.tanh(g_xattn[1]) * _L1_xattn_ref(_layernorm(x, axis=-1), ctx_1024, ctx_1024, L1_xattn_Wq, L1_xattn_bq, L1_xattn_Wk, L1_xattn_bk, L1_xattn_Wv, L1_xattn_bv, L1_xattn_Wo, L1_xattn_bo)
    x = x + jnp.tanh(g_ffn[1]) * _L1_ffn_ref(_layernorm(x, axis=-1), L1_ffn_w_freq_real, L1_ffn_w_freq_imag, L1_ffn_bias)
    return x

_drawn_inputs = setup_inputs


def setup_inputs(seed=0):
    import zlib

    import numpy as np

    out = dict(_drawn_inputs(seed))
    spreads = {'g_ffn': (-1.0, 0.2),
     'L0_xattn_bq': (0.0, 0.1),
     'L0_xattn_bk': (0.0, 0.8),
     'L0_xattn_bv': (0.0, 0.1),
     'L0_xattn_bo': (0.0, 0.1),
     'L0_ffn_expert_bias': (0.0, 0.1)}
    factors = {'L0_ffn_b1': 6.076,
     'L0_ffn_b2': 4.902,
     'L1_xattn_bq': 4.686,
     'L1_xattn_bk': 8.0,
     'L1_ffn_bias': 8.0}
    for name, (base, spread) in spreads.items():
        noise = np.random.default_rng([zlib.crc32(name.encode()), seed]).standard_normal(out[name].shape)
        drawn = base * np.exp(spread * noise) if base else spread * noise
        out[name] = jnp.asarray(drawn.astype(out[name].dtype))
    for name, factor in factors.items():
        out[name] = (out[name] * factor).astype(out[name].dtype)
    return out
```

```python
from contextlib import ExitStack

import concourse.bass as bass
from concourse import mybir

ALU = mybir.AluOpType
ACT = mybir.ActivationFunctionType
AX_X = mybir.AxisListType.X
F32 = mybir.dt.float32
U32 = mybir.dt.uint32
I32 = mybir.dt.int32
U8 = mybir.dt.uint8

P = 128
B, S, D = 2, 1024, 256
KEYS = 77
HEADS, HD = 16, 16
NJ = S // P
NT = B * NJ
DC = D // P
QH = 4
QK = QH * KEYS
TW = 104
NW = 3
QP = NW * TW
VC = QH * (HD + 1)
NE, FF = 8, 1024
FC = FF // P
MT = NT + NE - 1
LAG_T, LAG_V = 2, 3
UNITS = 2 * NT
EPS = 1e-5
MASKED = -1e38

C_ID, C_TRI, C_KM, C_VM = 0, 128, 256, 260
C_RANK, C_LAST, C_RESET, C_THR, C_TILE = 272, 280, 288, 416, 432
C_SMALL = 456
C_CAUSAL = C_SMALL
C_ALL = C_CAUSAL + NJ * KEYS


def flamingo_kernel(nc, a, out):
    with ExitStack() as ctx:
        def sb(name, shape, dt=F32):
            return ctx.enter_context(nc.sbuf_tensor(name, shape, dt))

        def sem(name):
            return ctx.enter_context(nc.semaphore(name))

        def dram(name, shape):
            return nc.dram_tensor(name, shape, F32, kind="Internal").ap()

        w1_sb = sb("w1_sb", [P, NE * DC * FF])
        wide = sb("wide", [P, B * HEADS * NJ * KEYS])
        x_sb = sb("x_sb", [P, NT, D])
        s_sb = sb("s_sb", [P, 4, 2, QP])
        pt_sb = sb("pt_sb", [P, 2, 2, NW * P])
        xn_sb = sb("xn_sb", [P, B, D])
        xnT_sb = sb("xnT_sb", [P, DC, P])
        qT_sb = sb("qT_sb", [P, B, DC, P])
        on_sb = sb("on_sb", [P, B, D])
        oT_sb = sb("oT_sb", [P, B, DC, P])
        b2t_sb = sb("b2t_sb", [P, D])
        kbd = sb("kbd", [P, DC, B, QH, KEYS])
        vblk = sb("vblk", [P, B, NW, HEADS // QH, QH, HD + 1])
        wq_sb = sb("wq_sb", [P, DC, D])
        wo_sb = sb("wo_sb", [P, DC, D])
        m_sb = sb("m_sb", [P, DC, D])
        cst = sb("cst", [P, C_SMALL])
        rows = sb("rows", [P, 4, D])
        mx_sb = sb("mx_sb", [P, 4, 8])
        rs_sb = sb("rs_sb", [P, HEADS])
        no_key = sb("no_key", [P, NT])
        stats = sb("stats", [P, NT, 6])
        mv = sb("mv", [P, NT, 2])
        rstd = sb("rstd", [P, NT])
        power = sb("power", [P, NT])
        cols = sb("cols", [P, 8])
        tg = sb("tg", [P, 4])
        b1T = sb("b1T", [P, NE * FC])
        gwT = sb("gwT", [P, DC, NE])
        gb = sb("gb", [P, 2, NE])
        slot_u = sb("slot_u", [P, NT], U32)
        tile_e = sb("tile_e", [P, MT + 1], I32)


        last_w1 = (NE - 1) * DC * FF
        pen = w1_sb[:, last_w1:last_w1 + B * NJ * KEYS].rearrange("p (b j k) -> p b j k", b=B, j=NJ)
        st0 = 5 * DC * FF

        def mat(t, at):
            return t[:, at:at + DC * D].rearrange("p (c n) -> p c n", c=DC)

        raw = [mat(w1_sb, st0 + 512 * i) for i in range(4)]
        wkT, wvT = mat(w1_sb, st0 + 2048), mat(w1_sb, st0 + 2560)
        causal = w1_sb[:, st0 + 3072:st0 + 3072 + NJ * KEYS].rearrange("p (j k) -> p j k", j=NJ)
        padraw = w1_sb[:, st0 + 3712:st0 + 3712 + 64].bitcast(U8)[:, 0:B * KEYS].rearrange("p (b k) -> p b k", b=B)
        padrow = w1_sb[:, st0 + 3776:st0 + 3776 + B * KEYS].rearrange("p (b k) -> p b k", b=B)
        PAIR = B * HEADS * 2 * KEYS
        w2_sb = wide[:, 0:NE * FC * D]
        XN0 = NJ // 2 * PAIR - NT * D
        xn_all = wide[:, XN0:XN0 + NT * D].rearrange("p (t d) -> p t d", d=D)
        y_all = xn_all
        wk1, wv1 = mat(wide, (NE - 1) * FC * D), mat(wide, (NE - 1) * FC * D + 512)
        flat = s_sb[:, :, :, :].rearrange("p a b c -> p (a b c)")
        ptf = pt_sb[:, :, :, :].rearrange("p a b c -> p (a b c)")
        ctx_sb = flat[0:KEYS, 0:B * D].rearrange("p (b d) -> p b d", b=B)
        ctxT = ptf[:, 0:DC * B * QP].rearrange("p (c b k) -> p c b k", c=DC, b=B)
        ctxT_heads = [ptf[:, 0:DC * B * QP].rearrange("p (cb k) -> p cb k", cb=DC * B)[:, :, KEYS * r:KEYS * r + KEYS]
                      for r in range(QH)]
        ctxT_pad = ptf[:, 0:DC * B * QP].rearrange("p (cb k) -> p cb k", cb=DC * B)[:, :, QK:QP]
        kb_sb = flat[:, 512:512 + DC * B * KEYS].rearrange("p (c b k) -> p c b k", c=DC, b=B)
        vb_sb = flat[:, 1024:1024 + 2 * D].rearrange("p (i d) -> p i d", i=2)
        dft = [mat(flat, 512 * i) for i in range(3)]
        wfr = on_sb[:, :, :]
        wfi = oT_sb[:, :, :, :].rearrange("p b c n -> p b (c n)")
        arT = xn_sb[:, :, :]
        aiT = qT_sb[:, :, :, :].rearrange("p b c n -> p b (c n)")
        xs_sb, xsT_sb = xn_sb[:, 0, :], xnT_sb
        h_sb = flat[:, 0:FF]
        hT_sb = ptf[:, 0:FF].rearrange("p (c t) -> p c t", c=FC)
        y_sb = flat[:, FF:FF + D]
        b1_raw = flat[0:NE * FC, 1600:1600 + P]
        gw_raw = flat[0:NE, 1728:1728 + D]
        s_pad = flat.rearrange("p (a n) -> p a n", n=QP)[:, :, QK:QP]
        rt = w1_sb[:, last_w1:last_w1 + 2048].rearrange("p (i n) -> p i n", n=P)

        score_ps = ctx.enter_context(nc.psum_tensor("score_ps", [P, 2, 512], F32))
        pt_ps = ctx.enter_context(nc.psum_tensor("pt_ps", [P, 2, 512], F32))
        o_ps = ctx.enter_context(nc.psum_tensor("o_ps", [P, B, 512], F32))
        in_ps = ctx.enter_context(nc.psum_tensor("in_ps", [P, 512], F32))
        out_ps = ctx.enter_context(nc.psum_tensor("out_ps", [P, 512], F32))


        xs_dram = dram("sorted_x", [MT * P, D])
        ys_dram = dram("sorted_y", [MT * P, D])
        zero_sb = b2t_sb[:, :]

        cst_in, x_in, ctx_in, raw_in, col_in, row_in, small_in, pad_in = [
            sem(n) for n in ("cst_in", "x_in", "ctx_in", "raw_in", "col_in", "row_in", "small_in", "pad_in")]
        bias_in = [sem(f"bias_in{i}") for i in range(NJ // 2)]
        bias_ready = sem("bias_ready")
        zero_ready, zeroed = sem("zero_ready"), sem("zeroed")
        w1_in, w2_in, w1_last_in, w2_last_in = sem("w1_in"), sem("w2_in"), sem("w1_last_in"), sem("w2_last_in")
        l1_in, l1w_in, l1q_in, dft_in, ctx1_in = [sem(n) for n in ("l1_in", "l1w_in", "l1q_in", "dft_in", "ctx1_in")]
        tg_ready, rows_ready = sem("tg_ready"), sem("rows_ready")
        flags_made, flags_read = sem("flags_made"), sem("flags_read")
        pads_ready, pen_made, pen_done = sem("pads_ready"), sem("pen_made"), sem("pen_done")
        wT_done, wT_ev = sem("wT_done"), sem("wT_ev")
        sm_done, sm_ev = sem("sm_done"), sem("sm_ev")
        dve_step = sem("dve_step")
        pool_step = sem("pool_step")
        stats_ready = [sem(f"stats_ready{i}") for i in range(4)]
        rstd_ready = [sem(f"rstd_ready{i}") for i in range(4)]
        names = ("ctx_T ctx_ev k_done kb_ready kbd_ready v_done vb_taken v_ready scored s_taken maxed subbed exp_done "
                 "pt_done pt_ev pv_done rs_ready on_done oT_done oT_ev wo_done resid x_stats xn_done xnT_done xnT_ev "
                 "q_done q_ev xb_done").split()
        L = [{n: sem(f"{n}_{l}") for n in names} for l in range(2)]
        xna_done, gT_done, gT_ev, lg_done, hot, ranked, slots, scattered = [
            sem(n) for n in ("xna_done", "gT_done", "gT_ev", "lg_done", "hot", "ranked", "slots", "scattered")]
        ar_done, ar_ev, m_done, m_ready = sem("ar_done"), sem("ar_ev"), sem("m_done"), sem("m_ready")
        xs_in, b2_in, xsT_done, xsT_ev, h_done, h_ev_a, h_ev_v, hT_done, hT_ev_a, hT_ev_v, y_done, y_ev, y_out = [
            sem(n) for n in ("xs_in", "b2_in", "xsT_done", "xsT_ev", "h_done", "h_ev_a", "h_ev_v", "hT_done",
                             "hT_ev_a", "hT_ev_v", "y_done", "y_ev", "y_out")]
        gathered = [sem(f"gathered{i}") for i in range(4)]
        f_xn, f_T, f_ev, f_y, f_xb, f_x, f_out = [
            sem(n) for n in ("f_xn", "f_T", "f_ev", "f_y", "f_xb", "f_x", "f_out")]

        def wait(eng, s, value):
            if not isinstance(value, int) or value > 0:
                eng.wait_ge(s, value)

        def unit_on(j, k, back=0):
            return not isinstance(j, int) or 0 <= 4 * j + k - back < UNITS

        def tile_on(j, m):
            return not isinstance(j, int) or 0 <= m < NT

        def attention_steps(eng, body):
            for j in (0, 1):
                for k in range(4):
                    body(j, k)
            with eng.Fori(2, NJ - 1) as j:
                for k in range(4):
                    body(j, k)
            for j, k in [(j, k) for j in (NJ - 1, NJ) for k in range(4)] + [(NJ + 1, 0)]:
                body(j, k)

        ident = cst[:, C_ID:C_ID + P]
        W = dict(q=a["L0_xattn_wq"], k=a["L0_xattn_wk"], v=a["L0_xattn_wv"], o=a["L0_xattn_wo"])
        x_v = a["x"].rearrange("b (p j) d -> p b j d", j=NJ)
        out_v = out.rearrange("b (p j) d -> p b j d", j=NJ)
        bias_v = a["fside_Bx16xSxS2_0"].rearrange("b h (p j) k -> b p h (j k)", j=NJ)
        ctx_v = a["ctx_1024"].rearrange("b k d -> k b d")

        def bcast(row):
            return row.rearrange("(o n) -> o n", o=1).to_broadcast([P, row.shape[0]])

        def bias_heads(j, b, h0, n):
            at = (j // 2) * PAIR + b * HEADS * 2 * KEYS + h0 * 2 * KEYS
            v = wide[:, bass.ds(at, n * 2 * KEYS)].rearrange("p (h i k) -> p h i k", h=n, i=2)
            return v[:, :, bass.ds(j % 2, 1), :]

        block = ctx.enter_context(nc.Block())

        @block.sync
        def _(sp):
            sp.dma_start(cst[:, :], a["c_all"][:, 0:C_SMALL]).then_inc(cst_in, 16)
            for b in range(B):
                sp.dma_start(x_sb[:, b * NJ:(b + 1) * NJ, :], x_v[:, b]).then_inc(x_in, 16)
            sp.dma_start(ctx_sb, ctx_v).then_inc(ctx_in, 16)
            for i, n in enumerate("qkvo"):
                sp.dma_start(raw[i], W[n].rearrange("(c p) n -> p c n", c=DC)).then_inc(raw_in, 16)
            for i, n in enumerate(("L0_xattn_bq", "L0_xattn_bk", "L1_xattn_bq", "L1_xattn_bk")):
                sp.dma_start(cols[:, 2 * i:2 * i + 2], a[n].rearrange("(c p) -> p c", c=DC),
                             allow_slow_non_contiguous=True).then_inc(col_in, 16)
            sp.dma_start(tg[:, 0:4:2], bcast(a["g_xattn"]), allow_slow_non_contiguous=True).then_inc(row_in, 16)
            sp.dma_start(tg[:, 1:4:2], bcast(a["g_ffn"]), allow_slow_non_contiguous=True).then_inc(row_in, 16)
            for i, n in enumerate(("L0_xattn_bv", "L0_xattn_bo", "L1_xattn_bo", "L1_ffn_bias")):
                sp.dma_start(rows[:, i, :], bcast(a[n])).then_inc(row_in, 16)
            sp.dma_start(causal, a["c_all"][:, C_CAUSAL:C_ALL].rearrange("p (j k) -> p j k", j=NJ)).then_inc(pad_in, 16)
            for b in range(B):
                sp.dma_start(padraw[:, b, :], bcast(a["mask_BxS2_bf0"][b])).then_inc(pad_in, 16)
            for i in range(NJ // 2):
                for b in range(B):
                    at = i * PAIR + b * HEADS * 2 * KEYS
                    sp.dma_start(wide[:, at:at + HEADS * 2 * KEYS].rearrange("p (h n) -> p h n", h=HEADS),
                                 bias_v[b, :, :, 2 * i * KEYS:2 * (i + 1) * KEYS]).then_inc(bias_in[i], 16)
                if i == 0:
                    sp.dma_start(b1_raw, a["L0_ffn_b1"].rearrange("e (c p) -> (e c) p", c=FC)).then_inc(small_in, 16)
                    sp.dma_start(gw_raw, a["L0_ffn_gate_w"]).then_inc(small_in, 16)
                    sp.dma_start(gb[:, 0, :], bcast(a["L0_ffn_gate_b"])).then_inc(small_in, 16)
                    sp.dma_start(gb[:, 1, :], bcast(a["L0_ffn_expert_bias"])).then_inc(small_in, 16)

            def load_w1(e, s):
                sp.dma_start(w1_sb[:, e * DC * FF:(e + 1) * DC * FF].rearrange("p (c n) -> p c n", c=DC),
                             a["L0_ffn_w1"][e].rearrange("(c p) n -> p c n", c=DC)).then_inc(s, 16)

            def load_w2(e, s):
                sp.dma_start(w2_sb[:, e * FC * D:(e + 1) * FC * D].rearrange("p (c n) -> p c n", c=FC),
                             a["L0_ffn_w2"][e].rearrange("(c p) n -> p c n", c=FC)).then_inc(s, 16)

            for e in range(5):
                load_w1(e, w1_in)
            sp.wait_ge(zero_ready, 1)
            sp.dma_start(xs_dram.rearrange("(r p) d -> p r d", p=P),
                         zero_sb.unsqueeze(1).to_broadcast([P, MT, D])).then_inc(zeroed, 16)
            sp.wait_ge(wT_ev, 4)
            sp.wait_ge(L[0]["k_done"], 1)
            sp.wait_ge(L[0]["v_done"], B * NW)
            sp.wait_ge(pen_made, 1)
            for e in (5, 6):
                load_w1(e, w1_in)
            for i in range(NJ // 2):
                sp.wait_ge(bias_in[i], 16 * B)
                sp.sem_inc(bias_ready, 1)
            for e in range(NE - 1):
                last_pair = ((e + 1) * FC * D - 1) // PAIR
                sp.wait_ge(L[0]["s_taken"], 8 * (last_pair + 1))
                load_w2(e, w2_in)
            sp.wait_ge(L[0]["s_taken"], UNITS)
            sp.wait_ge(L[0]["resid"], NT)
            sp.dma_start(wk1, a["L1_xattn_Wk"].rearrange("(c p) n -> p c n", c=DC)).then_inc(l1w_in, 16)
            sp.dma_start(wv1, a["L1_xattn_Wv"].rearrange("(c p) n -> p c n", c=DC)).then_inc(l1w_in, 16)
            sp.dma_start(rows[:, 0, :], bcast(a["L1_xattn_bv"])).then_inc(l1w_in, 16)
            for i in range(3):
                sp.dma_start(dft[i], a["c_dft"][i].rearrange("(c p) n -> p c n", c=DC)).then_inc(dft_in, 16)
            sp.dma_start(wfr, a["L1_ffn_w_freq_real"].rearrange("(c p) n -> p c n", c=DC)).then_inc(dft_in, 16)
            sp.dma_start(wfi, a["L1_ffn_w_freq_imag"].rearrange("(c p) n -> p c n", c=DC)).then_inc(dft_in, 16)
            sp.dma_start(wq_sb[:, :, :], a["L1_xattn_Wq"].rearrange("(c p) n -> p c n", c=DC)).then_inc(l1q_in, 16)
            sp.dma_start(wo_sb[:, :, :], a["L1_xattn_Wo"].rearrange("(c p) n -> p c n", c=DC)).then_inc(l1q_in, 16)
            sp.wait_ge(m_done, 1)
            sp.dma_start(ctx_sb, ctx_v).then_inc(ctx1_in, 16)
            sp.wait_ge(slots, 1)
            load_w1(NE - 1, w1_last_in)
            sp.wait_ge(L[1]["k_done"], 1)
            sp.wait_ge(L[1]["v_done"], B * NW)
            sp.wait_ge(scattered, 16 * NT)
            load_w2(NE - 1, w2_last_in)
            sp.wait_ge(slots, 2)

            def store_y(t):
                sp.wait_ge(y_ev, t + 1)
                sp.dma_start(ys_dram[bass.ds(t * P, P), :], y_sb).then_inc(y_out, 16)

            def load_xs(t):
                wait(sp, xsT_done, t)
                sp.dma_start(xs_sb, xs_dram[bass.ds(t * P, P), :]).then_inc(xs_in, 16)

            def load_b2(t):
                e = sp.value_load(tile_e[0:1, bass.ds(t, 1)], min_val=0, max_val=NE - 1)
                sp.dma_start(b2t_sb[:, :], a["L0_ffn_b2"][bass.ds(e, 1), :].to_broadcast([P, D])).then_inc(b2_in, 16)

            sp.wait_ge(m_done, 1)
            load_xs(0)
            sp.wait_ge(zeroed, 16)
            load_b2(0)
            load_xs(1)
            with sp.Fori(0, MT - 2) as t:
                load_xs(t + 2)
                store_y(t)
                load_b2(t + 1)
            store_y(MT - 2)
            load_b2(MT - 1)
            store_y(MT - 1)
            with sp.Fori(0, NJ) as j:
                for b in range(B):
                    sp.wait_ge(f_x, 2 * j + b + 1)
                    sp.dma_start(out_v[:, b, bass.ds(j, 1), :], x_sb[:, bass.ds(b * NJ + j, 1), :]).then_inc(f_out, 16)
            sp.wait_ge(f_out, 16 * NT)

        @block.tensor
        def _(pe):
            def prepare(l):
                s = L[l]
                wk, wv = (wkT, wvT) if l == 0 else (wk1, wv1)
                pe.wait_ge(ctx_in if l == 0 else ctx1_in, 16)
                for c in range(DC):
                    for b in range(B):
                        at = (c * B + b) * KEYS
                        t = nc.tensor.transpose(pt_ps[:, 0, at:at + KEYS], ctx_sb[:, b, c * P:(c + 1) * P],
                                                ident[0:KEYS, 0:KEYS])
                t.then_inc(s["ctx_T"], 1)
                pe.wait_ge(s["ctx_ev"], 2)
                for oc in range(DC):
                    for ic in range(DC):
                        t = nc.tensor.matmul(score_ps[:, 0, oc * B * KEYS:(oc + 1) * B * KEYS],
                                             wk[:, ic, oc * P:(oc + 1) * P], ctxT[:, ic, :, 0:KEYS],
                                             start=(ic == 0), stop=(ic == DC - 1))
                t.then_inc(s["k_done"], 1)
                for b in range(B):
                    for w in range(NW):
                        i = b * NW + w
                        if i >= 2:
                            pe.wait_ge(s["vb_taken"], i - 1)
                        for ic in range(DC):
                            t = nc.tensor.matmul((score_ps if i % 2 else pt_ps)[0:TW, 1, 0:D],
                                                 ctxT[:, ic, b, w * TW:(w + 1) * TW], wv[:, ic, :],
                                                 start=(ic == 0), stop=(ic == DC - 1))
                        t.then_inc(s["v_done"], 1)
                pe.wait_ge(s["kbd_ready"], QH)
                pe.wait_ge(s["v_ready"], B * NW + 1)

            def attend(l):
                s = L[l]

                def transpose_x(j, m, b):
                    pe.wait_ge(s["xn_done"], m + 1)
                    wait(pe, s["q_ev"], m)
                    for c in range(DC):
                        t = nc.tensor.transpose(in_ps[:, c * P:(c + 1) * P], xn_sb[:, b, c * P:(c + 1) * P], ident)
                    t.then_inc(s["xnT_done"], 1)

                def project_q(m):
                    pe.wait_ge(s["xnT_ev"], m + 1)
                    for oc in range(DC):
                        for ic in range(DC):
                            t = nc.tensor.matmul(in_ps[:, oc * P:(oc + 1) * P], wq_sb[:, ic, oc * P:(oc + 1) * P],
                                                 xnT_sb[:, ic, :], start=(ic == 0), stop=(ic == DC - 1))
                    t.then_inc(s["q_done"], 1)

                transpose_x(0, 0, 0)
                project_q(0)
                transpose_x(0, 1, 1)

                def step(j, k):
                    if unit_on(j, k):
                        c, b = k % 2, k // 2
                        if c == 0:
                            pe.wait_ge(s["q_ev"], 2 * j + b + 1)
                        wait(pe, s["s_taken"], 4 * j + k)
                        for h in range(2):
                            t = nc.tensor.matmul(
                                score_ps[:, h, 0:QK], qT_sb[64 * h:64 * h + 64, b, c, :],
                                kbd[64 * h:64 * h + 64, c, b, :, :].rearrange("p h k -> p (h k)"),
                                start=True, stop=True)
                        t.then_inc(s["scored"], 1)
                    if k % 2 == 0:
                        m = 2 * j + k // 2 + 1
                        if tile_on(j, m):
                            project_q(m)
                    if unit_on(j, k, LAG_T):
                        k2 = (k - LAG_T) % 4
                        pe.wait_ge(s["exp_done"], 4 * j + k - LAG_T + 1)
                        wait(pe, s["pt_ev"], 4 * j + k - LAG_T)
                        for h in range(2):
                            for w in range(NW):
                                t = nc.tensor.transpose(pt_ps[0:TW, h, w * P:(w + 1) * P],
                                                        s_sb[:, k2, h, w * TW:(w + 1) * TW], ident)
                        t.then_inc(s["pt_done"], 1)
                    if k % 2 == 0:
                        m = 2 * j + k // 2 - 3
                        if tile_on(j, m):
                            b = (k // 2 + 1) % 2
                            pe.wait_ge(s["oT_ev"], m + 1)
                            for ic in range(DC):
                                t = nc.tensor.matmul(out_ps[:, 0:D], oT_sb[:, b, ic, :], wo_sb[:, ic, :],
                                                     start=(ic == 0), stop=(ic == DC - 1))
                            t.then_inc(s["wo_done"], 1)
                    if unit_on(j, k, LAG_V):
                        kv = (k - LAG_V) % 4
                        c, b = kv % 2, kv // 2
                        u = 4 * j + k - LAG_V
                        pe.wait_ge(s["pt_ev"], u + 1)
                        if c == 0:
                            wait(pe, s["on_done"], 2 * j + (k - LAG_V) // 2 - 1)
                        for h in range(2):
                            for w in range(NW):
                                at = (2 * c + h) * VC
                                t = nc.tensor.matmul(
                                    o_ps[:, b, at:at + VC], pt_sb[0:TW, kv % 2, h, w * P:(w + 1) * P],
                                    vblk[0:TW, b, w, 2 * c + h, :, :].rearrange("p h e -> p (h e)"),
                                    start=(w == 0), stop=(w == NW - 1))
                        t.then_inc(s["pv_done"], 1)
                    if k % 2 == 1:
                        m, b = 2 * j + (k - 1) // 2 - 2, (k - 1) // 2
                        if tile_on(j, m):
                            pe.wait_ge(s["on_done"], m + 1)
                            wait(pe, s["resid"], m)
                            for c in range(DC):
                                t = nc.tensor.transpose(out_ps[:, c * P:(c + 1) * P],
                                                        on_sb[:, b, c * P:(c + 1) * P], ident)
                            t.then_inc(s["oT_done"], 1)
                        m = 2 * j + (k - 1) // 2 + 2
                        if tile_on(j, m):
                            transpose_x(j, m, b)

                attention_steps(pe, step)

            pe.wait_ge(cst_in, 16)
            pe.wait_ge(raw_in, 16 * 4)
            for i in range(4):
                if i >= 2:
                    pe.wait_ge(wT_ev, i - 1)
                bank = in_ps if i % 2 == 0 else out_ps
                for ic in range(DC):
                    for oc in range(DC):
                        at = (ic * DC + oc) * P
                        t = nc.tensor.transpose(bank[:, at:at + P], raw[i][:, oc, ic * P:(ic + 1) * P], ident)
                t.then_inc(wT_done, 1)
            pe.wait_ge(wT_ev, 4)
            prepare(0)
            pe.wait_ge(small_in, 16 * 4)
            for c in range(DC):
                nc.tensor.transpose(o_ps[:, 0, c * NE:(c + 1) * NE], gw_raw[:, c * P:(c + 1) * P], ident[0:NE, 0:NE])
            nc.tensor.transpose(o_ps[:, 0, DC * NE:DC * NE + NE * FC], b1_raw,
                                ident[0:NE * FC, 0:NE * FC]).then_inc(sm_done, 1)
            pe.wait_ge(sm_ev, 2)
            attend(0)

            pe.wait_ge(L[0]["resid"], NT)
            for t in range(NT):
                bank = in_ps if t % 2 == 0 else out_ps
                pe.wait_ge(xna_done, t + 1)
                wait(pe, gT_ev, t - 1)
                for c in range(DC):
                    i = nc.tensor.transpose(bank[:, c * P:(c + 1) * P], xn_all[:, t, c * P:(c + 1) * P], ident)
                i.then_inc(gT_done, 1)
                if t >= 1:
                    pe.wait_ge(gT_ev, t)
                    for c in range(DC):
                        i = nc.tensor.matmul(o_ps[:, 0, (t - 1) * NE:t * NE], qT_sb[:, (t - 1) % 2, c, :],
                                             gwT[:, c, :], start=(c == 0), stop=(c == DC - 1))
                    i.then_inc(lg_done, 1)
            pe.wait_ge(gT_ev, NT)
            for c in range(DC):
                i = nc.tensor.matmul(o_ps[:, 0, (NT - 1) * NE:NT * NE], qT_sb[:, (NT - 1) % 2, c, :],
                                     gwT[:, c, :], start=(c == 0), stop=(c == DC - 1))
            i.then_inc(lg_done, 1)

            pe.wait_ge(dft_in, 16 * 5)
            for part, (one, two) in enumerate((((wfr, dft[0]), (wfi, dft[1])), ((wfi, dft[0]), (wfr, dft[2])))):
                for oc in range(DC):
                    n = 0
                    for w, f in (one, two):
                        for ic in range(DC):
                            i = nc.tensor.matmul(score_ps[:, part, oc * D:(oc + 1) * D], w[:, ic, oc * P:(oc + 1) * P],
                                                 f[:, ic, :], start=(n == 0), stop=(n == 2 * DC - 1))
                            n += 1
                i.then_inc(ar_done, 1)
            pe.wait_ge(hot, 1)
            nc.tensor.matmul(o_ps[:, 1, 0:P], cst[:, C_TRI:C_TRI + P], rt[:, 2, :], start=True, stop=True)
            nc.tensor.matmul(o_ps[:, 1, P:2 * P], rt[:, 15, :], rt[:, 2, :], start=True, stop=True).then_inc(ranked, 1)
            pe.wait_ge(ar_ev, 2)
            for oc in range(DC):
                n = 0
                for w, f in ((arT, dft[0]), (aiT, dft[2])):
                    for ic in range(DC):
                        i = nc.tensor.matmul(pt_ps[:, 0, oc * D:(oc + 1) * D], w[:, ic, oc * P:(oc + 1) * P],
                                             f[:, ic, :], start=(n == 0), stop=(n == 2 * DC - 1))
                        n += 1
            i.then_inc(m_done, 1)
            pe.wait_ge(m_ready, 1)
            pe.wait_ge(l1w_in, 16 * 3)
            prepare(1)

            for s_, v in ((w1_in, 16 * 7), (w2_in, 16 * 7), (w1_last_in, 16), (w2_last_in, 16)):
                pe.wait_ge(s_, v)

            def turn_xs(t):
                pe.wait_ge(xs_in, 16 * (t + 1))
                wait(pe, xsT_ev, t)
                for c in range(DC):
                    i = nc.tensor.transpose(in_ps[:, c * P:(c + 1) * P], xs_sb[:, c * P:(c + 1) * P], ident)
                i.then_inc(xsT_done, 1)

            def hidden(t):
                e = pe.value_load(tile_e[0:1, bass.ds(t, 1)], min_val=0, max_val=NE - 1)
                pe.wait_ge(xsT_ev, t + 1)
                wait(pe, h_ev_a, t)
                wait(pe, h_ev_v, t)
                for c in range(DC):
                    for n in range(2):
                        i = nc.tensor.matmul(score_ps[:, n, :], xsT_sb[:, c, :],
                                             w1_sb[:, bass.ds(e * (DC * FF) + c * FF + n * 512, 512)],
                                             start=(c == 0), stop=(c == DC - 1))
                i.then_inc(h_done, 1)

            def turn_h(t):
                pe.wait_ge(h_ev_a, t + 1)
                pe.wait_ge(h_ev_v, t + 1)
                wait(pe, hT_ev_a, t)
                wait(pe, hT_ev_v, t)
                for f in range(FC):
                    i = nc.tensor.transpose(pt_ps[:, f // 4, f % 4 * P:(f % 4 + 1) * P],
                                            h_sb[:, f * P:(f + 1) * P], ident)
                i.then_inc(hT_done, 1)

            def outputs(t):
                e = pe.value_load(tile_e[0:1, bass.ds(t, 1)], min_val=0, max_val=NE - 1)
                pe.wait_ge(hT_ev_a, t + 1)
                pe.wait_ge(hT_ev_v, t + 1)
                wait(pe, y_ev, t)
                for f in range(FC):
                    i = nc.tensor.matmul(o_ps[:, 0, 0:D], hT_sb[:, f, :],
                                         w2_sb[:, bass.ds(e * (FC * D) + f * D, D)],
                                         start=(f == 0), stop=(f == FC - 1))
                i.then_inc(y_done, 1)

            turn_xs(0)
            hidden(0)
            turn_xs(1)
            turn_h(0)
            hidden(1)
            turn_xs(2)
            outputs(0)
            with pe.Fori(1, MT - 2) as t:
                turn_h(t)
                hidden(t + 1)
                turn_xs(t + 2)
                outputs(t)
            turn_h(MT - 2)
            hidden(MT - 1)
            outputs(MT - 2)
            turn_h(MT - 1)
            outputs(MT - 1)

            pe.wait_ge(l1q_in, 32)
            attend(1)

            def spectral_turn(j):
                for b in range(B):
                    pe.wait_ge(f_xn, 2 * j + b + 1)
                    for c in range(DC):
                        i = nc.tensor.transpose((out_ps if b else in_ps)[:, c * P:(c + 1) * P],
                                                xn_sb[:, b, c * P:(c + 1) * P], ident)
                    i.then_inc(f_T, 1)
                for b in range(B):
                    pe.wait_ge(f_ev, 2 * j + b + 1)
                    wait(pe, f_x, 2 * j)
                    for c in range(DC):
                        i = nc.tensor.matmul(o_ps[:, b, 0:D], qT_sb[:, b, c, :], m_sb[:, c, :],
                                             start=(c == 0), stop=(c == DC - 1))
                    i.then_inc(f_y, 1)

            spectral_turn(0)
            with pe.Fori(1, NJ) as j:
                spectral_turn(j)

        @block.scalar
        def _(act):
            def copy(out_, in_, s):
                nc.scalar.activation(out_, in_, ACT.Copy).then_inc(s, 1)

            def attend(l):
                s = L[l]

                def keep_xT(m):
                    act.wait_ge(s["xnT_done"], m + 1)
                    wait(act, s["q_done"], m)
                    copy(xnT_sb[:, :, :].rearrange("p c t -> p (c t)"), in_ps[:, 0:D], s["xnT_ev"])

                def keep_q(m, b):
                    act.wait_ge(s["q_done"], m + 1)
                    wait(act, s["scored"], 2 * m - 2)
                    nc.scalar.activation(qT_sb[:, b, 0, :], in_ps[:, 0:P], ACT.Identity, bias=cols[:, 4 * l:4 * l + 1])
                    nc.scalar.activation(qT_sb[:, b, 1, :], in_ps[:, P:2 * P], ACT.Identity,
                                         bias=cols[:, 4 * l + 1:4 * l + 2]).then_inc(s["q_ev"], 1)

                keep_xT(0)
                keep_q(0, 0)

                def step(j, k):
                    if k % 2 == 0:
                        m, b = 2 * j + k // 2 - 3, (k // 2 + 1) % 2
                        if tile_on(j, m):
                            act.wait_ge(s["oT_done"], m + 1)
                            copy(oT_sb[:, b, :, :].rearrange("p c t -> p (c t)"), out_ps[:, 0:D], s["oT_ev"])
                        m = 2 * j + k // 2 + 1
                        if tile_on(j, m):
                            keep_xT(m)
                    if unit_on(j, k, 1):
                        kk = (k - 1) % 4
                        act.wait_ge(s["subbed" if l == 0 else "s_taken"], 4 * j + k)
                        nc.scalar.activation(s_sb[:, kk, :, 0:QK], s_sb[:, kk, :, 0:QK],
                                             ACT.Exp).then_inc(s["exp_done"], 1)
                    if unit_on(j, k, 2):
                        act.wait_ge(s["pt_done"], 4 * j + k - 1)
                        wait(act, s["pv_done"], 4 * j + k - 3)
                        nc.scalar.activation(pt_sb[0:TW, k % 2, :, :], pt_ps[0:TW, :, 0:NW * P],
                                             ACT.Copy).then_inc(s["pt_ev"], 1)
                    if k % 2 == 1:
                        m = 2 * j + (k - 1) // 2 + 1
                        if tile_on(j, m):
                            keep_q(m, ((k - 1) // 2 + 1) % 2)

                attention_steps(act, step)

            act.wait_ge(row_in, 16 * 6)
            nc.scalar.activation(tg[:, :], tg[:, :], ACT.Tanh).then_inc(tg_ready, 1)
            for i, dst in enumerate((wq_sb[:, :, :], wkT, wvT, wo_sb[:, :, :])):
                act.wait_ge(wT_done, i + 1)
                copy(dst.rearrange("p c n -> p (c n)"), (in_ps if i % 2 == 0 else out_ps)[:, :], wT_ev)

            def keep_context(l):
                s = L[l]
                act.wait_ge(s["ctx_T"], 1)
                for r in range(QH):
                    i = nc.scalar.activation(ctxT_heads[r], pt_ps[:, 0, 0:DC * B * KEYS].rearrange(
                        "p (c k) -> p c k", c=DC * B), ACT.Copy)
                i.then_inc(s["ctx_ev"], 1)

            keep_context(0)
            act.wait_ge(sm_done, 1)
            copy(gwT[:, :, :].rearrange("p c e -> p (c e)"), o_ps[:, 0, 0:DC * NE], sm_ev)
            copy(b1T[:, :], o_ps[:, 0, DC * NE:DC * NE + NE * FC], sm_ev)
            act.wait_ge(col_in, 16 * 4)
            attend(0)

            for t in range(NT):
                act.wait_ge(gT_done, t + 1)
                wait(act, lg_done, t - 1)
                copy(qT_sb[:, t % 2, :, :].rearrange("p c n -> p (c n)"), (in_ps if t % 2 == 0 else out_ps)[:, 0:D],
                     gT_ev)
            act.wait_ge(ar_done, 2)
            act.wait_ge(lg_done, NT)
            copy(arT.rearrange("p b n -> p (b n)"), score_ps[:, 0, :], ar_ev)
            copy(aiT.rearrange("p b n -> p (b n)"), score_ps[:, 1, :], ar_ev)
            act.wait_ge(m_done, 1)
            nc.scalar.activation(m_sb[:, :, :].rearrange("p c n -> p (c n)"), pt_ps[:, 0, :], ACT.Copy,
                                 scale=1.0 / D).then_inc(m_ready, 1)
            keep_context(1)

            def keep_xs(t):
                act.wait_ge(xsT_done, t + 1)
                wait(act, h_done, t)
                copy(xsT_sb[:, :, :].rearrange("p c t -> p (c t)"), in_ps[:, 0:D], xsT_ev)

            def keep_h(t):
                act.wait_ge(h_done, t + 1)
                wait(act, hT_done, t)
                copy(h_sb[:, 0:512], score_ps[:, 0, :], h_ev_a)

            def relu_h(t):
                e = act.value_load(tile_e[0:1, bass.ds(t, 1)], min_val=0, max_val=NE - 1)
                act.wait_ge(hT_done, t + 1)
                wait(act, y_done, t)
                for f in range(4):
                    i = nc.scalar.activation(hT_sb[:, f, :], pt_ps[:, 0, f * P:(f + 1) * P], ACT.Relu,
                                             bias=b1T[:, bass.ds(e * FC + f, 1)])
                i.then_inc(hT_ev_a, 1)

            act.wait_ge(slots, 2)
            act.wait_ge(L[1]["kbd_ready"], QH)
            act.wait_ge(L[1]["v_ready"], B * NW + 1)
            keep_xs(0)
            keep_h(0)
            keep_xs(1)
            relu_h(0)
            keep_h(1)
            keep_xs(2)
            with act.Fori(1, MT - 2) as t:
                relu_h(t)
                keep_h(t + 1)
                keep_xs(t + 2)
            relu_h(MT - 2)
            keep_h(MT - 1)
            relu_h(MT - 1)

            attend(1)
            def spectral_turn(j):
                for b in range(B):
                    act.wait_ge(f_T, 2 * j + b + 1)
                    wait(act, f_y, 2 * j)
                    copy(qT_sb[:, b, :, :].rearrange("p c n -> p (c n)"), (out_ps if b else in_ps)[:, 0:D], f_ev)

            spectral_turn(0)
            with act.Fori(1, NJ) as j:
                spectral_turn(j)

        @block.gpsimd
        def _(pool):
            steps = [0]

            def link(i):
                steps[0] += 1
                i.then_inc(pool_step, 1)
                pool.wait_ge(pool_step, steps[0])

            def make_rstd(n):
                pool.wait_ge(stats_ready[n], NT)
                link(nc.gpsimd.tensor_scalar(rstd[:, :], mv[:, :, 1], EPS, None, ALU.add))
                nc.gpsimd.tensor_tensor(rstd[:, :], rstd[:, :], power[:, :], ALU.pow).then_inc(rstd_ready[n], 1)

            nc.gpsimd.memset(zero_sb, 0.0).then_inc(zero_ready, 1)
            link(nc.gpsimd.memset(power[:, :], -0.5))
            nc.gpsimd.memset(ctxT_pad, 0.0).then_inc(L[0]["ctx_ev"], 1)
            pool.wait_ge(pad_in, 16 * 3)
            link(nc.gpsimd.tensor_copy(padrow, padraw))
            for b in range(B):
                i = nc.gpsimd.tensor_tensor(pen[:, b, :, :], causal,
                                            padrow[:, b, :].unsqueeze(1).to_broadcast([P, NJ, KEYS]), ALU.add)
            i.then_inc(flags_made, 1)
            pool.wait_ge(flags_read, 1)
            nc.gpsimd.tensor_scalar(pen.rearrange("p b j k -> p (b j k)"), pen.rearrange("p b j k -> p (b j k)"),
                                    MASKED, None, ALU.mult).then_inc(pen_made, 1)
            make_rstd(0)
            pool.wait_ge(pen_made, 1)
            pool.wait_ge(L[0]["kbd_ready"], QH)
            pool.wait_ge(L[0]["v_ready"], B * NW + 1)
            pool.wait_ge(sm_done, 1)
            nc.gpsimd.memset(s_pad, 0.0).then_inc(pads_ready, 1)

            def penalize(j, b):
                pool.wait_ge(bias_ready, j // 2 + 1)
                v = bias_heads(j, b, 0, HEADS)[:, :, 0, :]
                nc.gpsimd.tensor_tensor(v, v, pen[:, b, bass.ds(j, 1), :].to_broadcast([P, HEADS, KEYS]),
                                        ALU.add).then_inc(pen_done, 1)

            def attend(l):
                s = L[l]

                def add_bo(j, b, m):
                    pool.wait_ge(s["xn_done"], m + 1)
                    xt = x_sb[:, bass.ds(b * NJ + j, 1), :]
                    nc.gpsimd.tensor_tensor(xt, xt, rows[:, 1 + l:2 + l, :], ALU.add).then_inc(s["xb_done"], 1)

                if l == 0:
                    penalize(0, 0)
                    penalize(0, 1)
                pool.wait_ge(rows_ready, 3)
                add_bo(0, 0, 0)
                add_bo(0, 1, 1)

                def step(j, k):
                    if l == 0 and unit_on(j, k):
                        pool.wait_ge(s["maxed"], 4 * j + k + 1)
                        v = s_sb[:, k, :, 0:QK].rearrange("p q (h k) -> p q h k", h=QH)
                        mxb = mx_sb[:, k, :].rearrange("p (q h) -> p q h", q=2).unsqueeze(3).to_broadcast(
                            [P, 2, QH, KEYS])
                        nc.gpsimd.tensor_tensor(v, v, mxb, ALU.subtract).then_inc(s["subbed"], 1)
                    if k % 2 == 1:
                        m, b = 2 * j + (k - 1) // 2 + 2, k // 2
                        if tile_on(j, m):
                            add_bo(j + 1, b, m)
                            if l == 0:
                                penalize(j + 1, b)

                attention_steps(pool, step)

            attend(0)
            make_rstd(1)
            pool.wait_ge(L[0]["pv_done"], UNITS)
            nc.gpsimd.memset(ctxT_pad, 0.0).then_inc(L[1]["ctx_ev"], 1)
            pool.wait_ge(slots, 2)
            pool.wait_ge(zeroed, 16)
            for t in range(NT):
                nc.gpsimd.indirect_dma_start(out=xs_dram, out_offset=bass.IndirectOffsetOnAxis(slot_u[:, t:t + 1], 0),
                                             in_=xn_all[:, t, :], in_offset=None).then_inc(scattered, 16)
            pool.wait_ge(scattered, 16 * NT)
            pool.wait_ge(gT_done, NT)
            pool.wait_ge(y_out, 16 * MT)
            for t in range(NT):
                nc.gpsimd.indirect_dma_start(out=y_all[:, t, :], out_offset=None, in_=ys_dram,
                                             in_offset=bass.IndirectOffsetOnAxis(slot_u[:, t:t + 1], 0)
                                             ).then_inc(gathered[t // 4], 16)
            make_rstd(2)
            pool.wait_ge(y_out, 16 * MT)
            nc.gpsimd.memset(s_pad, 0.0).then_inc(pads_ready, 1)
            attend(1)
            make_rstd(3)
            with pool.Fori(0, NJ) as j:
                for b in range(B):
                    pool.wait_ge(f_xn, 2 * j + b + 1)
                    xt = x_sb[:, bass.ds(b * NJ + j, 1), :]
                    nc.gpsimd.tensor_tensor(xt, xt, rows[:, 3:4, :], ALU.add).then_inc(f_xb, 1)

        @block.vector
        def _(dve):
            steps = [0]

            def link(i):
                steps[0] += 1
                i.then_inc(dve_step, 1)
                dve.wait_ge(dve_step, steps[0])

            def finish_stats(n):
                for t in range(NT):
                    nc.vector.bn_aggr(mv[:, t, :], stats[:, t, :]).then_inc(stats_ready[n], 1)

            dve.wait_ge(tg_ready, 1)
            for i, g in ((1, 0), (2, 2), (3, 3)):
                nc.vector.tensor_scalar(rows[:, i, :], rows[:, i, :], tg[:, g:g + 1], None, ALU.mult
                                        ).then_inc(rows_ready, 1)
            dve.wait_ge(x_in, 16 * B)
            for t in range(NT):
                i = nc.vector.bn_stats(stats[:, t, :], x_sb[:, t, :])
            link(i)
            finish_stats(0)

            def prepare(l):
                s = L[l]
                dve.wait_ge(s["k_done"], 1)
                if l == 0:
                    dve.wait_ge(cst_in, 16)
                    dve.wait_ge(col_in, 16 * 4)
                for c in range(DC):
                    i = nc.vector.tensor_scalar(
                        kb_sb[:, c, :, :], score_ps[:, 0, c * B * KEYS:(c + 1) * B * KEYS].rearrange(
                            "p (b k) -> p b k", b=B),
                        cols[:, 4 * l + 2 + c:4 * l + 3 + c], HD ** -0.5, ALU.add, ALU.mult)
                    link(i)
                for h in range(QH):
                    nc.vector.tensor_scalar(kbd[:, :, :, h, :].rearrange("p c b k -> p (c b) k"),
                                            kb_sb.rearrange("p c b k -> p (c b) k"),
                                            cst[:, C_KM + h:C_KM + h + 1], None, ALU.mult).then_inc(s["kbd_ready"], 1)
                vmask = cst[0:TW, C_VM:C_VM + NW * QH].rearrange("p (w h) -> p w h", w=NW)
                for b in range(B):
                    for w in range(NW):
                        n = b * NW + w
                        dve.wait_ge(s["v_done"], n + 1)
                        if l == 1 and n == 0:
                            dve.wait_ge(l1w_in, 16 * 3)
                        link(nc.vector.tensor_tensor(vb_sb[0:TW, n % 2, :],
                                                     (score_ps if n % 2 else pt_ps)[0:TW, 1, 0:D], rows[0:TW, 0, :],
                                                     ALU.add))
                        dve.sem_inc(s["vb_taken"], 1)
                        nc.vector.tensor_tensor(
                            vblk[0:TW, b, w, :, :, 0:HD],
                            vb_sb[0:TW, n % 2, :].rearrange("p (q h d) -> p q h d", q=4, h=QH),
                            vmask[:, w, :].unsqueeze(1).unsqueeze(3).to_broadcast([TW, 4, QH, HD]),
                            ALU.mult).then_inc(s["v_ready"], 1)
                        i = nc.vector.tensor_copy(vblk[0:TW, b, w, :, :, HD],
                                                  vmask[:, w, :].unsqueeze(1).to_broadcast([TW, 4, QH]))
                i.then_inc(s["v_ready"], 1)

            dve.wait_ge(flags_made, 1)
            nc.vector.tensor_reduce(no_key[:, :], pen.rearrange("p b j k -> p (b j) k"), AX_X,
                                    ALU.min).then_inc(flags_read, 1)
            dve.wait_ge(flags_read, 1)
            link(nc.vector.tensor_scalar(no_key[:, :], no_key[:, :], 3e38, 10.0, ALU.mult, ALU.mult))
            link(nc.vector.tensor_scalar(no_key[:, :], no_key[:, :], 0.0, None, ALU.mult))
            prepare(0)

            def attend(l, n):
                s = L[l]

                def norm_x(j, b, m):
                    t = b * NJ + j
                    wait(dve, s["xnT_done"], m - 1)
                    nc.vector.tensor_scalar(xn_sb[:, b:b + 1, :], x_sb[:, bass.ds(t, 1), :],
                                            mv[:, bass.ds(t, 1), 0], rstd[:, bass.ds(t, 1)],
                                            ALU.subtract, ALU.mult).then_inc(s["xn_done"], 1)

                dve.wait_ge(rstd_ready[n], 1)
                norm_x(0, 0, 0)
                norm_x(0, 1, 1)
                dve.wait_ge(pads_ready, l + 1)

                def step(j, k):
                    if unit_on(j, k):
                        c, b = k % 2, k // 2
                        sv = s_sb[:, k, :, 0:QK].rearrange("p q (h k) -> p q h k", h=QH)
                        pv = score_ps[:, :, 0:QK].rearrange("p q (h k) -> p q h k", h=QH)
                        mv_ = mx_sb[:, k, :].rearrange("p (q h) -> p q h", q=2)
                        dve.wait_ge(s["scored"], 4 * j + k + 1)
                        wait(dve, s["pt_done"], 4 * j + k - 3)
                        if l == 0:
                            dve.wait_ge(pen_done, 2 * j + b + 1)
                            nc.vector.tensor_tensor(
                                sv, pv, bias_heads(j, b, 8 * c, 8).rearrange("p (q h) i k -> p q h (i k)", q=2), ALU.add).then_inc(s["s_taken"], 1)
                            dve.wait_ge(s["s_taken"], 4 * j + k + 1)
                            wait(dve, s["subbed"], 4 * j + k - 3)
                            nc.vector.tensor_reduce(mv_, sv, AX_X, ALU.max).then_inc(s["maxed"], 1)
                        else:
                            nc.vector.tensor_reduce(mv_, pv, AX_X, ALU.max).then_inc(s["maxed"], 1)
                            dve.wait_ge(s["maxed"], 4 * j + k + 1)
                            nc.vector.tensor_tensor(
                                sv, pv, mv_.unsqueeze(3).to_broadcast([P, 2, QH, KEYS]), ALU.subtract
                            ).then_inc(s["s_taken"], 1)
                    if k % 2 == 0:
                        m, b = 2 * j + k // 2 - 3, (k // 2 + 1) % 2
                        if tile_on(j, m):
                            dve.wait_ge(s["wo_done"], m + 1)
                            dve.wait_ge(s["xb_done"], m + 1)
                            t = b * NJ + (j - 2 if k == 0 else j - 1)
                            xt = x_sb[:, bass.ds(t, 1), :]
                            nc.vector.scalar_tensor_tensor(
                                out=xt, in0=out_ps[:, 0:D].unsqueeze(1), scalar=tg[:, 2 * l:2 * l + 1], in1=xt,
                                op0=ALU.mult, op1=ALU.add).then_inc(s["resid"], 1)
                            dve.wait_ge(s["resid"], m + 1)
                            nc.vector.bn_stats(stats[:, bass.ds(t, 1), :], xt).then_inc(s["x_stats"], 1)
                        m, b = 2 * j + k // 2 + 2, k // 2
                        if tile_on(j, m):
                            norm_x(j + 1, b, m)
                    else:
                        m, b = 2 * j + (k - 1) // 2 - 2, (k - 1) // 2
                        if tile_on(j, m):
                            ov = o_ps[:, b, 0:HEADS * (HD + 1)].rearrange("p (h e) -> p h e", e=HD + 1)
                            dve.wait_ge(s["pv_done"], 2 * m + 2)
                            nc.vector.reciprocal(rs_sb[:, :], ov[:, :, HD]).then_inc(s["rs_ready"], 1)
                            dve.wait_ge(s["rs_ready"], m + 1)
                            wait(dve, s["oT_done"], m - 1)
                            onv = on_sb[:, b, :].rearrange("p (h d) -> p h d", d=HD)
                            rsv = rs_sb[:, :].unsqueeze(2).to_broadcast([P, HEADS, HD])
                            if l == 0:
                                jm = j - 1
                                nc.vector.scalar_tensor_tensor(
                                    out=onv, in0=ov[:, :, 0:HD], scalar=no_key[:, bass.ds(b * NJ + jm, 1)],
                                    in1=rsv, op0=ALU.add, op1=ALU.mult).then_inc(s["on_done"], 1)
                            else:
                                nc.vector.tensor_tensor(onv, ov[:, :, 0:HD], rsv, ALU.mult).then_inc(s["on_done"], 1)

                attention_steps(dve, step)

            attend(0, 0)

            dve.wait_ge(L[0]["x_stats"], NT)
            finish_stats(1)
            dve.wait_ge(rstd_ready[1], 1)
            dve.wait_ge(pen_done, NT)
            dve.wait_ge(L[0]["s_taken"], UNITS)
            for t in range(NT):
                nc.vector.tensor_scalar(xn_all[:, t, :], x_sb[:, t, :], mv[:, t, 0:1], rstd[:, t:t + 1],
                                        ALU.subtract, ALU.mult).then_inc(xna_done, 1)

            def te(i):
                return rt[:, i, :].rearrange("p (t e) -> p t e", e=NE)

            def et(i):
                return rt[:, i, :].rearrange("p (e t) -> p e t", e=NE)

            def c8(at):
                return cst[:, at:at + NE].unsqueeze(1).to_broadcast([P, NT, NE])

            link(nc.vector.memset(rt[:, 15, :], 1.0))
            dve.wait_ge(lg_done, NT)
            link(nc.vector.tensor_tensor(te(0), o_ps[:, 0, 0:P].rearrange("p (t e) -> p t e", e=NE),
                                         gb[:, 0, :].unsqueeze(1).to_broadcast([P, NT, NE]), ALU.add))
            link(nc.vector.tensor_tensor(te(0), te(0), gb[:, 1, :].unsqueeze(1).to_broadcast([P, NT, NE]), ALU.add))
            top = rt[:, 3, 0:NT]
            link(nc.vector.tensor_reduce(top, te(0), AX_X, ALU.max))
            link(nc.vector.tensor_tensor(te(1), te(0), top.unsqueeze(2).to_broadcast([P, NT, NE]), ALU.is_equal))
            link(nc.vector.tensor_tensor(te(1), te(1), c8(C_RANK), ALU.mult))
            link(nc.vector.tensor_tensor(te(1), te(1), c8(C_LAST), ALU.max))
            link(nc.vector.tensor_reduce(top, te(1), AX_X, ALU.max))
            nc.vector.tensor_tensor(te(2), te(1), top.unsqueeze(2).to_broadcast([P, NT, NE]),
                                    ALU.is_equal).then_inc(hot, 1)
            dve.wait_ge(ranked, 1)
            link(nc.vector.tensor_copy(et(4), o_ps[:, 1, P:2 * P].rearrange("p (t e) -> p e t", e=NE)))
            link(nc.vector.tensor_tensor_scan(rt[:, 5, :], cst[:, C_RESET:C_RESET + P], rt[:, 4, :], 0.0,
                                              ALU.mult, ALU.add))
            link(nc.vector.tensor_tensor(et(6), et(5)[:, :, NT - 1:NT].to_broadcast([P, NE, NT]),
                                         cst[:, C_THR:C_THR + NT].unsqueeze(1).to_broadcast([P, NE, NT]),
                                         ALU.is_gt))
            n_tiles, ends, start = rt[:, 7, 0:NE], rt[:, 7, 16:16 + NE], rt[:, 7, 32:32 + NE]
            link(nc.vector.tensor_reduce(n_tiles, et(6), AX_X, ALU.add))
            link(nc.vector.tensor_tensor_scan(ends, rt[:, 15, 0:NE], n_tiles, 0.0, ALU.mult, ALU.add))
            link(nc.vector.tensor_tensor(start, ends, n_tiles, ALU.subtract))
            link(nc.vector.tensor_scalar(start, start, float(P), None, ALU.mult))
            link(nc.vector.tensor_tensor(rt[:, 5, :], rt[:, 5, :], rt[:, 4, :], ALU.subtract))
            link(nc.vector.tensor_tensor(et(5), et(5), start.unsqueeze(2).to_broadcast([P, NE, NT]), ALU.add))
            link(nc.vector.tensor_tensor(te(8), o_ps[:, 1, 0:P].rearrange("p (t e) -> p t e", e=NE),
                                         rt[:, 5, :].rearrange("p (e t) -> p t e", e=NE), ALU.add))
            link(nc.vector.tensor_tensor(te(8), te(8), te(2), ALU.mult))
            link(nc.vector.tensor_reduce(top, te(8), AX_X, ALU.add))
            link(nc.vector.tensor_copy(slot_u[:, :], top))
            cmp_ = rt[:, 9:11, :].rearrange("p i n -> p (i n)")[:, 0:MT * (NE - 1)].rearrange("p (t e) -> p t e", t=MT)
            link(nc.vector.tensor_tensor(cmp_, cst[:, C_TILE:C_TILE + MT].unsqueeze(2).to_broadcast([P, MT, NE - 1]),
                                         ends[:, 0:NE - 1].unsqueeze(1).to_broadcast([P, MT, NE - 1]), ALU.is_ge))
            link(nc.vector.tensor_reduce(rt[:, 11, 0:MT], cmp_, AX_X, ALU.add))
            nc.vector.tensor_copy(tile_e[:, 0:MT], rt[:, 11, 0:MT]).then_inc(slots, 2)

            prepare(1)

            def keep_h(t):
                dve.wait_ge(h_done, t + 1)
                wait(dve, hT_done, t)
                nc.vector.tensor_copy(h_sb[:, 512:1024], score_ps[:, 1, :]).then_inc(h_ev_v, 1)

            def relu_h(t):
                e = dve.value_load(tile_e[0:1, bass.ds(t, 1)], min_val=0, max_val=NE - 1)
                dve.wait_ge(hT_done, t + 1)
                wait(dve, y_done, t)
                for f in range(4, FC):
                    i = nc.vector.tensor_scalar(hT_sb[:, f, :], pt_ps[:, 1, (f - 4) * P:(f - 3) * P],
                                                b1T[:, bass.ds(e * FC + f, 1)], 0.0, ALU.add, ALU.max)
                i.then_inc(hT_ev_v, 1)

            def keep_y(t):
                dve.wait_ge(y_done, t + 1)
                dve.wait_ge(b2_in, 16 * (t + 1))
                wait(dve, y_out, 16 * t)
                nc.vector.tensor_tensor(y_sb, o_ps[:, 0, 0:D], b2t_sb[:, :], ALU.add).then_inc(y_ev, 1)

            keep_h(0)
            relu_h(0)
            keep_h(1)
            keep_y(0)
            with dve.Fori(1, MT - 2) as t:
                relu_h(t)
                keep_h(t + 1)
                keep_y(t)
            relu_h(MT - 2)
            keep_h(MT - 1)
            keep_y(MT - 2)
            relu_h(MT - 1)
            keep_y(MT - 1)
            for t in range(NT):
                dve.wait_ge(gathered[t // 4], 64)
                link(nc.vector.scalar_tensor_tensor(out=x_sb[:, t, :], in0=y_all[:, t, :], scalar=tg[:, 1:2],
                                                    in1=x_sb[:, t, :], op0=ALU.mult, op1=ALU.add))
                link(nc.vector.bn_stats(stats[:, t, :], x_sb[:, t, :]))
            finish_stats(2)
            attend(1, 2)
            dve.wait_ge(L[1]["x_stats"], NT)
            finish_stats(3)
            dve.wait_ge(rstd_ready[3], 1)
            def spectral_turn(j):
                for b in range(B):
                    t = b * NJ + j
                    wait(dve, f_T, 2 * j)
                    nc.vector.tensor_scalar(xn_sb[:, b:b + 1, :], x_sb[:, bass.ds(t, 1), :],
                                            mv[:, bass.ds(t, 1), 0], rstd[:, bass.ds(t, 1)],
                                            ALU.subtract, ALU.mult).then_inc(f_xn, 1)
                for b in range(B):
                    xt = x_sb[:, bass.ds(b * NJ + j, 1), :]
                    dve.wait_ge(f_y, 2 * j + b + 1)
                    dve.wait_ge(f_xb, 2 * j + b + 1)
                    nc.vector.scalar_tensor_tensor(out=xt, in0=o_ps[:, b, 0:D].unsqueeze(1), scalar=tg[:, 3:4],
                                                   in1=xt, op0=ALU.mult, op1=ALU.add).then_inc(f_x, 1)

            spectral_turn(0)
            with dve.Fori(1, NJ) as j:
                spectral_turn(j)


_INS = ['x', 'ctx_1024', 'fside_Bx16xSxS2_0', 'mask_BxS2_bf0', 'g_xattn', 'g_ffn',
        'L0_xattn_wq', 'L0_xattn_bq', 'L0_xattn_wk', 'L0_xattn_bk', 'L0_xattn_wv', 'L0_xattn_bv',
        'L0_xattn_wo', 'L0_xattn_bo', 'L0_ffn_gate_w', 'L0_ffn_gate_b', 'L0_ffn_expert_bias',
        'L0_ffn_w1', 'L0_ffn_b1', 'L0_ffn_w2', 'L0_ffn_b2',
        'L1_xattn_Wq', 'L1_xattn_bq', 'L1_xattn_Wk', 'L1_xattn_bk', 'L1_xattn_Wv', 'L1_xattn_bv',
        'L1_xattn_Wo', 'L1_xattn_bo', 'L1_ffn_w_freq_real', 'L1_ffn_w_freq_imag', 'L1_ffn_bias']


def _constants():
    import numpy as np
    c = np.zeros((P, C_ALL), np.float32)
    p = np.arange(P)
    c[:, C_ID:C_ID + P] = np.eye(P)
    c[:, C_TRI:C_TRI + P] = p[:, None] < p[None, :]
    c[:, C_KM:C_KM + QH] = (p[:, None] % 64) // HD == np.arange(QH)
    for w in range(NW):
        c[:TW, C_VM + w * QH:C_VM + (w + 1) * QH] = (w * TW + p[:TW, None]) // KEYS == np.arange(QH)
    c[:, C_RANK:C_RANK + NE] = NE - np.arange(NE)
    c[:, C_LAST + NE - 1] = 1.0
    c[:, C_RESET:C_RESET + P] = p % NT != 0
    c[:, C_THR:C_THR + NT] = P * np.arange(NT)
    c[:, C_TILE:C_TILE + MT] = np.arange(MT)
    query = p[:, None, None] * NJ + np.arange(NJ)[None, :, None]
    c[:, C_CAUSAL:C_ALL] = np.where(np.arange(KEYS)[None, None, :] > query, 1.0, 0.0).reshape(P, -1)
    angle = 2 * np.pi * (np.outer(np.arange(D), np.arange(D)) % D) / D
    dft = np.stack([np.cos(angle), np.sin(angle), -np.sin(angle)]).astype(np.float32)
    return c, dft


def kernel(**inputs):
    import numpy as _np
    import concourse.bacc as _bacc
    from concourse import mybir as _mybir
    from concourse.bass_utils import run_bass_kernel_spmd as _run

    nc = _bacc.Bacc("TRN2", target_bir_lowering=False, num_devices=1)
    arrays, args = {}, {}
    c_all, c_dft = _constants()
    for name, value in [(n, inputs[n]) for n in _INS] + [("c_all", c_all), ("c_dft", c_dft)]:
        v = _np.ascontiguousarray(value)
        arrays[f"in_{name}_dram"] = v
        args[name] = nc.dram_tensor(f"in_{name}_dram", v.shape, _mybir.dt.from_np(v.dtype), kind="ExternalInput").ap()
    out = nc.dram_tensor("out_0_dram", (B, S, D), F32, kind="ExternalOutput").ap()
    flamingo_kernel(nc, args, out)
    r = _run(nc, [arrays], core_ids=[0])
    return r.results[0]["out_0_dram"]
```

```python
from contextlib import ExitStack

import concourse.bass as bass
from concourse import mybir

ALU = mybir.AluOpType
ACT = mybir.ActivationFunctionType
AX_X = mybir.AxisListType.X
F32 = mybir.dt.float32
U32 = mybir.dt.uint32
I32 = mybir.dt.int32
U8 = mybir.dt.uint8

P = 128
B, S, D = 2, 1024, 256
KEYS = 77
HEADS, HD = 16, 16
NJ = S // P
NT = B * NJ
DC = D // P
QH = 4
QK = QH * KEYS
UH = 8
UK = UH * KEYS
NW = 5
TW = -(-UK // NW)
UP = NW * TW
WH = 3
HV = HD + 1
FIRST_HEAD = [min(w * TW // KEYS, UH - WH) for w in range(NW)]
NE, FF = 8, 1024
FC = FF // P
MT = NT + NE - 1
LAG_T, LAG_V = 2, 3
GATHERED_FIRST = 6
LAG_POST = 9
UNITS = 2 * NT
CTX_COPIES = 3
EPS = 1e-5
MASKED = -1e38

C_ID, C_TRI, C_ONE, C_KM, C_VM = 0, P, 2 * P, 3 * P, 3 * P + QH
C_RANK = C_VM + NW * WH
C_LAST, C_RESET = C_RANK + NE, C_RANK + 2 * NE
C_THR = C_RESET + P
C_TILE = C_THR + NT
C_SMALL = C_TILE + MT
C_CAUSAL = C_SMALL
C_ALL = C_CAUSAL + NJ * KEYS


def flamingo_kernel(nc, a, out):
    with ExitStack() as ctx:
        def sb(name, shape, dt=F32):
            return ctx.enter_context(nc.sbuf_tensor(name, shape, dt))

        def sem(name):
            return ctx.enter_context(nc.semaphore(name))

        def dram(name, shape):
            return nc.dram_tensor(name, shape, F32, kind="Internal").ap()

        w1_sb = sb("w1_sb", [P, NE * DC * FF])
        wide = sb("wide", [P, B * HEADS * NJ * KEYS])
        x_sb = sb("x_sb", [P, NT, D])
        s_sb = sb("s_sb", [P, 4, UP])
        pt_sb = sb("pt_sb", [P, 2, NW * P])
        xn_sb = sb("xn_sb", [P, B, D])
        xnT_sb = sb("xnT_sb", [P, DC, P])
        qT_sb = sb("qT_sb", [P, B, DC, P])
        on_sb = sb("on_sb", [P, B, D])
        oT_sb = sb("oT_sb", [P, B, DC, P])
        b2t_sb = sb("b2t_sb", [P, D])
        kbd = sb("kbd", [P, DC, B, QH, KEYS])
        vblk = sb("vblk", [P, B, NW, DC, WH, HV])
        wq_sb = sb("wq_sb", [P, DC, D])
        wo_sb = sb("wo_sb", [P, DC, D])
        m_sb = sb("m_sb", [P, DC, D])
        cst = sb("cst", [P, C_SMALL])
        rows = sb("rows", [P, 4, D])
        mx_sb = sb("mx_sb", [P, 4, 8])
        rs_sb = sb("rs_sb", [P, HEADS])
        no_key = sb("no_key", [P, NT])
        in_st, in_mv = sb("in_st", [P, B, 6]), sb("in_mv", [P, B, 2])
        in_ve, in_rs = sb("in_ve", [P, B]), sb("in_rs", [P, B])
        po_st, po_mv = sb("po_st", [P, B, 6]), sb("po_mv", [P, B, 2])
        po_ve, po_rs = sb("po_ve", [P, B]), sb("po_rs", [P, B])
        mean_all, rstd_all = sb("mean_all", [P, NT]), sb("rstd_all", [P, NT])
        logit = sb("logit", [P, NT, NE])
        power = sb("power", [P, 2])
        cols = sb("cols", [P, 8])
        tg = sb("tg", [P, 4])
        b1T = sb("b1T", [P, NE * FC])
        gwT = sb("gwT", [P, DC, NE])
        gb = sb("gb", [P, 2, NE])
        slot_u = sb("slot_u", [P, NT], U32)
        tile_e = sb("tile_e", [P, MT + 1], I32)


        last_w1 = (NE - 1) * DC * FF
        pen = w1_sb[:, last_w1:last_w1 + B * NJ * KEYS].rearrange("p (b j k) -> p b j k", b=B, j=NJ)
        st0 = 5 * DC * FF

        def mat(t, at):
            return t[:, at:at + DC * D].rearrange("p (c n) -> p c n", c=DC)

        raw = [mat(w1_sb, st0 + 512 * i) for i in range(4)]
        wkT, wvT = mat(w1_sb, st0 + 2048), mat(w1_sb, st0 + 2560)
        causal = w1_sb[:, st0 + 3072:st0 + 3072 + NJ * KEYS].rearrange("p (j k) -> p j k", j=NJ)
        padraw = w1_sb[:, st0 + 3712:st0 + 3712 + 64].bitcast(U8)[:, 0:B * KEYS].rearrange("p (b k) -> p b k", b=B)
        padrow = w1_sb[:, st0 + 3776:st0 + 3776 + B * KEYS].rearrange("p (b k) -> p b k", b=B)
        PAIR = B * HEADS * 2 * KEYS
        w2_sb = wide[:, 0:NE * FC * D]
        XN0 = NJ // 2 * PAIR - NT * D
        xn_all = wide[:, XN0:XN0 + NT * D].rearrange("p (t d) -> p t d", d=D)
        y_all = xn_all
        wk1, wv1 = mat(wide, (NE - 1) * FC * D), mat(wide, (NE - 1) * FC * D + 512)
        flat = s_sb[:, :, :].rearrange("p a c -> p (a c)")
        ptf = pt_sb[:, :, :].rearrange("p a c -> p (a c)")
        ctx_at = 4 * UP - B * D
        ctx_sb = flat[0:KEYS, ctx_at:ctx_at + B * D].rearrange("p (b d) -> p b d", b=B)
        b1_raw = flat[0:NE * FC, ctx_at - 384:ctx_at - 256]
        gw_raw = flat[0:NE, ctx_at - 256:ctx_at]
        dft = [mat(flat, 512 * i) for i in range(3)]
        ctxT = ptf[:, 0:DC * B * CTX_COPIES * KEYS].rearrange("p (cb n) -> p cb n", cb=DC * B)
        kb_at = DC * B * CTX_COPIES * KEYS
        kb_sb = ptf[:, kb_at:kb_at + DC * B * KEYS].rearrange("p (c n) -> p c n", c=DC)
        wfr = on_sb[:, :, :]
        wfi = oT_sb[:, :, :, :].rearrange("p b c n -> p b (c n)")
        arT = xn_sb[:, :, :]
        aiT = qT_sb[:, :, :, :].rearrange("p b c n -> p b (c n)")
        xs_sb, xsT_sb = xn_sb[:, 0, :], xnT_sb
        h_sb = flat[:, 0:FF]
        hT_sb = ptf[:, 0:FF].rearrange("p (c t) -> p c t", c=FC)
        y_sb = flat[:, FF:FF + D]
        s_pad = s_sb[:, :, UK:UP]
        po_x = b2t_sb[:, :]
        po_xT = rows[:, 0, :].rearrange("p (c t) -> p c t", c=DC)
        rt = w1_sb[:, last_w1:last_w1 + 2048].rearrange("p (i n) -> p i n", n=P)

        score_ps = ctx.enter_context(nc.psum_tensor("score_ps", [P, 2, 512], F32))
        pt_ps = ctx.enter_context(nc.psum_tensor("pt_ps", [P, 2, 512], F32))
        o_ps = ctx.enter_context(nc.psum_tensor("o_ps", [P, B, 512], F32))
        in_ps = ctx.enter_context(nc.psum_tensor("in_ps", [P, 512], F32))
        out_ps = ctx.enter_context(nc.psum_tensor("out_ps", [P, 512], F32))


        xs_dram = dram("sorted_x", [MT * P, D])
        ys_dram = dram("sorted_y", [MT * P, D])
        zero_sb = b2t_sb[:, :]

        cst_in, ctx_in, col_in, row_in, small_in, pad_in = [
            sem(n) for n in ("cst_in", "ctx_in", "col_in", "row_in", "small_in", "pad_in")]
        x_in = [sem("x_in0"), sem("x_in1")]
        raw_in = [sem(f"raw_in{i}") for i in range(4)]
        bias_in = [sem(f"bias_in{i}") for i in range(NJ // 2)]
        bias_ready = sem("bias_ready")
        zero_ready, zeroed = sem("zero_ready"), sem("zeroed")
        w1_in, w2_in, w_last_in = sem("w1_in"), sem("w2_in"), sem("w_last_in")
        l1w_in, l1q_in, dft_in, ctx1_in = [sem(n) for n in ("l1w_in", "l1q_in", "dft_in", "ctx1_in")]
        tg_ready, rows_ready = sem("tg_ready"), sem("rows_ready")
        flags_made, flags_read = sem("flags_made"), sem("flags_read")
        pads_ready, pen_made, pen_done = sem("pads_ready"), sem("pen_made"), sem("pen_done")
        wT_done, wT_ev = sem("wT_done"), sem("wT_ev")
        sm_done, sm_ev = sem("sm_done"), sem("sm_ev")
        bv_in, gb_in, col1_in, power_ready, pads_read = [
            sem(n) for n in ("bv_in", "gb_in", "col1_in", "power_ready", "pads_read")]
        dve_step = sem("dve_step")
        names = ("ctx_T ctx_ev k_done kbd_ready v_done v_ready in_st in_mv in_ve in_rs scored s_taken maxed "
                 "exp_done pt_done pt_ev pv_done rs_ready on_done oT_done oT_ev wo_done resid po_st po_mv "
                 "po_ve po_rs po_xn po_T po_ev po_done po_read xn_done xnT_done xnT_ev q_done q_ev xb_done").split()
        L = [{n: sem(f"{n}_{l}") for n in names} for l in range(2)]
        subbed, in_x, fb_done = sem("subbed"), sem("in_x"), sem("fb_done")
        kept, xna_done, hot, ranked, slots, scattered = [
            sem(n) for n in ("kept", "xna_done", "hot", "ranked", "slots", "scattered")]
        ar_done, ar_ev, m_done, m_ready = sem("ar_done"), sem("ar_ev"), sem("m_done"), sem("m_ready")
        xs_in, b2_in, xsT_done, xsT_ev, h_done, h_ev_a, h_ev_v, hT_done, hT_ev_a, hT_ev_v, y_done, y_ev, y_out = [
            sem(n) for n in ("xs_in", "b2_in", "xsT_done", "xsT_ev", "h_done", "h_ev_a", "h_ev_v", "hT_done",
                             "hT_ev_a", "hT_ev_v", "y_done", "y_ev", "y_out")]
        gathered = [sem(f"gathered{i}") for i in range(NJ)]
        y_ready, x_out = sem("y_ready"), sem("x_out")

        def wait(eng, s, value):
            if not isinstance(value, int) or value > 0:
                eng.wait_ge(s, value)

        def unit_on(j, k, back=0):
            return not isinstance(j, int) or 0 <= 4 * j + k - back < UNITS

        def tile_on(j, m):
            return not isinstance(j, int) or 0 <= m < NT

        def attention_steps(eng, body):
            for j in range(3):
                for k in range(4):
                    body(j, k)
            with eng.Fori(3, NJ - 1) as j:
                for k in range(4):
                    body(j, k)
            for step in range(4 * (NJ - 1), 2 * (NT - 1) + LAG_POST + 3):
                body(step // 4, step % 4)

        ident = cst[:, C_ID:C_ID + P]
        W = dict(q=a["L0_xattn_wq"], k=a["L0_xattn_wk"], v=a["L0_xattn_wv"], o=a["L0_xattn_wo"])
        x_v = a["x"].rearrange("b (p j) d -> p b j d", j=NJ)
        out_v = out.rearrange("b (p j) d -> p b j d", j=NJ)
        bias_v = a["fside_Bx16xSxS2_0"].rearrange("b h (p j) k -> b p h (j k)", j=NJ)
        ctx_v = a["ctx_1024"].rearrange("b k d -> k b d")

        def bcast(row):
            return row.rearrange("(o n) -> o n", o=1).to_broadcast([P, row.shape[0]])

        def bias_heads(j, b, h0, n):
            at = (j // 2) * PAIR + b * HEADS * 2 * KEYS + h0 * 2 * KEYS
            v = wide[:, bass.ds(at, n * 2 * KEYS)].rearrange("p (h i k) -> p h i k", h=n, i=2)
            return v[:, :, bass.ds(j % 2, 1), :]

        def ptT(w):
            return pt_ps[0:TW, w // 4, w % 4 * P:(w % 4 + 1) * P]

        def at_most_tiles(j, count):
            return min(count, NT) if isinstance(j, int) else count

        block = ctx.enter_context(nc.Block())

        @block.sync
        def _(sp):
            sp.dma_start(cst[:, :], a["c_all"][:, 0:C_SMALL]).then_inc(cst_in, 16)
            sp.dma_start(ctx_sb, ctx_v).then_inc(ctx_in, 16)

            def load_raw(i):
                sp.dma_start(raw[i], W["kqvo"[i]].rearrange("(c p) n -> p c n", c=DC)).then_inc(raw_in[i], 16)

            def load_bias(i):
                for b in range(B):
                    at = i * PAIR + b * HEADS * 2 * KEYS
                    sp.dma_start(wide[:, at:at + HEADS * 2 * KEYS].rearrange("p (h n) -> p h n", h=HEADS),
                                 bias_v[b, :, :, 2 * i * KEYS:2 * (i + 1) * KEYS]).then_inc(bias_in[i], 16)

            load_raw(0)
            load_raw(1)
            for i in range(2):
                part = slice(0, 2) if i == 0 else slice(2, NJ)
                for b in range(B):
                    xb = x_sb[:, b * NJ:(b + 1) * NJ, :]
                    sp.dma_start(xb[:, part, :], x_v[:, b, part, :]).then_inc(x_in[i], 16)
                if i == 0:
                    load_bias(0)
                    load_raw(2)
                    load_raw(3)
            load_bias(1)
            sp.dma_start(b1_raw, a["L0_ffn_b1"].rearrange("e (c p) -> (e c) p", c=FC)).then_inc(small_in, 16)
            sp.dma_start(gw_raw, a["L0_ffn_gate_w"]).then_inc(small_in, 16)
            for i in range(2, NJ // 2):
                load_bias(i)

            def load_w1(e, s):
                sp.dma_start(w1_sb[:, e * DC * FF:(e + 1) * DC * FF].rearrange("p (c n) -> p c n", c=DC),
                             a["L0_ffn_w1"][e].rearrange("(c p) n -> p c n", c=DC)).then_inc(s, 16)

            def load_w2(e, s):
                sp.dma_start(w2_sb[:, e * FC * D:(e + 1) * FC * D].rearrange("p (c n) -> p c n", c=FC),
                             a["L0_ffn_w2"][e].rearrange("(c p) n -> p c n", c=FC)).then_inc(s, 16)

            sp.wait_ge(zero_ready, 1)
            sp.dma_start(xs_dram.rearrange("(r p) d -> p r d", p=P),
                         zero_sb.unsqueeze(1).to_broadcast([P, MT, D])).then_inc(zeroed, 16)
            for e in range(5):
                load_w1(e, w1_in)
            sp.wait_ge(wT_ev, 4)
            sp.wait_ge(L[0]["k_done"], 1)
            sp.wait_ge(L[0]["v_done"], B)
            sp.wait_ge(flags_made, 1)
            for e in (5, 6):
                load_w1(e, w1_in)
            for i in range(NJ // 2):
                sp.wait_ge(bias_in[i], 16 * B)
                sp.sem_inc(bias_ready, 1)
            for e in range(NE - 1):
                last_pair = ((e + 1) * FC * D - 1) // PAIR
                sp.wait_ge(L[0]["s_taken"], 8 * (last_pair + 1))
                load_w2(e, w2_in)
            sp.wait_ge(L[0]["s_taken"], UNITS)
            sp.dma_start(wk1, a["L1_xattn_Wk"].rearrange("(c p) n -> p c n", c=DC)).then_inc(l1w_in, 16)
            sp.dma_start(wv1, a["L1_xattn_Wv"].rearrange("(c p) n -> p c n", c=DC)).then_inc(l1w_in, 16)
            sp.wait_ge(L[0]["pt_done"], UNITS)
            for i in range(3):
                sp.dma_start(dft[i], a["c_dft"][i].rearrange("(c p) n -> p c n", c=DC)).then_inc(dft_in, 16)
            sp.dma_start(ctx_sb, ctx_v).then_inc(ctx1_in, 16)
            sp.wait_ge(L[0]["wo_done"], NT)
            sp.dma_start(wfr, a["L1_ffn_w_freq_real"].rearrange("(c p) n -> p c n", c=DC)).then_inc(dft_in, 16)
            sp.dma_start(wfi, a["L1_ffn_w_freq_imag"].rearrange("(c p) n -> p c n", c=DC)).then_inc(dft_in, 16)
            sp.dma_start(wq_sb[:, :, :], a["L1_xattn_Wq"].rearrange("(c p) n -> p c n", c=DC)).then_inc(l1q_in, 16)
            sp.dma_start(wo_sb[:, :, :], a["L1_xattn_Wo"].rearrange("(c p) n -> p c n", c=DC)).then_inc(l1q_in, 16)
            sp.wait_ge(L[0]["po_done"], NT)
            sp.dma_start(rows[0:1, 0, :], bcast(a["L1_xattn_bv"])[0:1]).then_inc(l1w_in, 16)
            sp.wait_ge(slots, 2)
            load_w1(NE - 1, w_last_in)
            sp.wait_ge(L[1]["k_done"], 1)
            sp.wait_ge(L[1]["v_done"], B)
            sp.wait_ge(scattered, 16 * NT)
            def load_xs(t):
                wait(sp, xsT_done, t)
                sp.dma_start(xs_sb, xs_dram[bass.ds(t * P, P), :]).then_inc(xs_in, 16)

            sp.wait_ge(m_done, 1)
            load_xs(0)
            load_w2(NE - 1, w_last_in)
            load_xs(1)
            with sp.Fori(2, MT) as t:
                load_xs(t)
            for i in range(NJ):
                sp.wait_ge(gathered[i], 16 * B)
                sp.sem_inc(y_ready, B)
            with sp.Fori(0, NJ) as j:
                for b in range(B):
                    sp.wait_ge(L[1]["po_read"], 2 * j + b + 1)
                    sp.dma_start(out_v[:, b, bass.ds(j, 1), :], x_sb[:, bass.ds(b * NJ + j, 1), :]).then_inc(x_out, 16)
            sp.wait_ge(x_out, 16 * NT)

        @block.tensor
        def _(pe):
            def prepare(l):
                s = L[l]
                wk, wv = (wkT, wvT) if l == 0 else (wk1, wv1)
                pe.wait_ge(ctx_in if l == 0 else ctx1_in, 16)
                for c in range(DC):
                    for b in range(B):
                        at = (c * B + b) * KEYS
                        t = nc.tensor.transpose(score_ps[:, 1, at:at + KEYS], ctx_sb[:, b, c * P:(c + 1) * P],
                                                ident[0:KEYS, 0:KEYS])
                t.then_inc(s["ctx_T"], 1)
                pe.wait_ge(s["ctx_ev"], 1)
                if l == 0:
                    pe.wait_ge(wT_ev, 1)
                else:
                    pe.wait_ge(l1w_in, 16 * 3)
                for oc in range(DC):
                    for ic in range(DC):
                        t = nc.tensor.matmul(score_ps[:, 0, oc * B * KEYS:(oc + 1) * B * KEYS],
                                             wk[:, ic, oc * P:(oc + 1) * P], ctxT[:, ic * B:(ic + 1) * B, 0:KEYS],
                                             start=(ic == 0), stop=(ic == DC - 1))
                t.then_inc(s["k_done"], 1)
                if l == 0:
                    turn_weights(2, 4)
                    pe.wait_ge(wT_ev, 3)
                    pe.wait_ge(bv_in, 16)
                for b in range(B):
                    for w in range(NW):
                        f, key = FIRST_HEAD[w] * HD, w * TW % KEYS
                        out_ = pt_ps[0:TW, b, w * DC * WH * HD:(w + 1) * DC * WH * HD].rearrange(
                            "p (c n) -> p c n", c=DC)
                        for ic in range(DC):
                            nc.tensor.matmul(out_, ctxT[:, ic * B + b, key:key + TW],
                                             wv[:, ic, :].rearrange("p (c n) -> p c n", c=DC)[:, :, f:f + WH * HD],
                                             start=(ic == 0), stop=False)
                        t = nc.tensor.matmul(out_, cst[0:1, C_ONE:C_ONE + TW],
                                             rows[0:1, 0, :].rearrange("p (c n) -> p c n", c=DC)[:, :, f:f + WH * HD],
                                             start=False, stop=True)
                    t.then_inc(s["v_done"], 1)

            def attend(l):
                s = L[l]

                def transpose_x(m, b):
                    pe.wait_ge(s["xn_done"], m + 1)
                    wait(pe, s["q_ev"], m)
                    for c in range(DC):
                        t = nc.tensor.transpose(in_ps[:, c * P:(c + 1) * P], xn_sb[:, b, c * P:(c + 1) * P], ident)
                    t.then_inc(s["xnT_done"], 1)

                def project_q(m):
                    pe.wait_ge(s["xnT_ev"], m + 1)
                    for oc in range(DC):
                        for ic in range(DC):
                            t = nc.tensor.matmul(in_ps[:, oc * P:(oc + 1) * P], wq_sb[:, ic, oc * P:(oc + 1) * P],
                                                 xnT_sb[:, ic, :], start=(ic == 0), stop=(ic == DC - 1))
                    t.then_inc(s["q_done"], 1)

                if l == 0:
                    pe.wait_ge(wT_ev, 2)
                else:
                    pe.wait_ge(l1q_in, 32)
                transpose_x(0, 0)
                project_q(0)
                transpose_x(1, 1)
                if l == 0:
                    pe.wait_ge(s["kbd_ready"], QH)

                def step(j, k):
                    if unit_on(j, k):
                        c, b = k % 2, k // 2
                        if c == 0:
                            pe.wait_ge(s["q_ev"], 2 * j + b + 1)
                        wait(pe, s["s_taken"], 4 * j + k)
                        for h in range(2):
                            t = nc.tensor.matmul(
                                score_ps[:, h, 0:QK], qT_sb[64 * h:64 * h + 64, b, c, :],
                                kbd[64 * h:64 * h + 64, c, b, :, :].rearrange("p h k -> p (h k)"),
                                start=True, stop=True)
                        t.then_inc(s["scored"], 1)
                    if k % 2 == 0:
                        m = 2 * j + k // 2 + 1
                        if tile_on(j, m):
                            project_q(m)
                    if unit_on(j, k, LAG_T):
                        k2 = (k - LAG_T) % 4
                        pe.wait_ge(s["exp_done"], 4 * j + k - LAG_T + 1)
                        wait(pe, s["pt_ev"], 4 * j + k - LAG_T)
                        for w in range(NW):
                            t = nc.tensor.transpose(ptT(w), s_sb[:, k2, w * TW:(w + 1) * TW], ident)
                        t.then_inc(s["pt_done"], 1)
                    if k % 2 == 0:
                        m = 2 * j + (k - LAG_POST - 1) // 2
                        if tile_on(j, m):
                            rhs, n = (gwT, NE) if l == 0 else (m_sb, D)
                            pe.wait_ge(s["po_ev"], m + 1)
                            if tile_on(j, 2 * j + k // 2 - 3):
                                pe.wait_ge(s["oT_ev"], 2 * j + k // 2 - 2)
                            for c in range(DC):
                                t = nc.tensor.matmul(out_ps[:, D:D + n], po_xT[:, c, :], rhs[:, c, :],
                                                     start=(c == 0), stop=(c == DC - 1))
                            t.then_inc(s["po_done"], 1)
                        m = 2 * j + k // 2 - 3
                        if tile_on(j, m):
                            b = (k // 2 + 1) % 2
                            pe.wait_ge(s["oT_ev"], m + 1)
                            for ic in range(DC):
                                t = nc.tensor.matmul(out_ps[:, 0:D], oT_sb[:, b, ic, :], wo_sb[:, ic, :],
                                                     start=(ic == 0), stop=(ic == DC - 1))
                            t.then_inc(s["wo_done"], 1)
                    else:
                        m = 2 * j + (k - LAG_POST) // 2
                        if tile_on(j, m):
                            pe.wait_ge(s["po_xn"], m + 1)
                            wait(pe, s["po_read"], m)
                            pe.wait_ge(s["resid"], at_most_tiles(j, m + 2))
                            for c in range(DC):
                                t = nc.tensor.transpose(out_ps[:, c * P:(c + 1) * P], po_x[:, c * P:(c + 1) * P],
                                                        ident)
                            t.then_inc(s["po_T"], 1)
                    if unit_on(j, k, LAG_V):
                        kv = (k - LAG_V) % 4
                        c, b = kv % 2, kv // 2
                        u = 4 * j + k - LAG_V
                        pe.wait_ge(s["pt_ev"], u + 1)
                        if c == 0:
                            wait(pe, s["on_done"], 2 * j + (k - LAG_V) // 2 - 1)
                        if l == 0 and isinstance(j, int) and u == 0:
                            pe.wait_ge(s["v_ready"], B * (DC + 1))
                        for w in range(NW):
                            at = (c * UH + FIRST_HEAD[w]) * HV
                            t = nc.tensor.matmul(
                                o_ps[:, b, at:at + WH * HV], pt_sb[0:TW, kv % 2, w * P:(w + 1) * P],
                                vblk[0:TW, b, w, c, :, :].rearrange("p h e -> p (h e)"),
                                start=(w == 0), stop=(w == NW - 1), skip_group_check=True)
                        t.then_inc(s["pv_done"], 1)
                    if k % 2 == 1:
                        m, b = 2 * j + (k - 1) // 2 - 2, (k - 1) // 2
                        if tile_on(j, m):
                            pe.wait_ge(s["on_done"], m + 1)
                            wait(pe, s["resid"], m)
                            if tile_on(j, m - 2):
                                pe.wait_ge(s["po_ev"], m - 1)
                            for c in range(DC):
                                t = nc.tensor.transpose(out_ps[:, c * P:(c + 1) * P],
                                                        on_sb[:, b, c * P:(c + 1) * P], ident)
                            t.then_inc(s["oT_done"], 1)
                        m = 2 * j + (k - 1) // 2 + 2
                        if tile_on(j, m):
                            transpose_x(m, b)

                attention_steps(pe, step)

            def turn_weights(first, last):
                for i in range(first, last):
                    pe.wait_ge(raw_in[i], 16)
                    if i >= 2:
                        pe.wait_ge(wT_ev, i - 1)
                    bank = in_ps if i % 2 == 0 else out_ps
                    for ic in range(DC):
                        for oc in range(DC):
                            at = (ic * DC + oc) * P
                            t = nc.tensor.transpose(bank[:, at:at + P], raw[i][:, oc, ic * P:(ic + 1) * P], ident)
                    t.then_inc(wT_done, 1)

            pe.wait_ge(cst_in, 16)
            turn_weights(0, 2)
            prepare(0)
            pe.wait_ge(small_in, 16 * 2)
            for c in range(DC):
                nc.tensor.transpose(o_ps[:, 0, c * NE:(c + 1) * NE], gw_raw[:, c * P:(c + 1) * P], ident[0:NE, 0:NE])
            nc.tensor.transpose(o_ps[:, 0, DC * NE:DC * NE + NE * FC], b1_raw,
                                ident[0:NE * FC, 0:NE * FC]).then_inc(sm_done, 1)
            pe.wait_ge(wT_ev, 4)
            pe.wait_ge(sm_ev, 2)
            attend(0)

            pe.wait_ge(hot, 1)
            nc.tensor.matmul(o_ps[:, 1, 0:P], cst[:, C_TRI:C_TRI + P], rt[:, 2, :], start=True, stop=True)
            nc.tensor.matmul(o_ps[:, 1, P:2 * P], cst[:, C_ONE:C_ONE + P], rt[:, 2, :],
                             start=True, stop=True).then_inc(ranked, 1)
            pe.wait_ge(dft_in, 16 * 5)
            for part, (one, two) in enumerate((((wfr, dft[0]), (wfi, dft[1])), ((wfi, dft[0]), (wfr, dft[2])))):
                for oc in range(DC):
                    n = 0
                    for w, f in (one, two):
                        for ic in range(DC):
                            i = nc.tensor.matmul(score_ps[:, part, oc * D:(oc + 1) * D], w[:, ic, oc * P:(oc + 1) * P],
                                                 f[:, ic, :], start=(n == 0), stop=(n == 2 * DC - 1))
                            n += 1
                i.then_inc(ar_done, 1)
            pe.wait_ge(ar_ev, 2)
            for oc in range(DC):
                n = 0
                for w, f in ((arT, dft[0]), (aiT, dft[2])):
                    for ic in range(DC):
                        i = nc.tensor.matmul(pt_ps[:, 0, oc * D:(oc + 1) * D], w[:, ic, oc * P:(oc + 1) * P],
                                             f[:, ic, :], start=(n == 0), stop=(n == 2 * DC - 1))
                        n += 1
            i.then_inc(m_done, 1)
            pe.wait_ge(m_ready, 1)
            prepare(1)

            for s_, v in ((w1_in, 16 * 7), (w2_in, 16 * 7), (w_last_in, 16 * 2)):
                pe.wait_ge(s_, v)
            pe.wait_ge(L[1]["kbd_ready"], QH)
            pe.wait_ge(L[1]["v_ready"], B * DC)

            def turn_xs(t):
                pe.wait_ge(xs_in, 16 * (t + 1))
                wait(pe, xsT_ev, t)
                for c in range(DC):
                    i = nc.tensor.transpose(in_ps[:, c * P:(c + 1) * P], xs_sb[:, c * P:(c + 1) * P], ident)
                i.then_inc(xsT_done, 1)

            def expert(t):
                return pe.value_load(tile_e[0:1, bass.ds(t, 1)], min_val=0, max_val=NE - 1)

            def hidden(t, e):
                pe.wait_ge(xsT_ev, t + 1)
                wait(pe, h_ev_a, t)
                wait(pe, h_ev_v, t)
                for c in range(DC):
                    for n in range(2):
                        i = nc.tensor.matmul(score_ps[:, n, :], xsT_sb[:, c, :],
                                             w1_sb[:, bass.ds(e * (DC * FF) + c * FF + n * 512, 512)],
                                             start=(c == 0), stop=(c == DC - 1))
                i.then_inc(h_done, 1)

            def turn_h(t):
                pe.wait_ge(h_ev_a, t + 1)
                pe.wait_ge(h_ev_v, t + 1)
                wait(pe, hT_ev_a, t)
                wait(pe, hT_ev_v, t)
                for f in range(FC):
                    i = nc.tensor.transpose(pt_ps[:, f // 4, f % 4 * P:(f % 4 + 1) * P],
                                            h_sb[:, f * P:(f + 1) * P], ident)
                i.then_inc(hT_done, 1)

            def outputs(t, e):
                pe.wait_ge(hT_ev_a, t + 1)
                pe.wait_ge(hT_ev_v, t + 1)
                wait(pe, y_ev, t)
                for f in range(FC):
                    i = nc.tensor.matmul(o_ps[:, 0, 0:D], hT_sb[:, f, :],
                                         w2_sb[:, bass.ds(e * (FC * D) + f * D, D)],
                                         start=(f == 0), stop=(f == FC - 1))
                i.then_inc(y_done, 1)

            turn_xs(0)
            hidden(0, expert(0))
            turn_xs(1)

            def turn(t):
                e, e_next = expert(t), expert(t + 1)
                turn_h(t)
                hidden(t + 1, e_next)
                if not isinstance(t, int) or t + 2 < MT:
                    turn_xs(t + 2)
                outputs(t, e)

            turn(0)
            with pe.Fori(1, MT - 2) as t:
                turn(t)
            turn(MT - 2)
            turn_h(MT - 1)
            outputs(MT - 1, expert(MT - 1))
            attend(1)

        @block.scalar
        def _(act):
            def copy(out_, in_, s):
                nc.scalar.activation(out_, in_, ACT.Copy).then_inc(s, 1)

            def attend(l):
                s = L[l]

                def keep_xT(m):
                    act.wait_ge(s["xnT_done"], m + 1)
                    wait(act, s["q_done"], m)
                    copy(xnT_sb[:, :, :].rearrange("p c t -> p (c t)"), in_ps[:, 0:D], s["xnT_ev"])

                def keep_q(m, b):
                    act.wait_ge(s["q_done"], m + 1)
                    wait(act, s["scored"], 2 * m - 2)
                    nc.scalar.activation(qT_sb[:, b, 0, :], in_ps[:, 0:P], ACT.Identity, bias=cols[:, 4 * l:4 * l + 1])
                    nc.scalar.activation(qT_sb[:, b, 1, :], in_ps[:, P:2 * P], ACT.Identity,
                                         bias=cols[:, 4 * l + 1:4 * l + 2]).then_inc(s["q_ev"], 1)

                keep_xT(0)
                keep_q(0, 0)

                def step(j, k):
                    if k % 2 == 0:
                        m, b = 2 * j + k // 2 - 3, (k // 2 + 1) % 2
                        if tile_on(j, m):
                            act.wait_ge(s["oT_done"], m + 1)
                            copy(oT_sb[:, b, :, :].rearrange("p c t -> p (c t)"), out_ps[:, 0:D], s["oT_ev"])
                        m = 2 * j + k // 2 + 1
                        if tile_on(j, m):
                            keep_xT(m)
                    else:
                        m = 2 * j + (k - 1) // 2 + 1
                        if tile_on(j, m):
                            keep_q(m, ((k - 1) // 2 + 1) % 2)
                    if unit_on(j, k, 1):
                        kk = (k - 1) % 4
                        act.wait_ge(subbed if l == 0 else s["s_taken"], 4 * j + k)
                        nc.scalar.activation(s_sb[:, kk, 0:UK], s_sb[:, kk, 0:UK], ACT.Exp).then_inc(s["exp_done"], 1)
                    if unit_on(j, k, 2):
                        act.wait_ge(s["pt_done"], 4 * j + k - 1)
                        wait(act, s["pv_done"], 4 * j + k - 3)
                        copy(pt_sb[0:TW, k % 2, :], pt_ps[0:TW, :, :].rearrange("p a n -> p (a n)")[:, 0:NW * P],
                             s["pt_ev"])
                    if k % 2 == 1:
                        m = 2 * j + (k - LAG_POST) // 2
                        if tile_on(j, m):
                            act.wait_ge(s["po_T"], m + 1)
                            wait(act, s["po_done"], m)
                            copy(po_xT.rearrange("p c t -> p (c t)"), out_ps[:, 0:D], s["po_ev"])

                attention_steps(act, step)

            act.dma_start(cols[:, 2:4], a["L0_xattn_bk"].rearrange("(c p) -> p c", c=DC),
                          allow_slow_non_contiguous=True).then_inc(col_in, 16)
            act.dma_start(cols[:, 0:2], a["L0_xattn_bq"].rearrange("(c p) -> p c", c=DC),
                          allow_slow_non_contiguous=True).then_inc(col_in, 16)
            act.dma_start(causal, a["c_all"][:, C_CAUSAL:C_ALL].rearrange("p (j k) -> p j k", j=NJ)).then_inc(pad_in, 16)
            act.dma_start(padraw.rearrange("p b k -> p (b k)"),
                          bcast(a["mask_BxS2_bf0"].rearrange("b k -> (b k)"))).then_inc(pad_in, 16)
            act.dma_start(rows[0:1, 0, :], bcast(a["L0_xattn_bv"])[0:1]).then_inc(bv_in, 16)
            act.dma_start(tg[:, 0:4:2], bcast(a["g_xattn"]), allow_slow_non_contiguous=True).then_inc(row_in, 16)
            act.dma_start(tg[:, 1:4:2], bcast(a["g_ffn"]), allow_slow_non_contiguous=True).then_inc(row_in, 16)
            for i, n in enumerate(("L0_xattn_bo", "L1_xattn_bo", "L1_ffn_bias")):
                act.dma_start(rows[:, i + 1, :], bcast(a[n])).then_inc(row_in, 16)
            for i in range(2):
                n = ("L0_ffn_gate_b", "L0_ffn_expert_bias")[i]
                act.dma_start(gb[:, i, :], bcast(a[n])).then_inc(gb_in, 16)
            for i, n in enumerate(("L1_xattn_bq", "L1_xattn_bk")):
                act.dma_start(cols[:, 4 + 2 * i:6 + 2 * i], a[n].rearrange("(c p) -> p c", c=DC),
                              allow_slow_non_contiguous=True).then_inc(col1_in, 16)

            def keep_weights(first, last):
                for i in range(first, last):
                    act.wait_ge(wT_done, i + 1)
                    dst = (wkT, wq_sb[:, :, :], wvT, wo_sb[:, :, :])[i]
                    copy(dst.rearrange("p c n -> p (c n)"), (in_ps if i % 2 == 0 else out_ps)[:, :], wT_ev)

            def keep_context(l):
                s = L[l]
                act.wait_ge(s["ctx_T"], 1)
                for r in range(CTX_COPIES):
                    i = nc.scalar.activation(ctxT[:, :, r * KEYS:(r + 1) * KEYS],
                                             score_ps[:, 1, 0:DC * B * KEYS].rearrange("p (c k) -> p c k", c=DC * B),
                                             ACT.Copy)
                i.then_inc(s["ctx_ev"], 1)

            keep_weights(0, 2)
            keep_context(0)
            keep_weights(2, 4)
            act.wait_ge(row_in, 16 * 5)
            nc.scalar.activation(tg[:, :], tg[:, :], ACT.Tanh).then_inc(tg_ready, 1)
            act.wait_ge(sm_done, 1)
            copy(gwT[:, :, :].rearrange("p c e -> p (c e)"), o_ps[:, 0, 0:DC * NE], sm_ev)
            copy(b1T[:, :], o_ps[:, 0, DC * NE:DC * NE + NE * FC], sm_ev)
            act.wait_ge(col_in, 16 * 2)
            attend(0)

            act.wait_ge(ar_done, 2)
            copy(arT.rearrange("p b n -> p (b n)"), score_ps[:, 0, :], ar_ev)
            copy(aiT.rearrange("p b n -> p (b n)"), score_ps[:, 1, :], ar_ev)
            act.wait_ge(m_done, 1)
            nc.scalar.activation(m_sb[:, :, :].rearrange("p c n -> p (c n)"), pt_ps[:, 0, :], ACT.Copy,
                                 scale=1.0 / D).then_inc(m_ready, 1)
            keep_context(1)

            def keep_xs(t):
                act.wait_ge(xsT_done, t + 1)
                wait(act, h_done, t)
                copy(xsT_sb[:, :, :].rearrange("p c t -> p (c t)"), in_ps[:, 0:D], xsT_ev)

            def keep_h(t):
                act.wait_ge(h_done, t + 1)
                wait(act, hT_done, t)
                copy(h_sb[:, 0:512], score_ps[:, 0, :], h_ev_a)

            def relu_h(t):
                e = act.value_load(tile_e[0:1, bass.ds(t, 1)], min_val=0, max_val=NE - 1)
                act.wait_ge(hT_done, t + 1)
                wait(act, y_done, t)
                for f in range(4):
                    i = nc.scalar.activation(hT_sb[:, f, :], pt_ps[:, 0, f * P:(f + 1) * P], ACT.Relu,
                                             bias=b1T[:, bass.ds(e * FC + f, 1)])
                i.then_inc(hT_ev_a, 1)

            act.wait_ge(slots, 2)
            act.wait_ge(L[1]["kbd_ready"], QH)
            act.wait_ge(L[1]["v_ready"], B * DC)
            act.wait_ge(col1_in, 16 * 2)
            keep_xs(0)
            keep_h(0)
            keep_xs(1)
            relu_h(0)
            keep_h(1)
            keep_xs(2)
            with act.Fori(1, MT - 2) as t:
                relu_h(t)
                keep_h(t + 1)
                keep_xs(t + 2)
            relu_h(MT - 2)
            keep_h(MT - 1)
            relu_h(MT - 1)

            attend(1)

        @block.gpsimd
        def _(pool):
            def scatter(t):
                pool.wait_ge(xna_done, t + 1)
                nc.gpsimd.indirect_dma_start(out=xs_dram, out_offset=bass.IndirectOffsetOnAxis(slot_u[:, t:t + 1], 0),
                                             in_=xn_all[:, t, :], in_offset=None).then_inc(scattered, 16)

            def gather(m):
                t = m % B * NJ + m // B
                nc.gpsimd.indirect_dma_start(out=y_all[:, t, :], out_offset=None, in_=ys_dram,
                                             in_offset=bass.IndirectOffsetOnAxis(slot_u[:, t:t + 1], 0)
                                             ).then_inc(gathered[m // B], 16)

            def make_rstd(s, m, b, mv_, ve, rs, done, name):
                pool.wait_ge(s[name + "_mv"], m + 1)
                wait(pool, s[done], m - 1)
                nc.gpsimd.tensor_tensor(ve[:, b:b + 1], mv_[:, b, 1:2], power[:, 1:2], ALU.add).then_inc(s[name + "_ve"], 1)
                pool.wait_ge(s[name + "_ve"], m + 1)
                nc.gpsimd.tensor_tensor(rs[:, b:b + 1], ve[:, b:b + 1], power[:, 0:1], ALU.pow).then_inc(s[name + "_rs"], 1)

            def rstd_in(s, m, b):
                make_rstd(s, m, b, in_mv, in_ve, in_rs, "xn_done", "in")

            nc.gpsimd.memset(power[:, 0:1], -0.5)
            nc.gpsimd.memset(power[:, 1:2], EPS).then_inc(power_ready, 1)
            nc.gpsimd.memset(zero_sb, 0.0).then_inc(zero_ready, 1)
            pool.wait_ge(pad_in, 16 * 2)
            nc.gpsimd.tensor_copy(padrow, padraw).then_inc(pads_read, 1)
            pool.wait_ge(pads_read, 1)
            for b in range(B):
                i = nc.gpsimd.tensor_tensor(pen[:, b, :, :], causal,
                                            padrow[:, b, :].unsqueeze(1).to_broadcast([P, NJ, KEYS]), ALU.add)
            i.then_inc(flags_made, 1)
            pool.wait_ge(power_ready, 1)
            rstd_in(L[0], 0, 0)
            rstd_in(L[0], 1, 1)

            def penalize(j, b, c):
                if c == 0:
                    pool.wait_ge(bias_ready, j // 2 + 1)
                v = bias_heads(j, b, c * UH, UH)[:, :, 0, :]
                nc.gpsimd.tensor_tensor(v, v, pen[:, b, bass.ds(j, 1), :].to_broadcast([P, UH, KEYS]),
                                        ALU.add).then_inc(pen_done, 1)

            def attend(l):
                s = L[l]

                def add_bo(j, b, m):
                    pool.wait_ge(s["xn_done"], m + 1)
                    xt = x_sb[:, bass.ds(b * NJ + j, 1), :]
                    nc.gpsimd.tensor_tensor(xt, xt, rows[:, 1 + l:2 + l, :], ALU.add).then_inc(s["xb_done"], 1)

                pool.wait_ge(rows_ready, 3)
                add_bo(0, 0, 0)
                add_bo(0, 1, 1)

                def step(j, k):
                    if l == 1 and isinstance(j, int):
                        for m in range(GATHERED_FIRST + 3 * (4 * j + k) // 2, GATHERED_FIRST + 3 * (4 * j + k + 1) // 2):
                            if m < NT:
                                gather(m)
                    if k % 2 == 0:
                        m = 2 * j + k // 2 + 2
                        if tile_on(j, m):
                            rstd_in(s, m, k // 2)
                    else:
                        m, b = 2 * j + (k - 7) // 2, (k - 7) // 2 % 2
                        if tile_on(j, m):
                            make_rstd(s, m, b, po_mv, po_ve, po_rs, "po_xn", "po")
                            if l == 0:
                                jm = j + (k - 7) // 4
                                pool.wait_ge(s["po_rs"], m + 1)
                                nc.gpsimd.tensor_copy(mean_all[:, bass.ds(b * NJ + jm, 1)], po_mv[:, b, 0:1])
                                nc.gpsimd.tensor_copy(rstd_all[:, bass.ds(b * NJ + jm, 1)],
                                                      po_rs[:, b:b + 1]).then_inc(kept, 1)
                    if l == 0 and unit_on(j, k):
                        pool.wait_ge(s["maxed"], 4 * j + k + 1)
                        v = s_sb[:, k, 0:UK].rearrange("p (h k) -> p h k", h=UH)
                        nc.gpsimd.tensor_tensor(v, v, mx_sb[:, k, :].unsqueeze(2).to_broadcast([P, UH, KEYS]),
                                                ALU.subtract).then_inc(subbed, 1)
                    if k % 2 == 1:
                        m, b = 2 * j + (k - 1) // 2 + 2, k // 2
                        if tile_on(j, m):
                            add_bo(j + 1, b, m)
                        m, b = 2 * j + (k - LAG_POST) // 2, (k - LAG_POST) // 2 % 2
                        if l == 1 and tile_on(j, m):
                            pool.wait_ge(s["po_xn"], m + 1)
                            xt = x_sb[:, bass.ds(b * NJ + j + (k - LAG_POST) // 4, 1), :]
                            nc.gpsimd.tensor_tensor(xt, xt, rows[:, 3:4, :], ALU.add).then_inc(fb_done, 1)
                    if l == 0 and tile_on(j, 2 * j + k // 2 + 2):
                        penalize(j + 1, k // 2, k % 2)

                if l == 0:
                    pool.wait_ge(pen_made, 1)
                    for b in range(B):
                        for c in range(2):
                            penalize(0, b, c)
                    pool.wait_ge(L[0]["ctx_T"], 1)
                    pool.wait_ge(sm_done, 1)
                pool.wait_ge(y_out, 16 * MT) if l == 1 else None
                nc.gpsimd.memset(s_pad, 0.0).then_inc(pads_ready, 1)
                attention_steps(pool, step)

            attend(0)
            pool.wait_ge(slots, 2)
            pool.wait_ge(zeroed, 16)
            for t in range(NT):
                scatter(t)

            def store_y(t):
                pool.wait_ge(y_ev, t + 1)
                pool.dma_start(ys_dram[bass.ds(t * P, P), :], y_sb).then_inc(y_out, 16)

            def load_b2(t):
                e = pool.value_load(tile_e[0:1, bass.ds(t, 1)], min_val=0, max_val=NE - 1)
                pool.dma_start(b2t_sb[:, :], a["L0_ffn_b2"][bass.ds(e, 1), :].to_broadcast([P, D])).then_inc(b2_in, 16)

            pool.wait_ge(L[0]["po_done"], NT)
            load_b2(0)
            with pool.Fori(0, MT - 1) as t:
                store_y(t)
                load_b2(t + 1)
            store_y(MT - 1)
            pool.wait_ge(y_out, 16 * MT)
            for m in range(GATHERED_FIRST):
                gather(m)
            rstd_in(L[1], 0, 0)
            rstd_in(L[1], 1, 1)
            attend(1)

        @block.vector
        def _(dve):
            steps = [0]

            def link(i):
                steps[0] += 1
                i.then_inc(dve_step, 1)
                dve.wait_ge(dve_step, steps[0])

            def stats_in(l, j, b, m):
                s = L[l]
                xt = x_sb[:, bass.ds(b * NJ + j, 1), :]
                if l == 1:
                    dve.wait_ge(y_ready, m + 1)
                    nc.vector.scalar_tensor_tensor(out=xt, in0=y_all[:, bass.ds(b * NJ + j, 1), :], scalar=tg[:, 1:2],
                                                   in1=xt, op0=ALU.mult, op1=ALU.add).then_inc(in_x, 1)
                    dve.wait_ge(x_in[1], 16 * B)
                    dve.wait_ge(in_x, m + 1)
                nc.vector.bn_stats(in_st[:, b, :], xt).then_inc(s["in_st"], 1)
                dve.wait_ge(s["in_st"], m + 1)

            def aggregate_in(s, b):
                nc.vector.bn_aggr(in_mv[:, b, :], in_st[:, b, :]).then_inc(s["in_mv"], 1)

            def norm_x(l, j, b, m):
                s = L[l]
                dve.wait_ge(s["in_rs"], m + 1)
                wait(dve, s["xnT_done"], m - 1)
                nc.vector.tensor_scalar(xn_sb[:, b:b + 1, :], x_sb[:, bass.ds(b * NJ + j, 1), :],
                                        in_mv[:, b, 0:1], in_rs[:, b:b + 1],
                                        ALU.subtract, ALU.mult).then_inc(s["xn_done"], 1)

            def prepare(l):
                s = L[l]
                dve.wait_ge(s["k_done"], 1)
                if l == 0:
                    dve.wait_ge(cst_in, 16)
                    dve.wait_ge(col_in, 16 * 2)
                else:
                    dve.wait_ge(col1_in, 16 * 2)
                for c in range(DC):
                    i = nc.vector.tensor_scalar(kb_sb[:, c, :], score_ps[:, 0, c * B * KEYS:(c + 1) * B * KEYS],
                                                cols[:, 4 * l + 2 + c:4 * l + 3 + c], HD ** -0.5, ALU.add, ALU.mult)
                link(i)
                for h in range(QH):
                    nc.vector.tensor_scalar(kbd[:, :, :, h, :].rearrange("p c b k -> p (c b) k"),
                                            kb_sb.rearrange("p c (b k) -> p (c b) k", b=B),
                                            cst[:, C_KM + h:C_KM + h + 1], None, ALU.mult).then_inc(s["kbd_ready"], 1)

            def prepare_values(l):
                s = L[l]
                vmask = cst[0:TW, C_VM:C_VM + NW * WH].rearrange("p (w h) -> p w h", w=NW)
                for b in range(B):
                    dve.wait_ge(s["v_done"], b + 1)
                    for c in range(DC):
                        if l == 0 and c == 0:
                            nc.vector.tensor_copy(vblk[0:TW, b, :, :, :, HD],
                                                  vmask.unsqueeze(2).to_broadcast([TW, NW, DC, WH])
                                                  ).then_inc(s["v_ready"], 1)
                        pv = pt_ps[0:TW, b, 0:NW * DC * WH * HD].rearrange("p (w c h d) -> p w c h d", w=NW, c=DC, h=WH)
                        nc.vector.tensor_tensor(vblk[0:TW, b, :, c, :, 0:HD], pv[:, :, c, :, :],
                                                vmask.unsqueeze(3).to_broadcast([TW, NW, WH, HD]),
                                                ALU.mult).then_inc(s["v_ready"], 1)

            dve.wait_ge(x_in[0], 16 * B)
            for b in range(B):
                stats_in(0, 0, b, b)
                aggregate_in(L[0], b)
            norm_x(0, 0, 0, 0)
            norm_x(0, 0, 1, 1)
            prepare(0)
            dve.wait_ge(flags_made, 1)
            nc.vector.tensor_reduce(no_key[:, :], pen.rearrange("p b j k -> p (b j) k"), AX_X,
                                    ALU.min).then_inc(flags_read, 1)
            dve.wait_ge(flags_read, 1)
            nc.vector.tensor_scalar(pen.rearrange("p b j k -> p (b j k)"), pen.rearrange("p b j k -> p (b j k)"),
                                    MASKED, None, ALU.mult).then_inc(pen_made, 1)
            link(nc.vector.tensor_scalar(no_key[:, :], no_key[:, :], 3e38, 10.0, ALU.mult, ALU.mult))
            link(nc.vector.tensor_scalar(no_key[:, :], no_key[:, :], 0.0, None, ALU.mult))
            dve.wait_ge(tg_ready, 1)
            for i, g in ((1, 0), (2, 2), (3, 3)):
                nc.vector.tensor_scalar(rows[:, i, :], rows[:, i, :], tg[:, g:g + 1], None, ALU.mult
                                        ).then_inc(rows_ready, 1)
            prepare_values(0)
            dve.wait_ge(x_in[1], 16 * B)
            dve.wait_ge(gb_in, 16 * 2)

            def attend(l):
                s = L[l]
                dve.wait_ge(pads_ready, l + 1)

                def step(j, k):
                    if k % 2 == 0:
                        m = 2 * j + k // 2 + 2
                        if tile_on(j, m):
                            stats_in(l, j + 1, k // 2, m)
                    else:
                        m, b = 2 * j + (k - 1) // 2 - 2, (k - 1) // 2
                        if tile_on(j, m):
                            ov = o_ps[:, b, 0:HEADS * HV].rearrange("p (h e) -> p h e", e=HV)
                            dve.wait_ge(s["pv_done"], 2 * m + 2)
                            nc.vector.reciprocal(rs_sb[:, :], ov[:, :, HD]).then_inc(s["rs_ready"], 1)
                            dve.wait_ge(s["rs_ready"], m + 1)
                            wait(dve, s["oT_done"], m - 1)
                            onv = on_sb[:, b, :].rearrange("p (h d) -> p h d", d=HD)
                            rsv = rs_sb[:, :].unsqueeze(2).to_broadcast([P, HEADS, HD])
                            if l == 0:
                                nc.vector.scalar_tensor_tensor(
                                    out=onv, in0=ov[:, :, 0:HD], scalar=no_key[:, bass.ds(b * NJ + j - 1, 1)],
                                    in1=rsv, op0=ALU.add, op1=ALU.mult).then_inc(s["on_done"], 1)
                            else:
                                nc.vector.tensor_tensor(onv, ov[:, :, 0:HD], rsv, ALU.mult).then_inc(s["on_done"], 1)
                        m, b = 2 * j + (k - 7) // 2, (k - 7) // 2 % 2
                        if tile_on(j, m):
                            t = b * NJ + j + (k - 7) // 4
                            xt = x_sb[:, bass.ds(t, 1), :]
                            dve.wait_ge(s["wo_done"], m + 1)
                            dve.wait_ge(s["xb_done"], m + 1)
                            nc.vector.scalar_tensor_tensor(
                                out=xt, in0=out_ps[:, 0:D].unsqueeze(1), scalar=tg[:, 2 * l:2 * l + 1], in1=xt,
                                op0=ALU.mult, op1=ALU.add).then_inc(s["resid"], 1)
                        m, b = 2 * j + (k - 11) // 2, (k - 11) // 2 % 2
                        if tile_on(j, m):
                            t = b * NJ + j + (k - 11) // 4
                            dve.wait_ge(s["po_done"], m + 1)
                            if l == 0:
                                nc.vector.tensor_tensor(logit[:, bass.ds(t, 1), :], out_ps[:, D:D + NE].unsqueeze(1),
                                                        gb[:, 0:1, :], ALU.add).then_inc(s["po_read"], 1)
                            else:
                                xt = x_sb[:, bass.ds(t, 1), :]
                                dve.wait_ge(fb_done, m + 1)
                                nc.vector.scalar_tensor_tensor(
                                    out=xt, in0=out_ps[:, D:2 * D].unsqueeze(1), scalar=tg[:, 3:4], in1=xt,
                                    op0=ALU.mult, op1=ALU.add).then_inc(s["po_read"], 1)
                        m, b = 2 * j + (k - 7) // 2, (k - 7) // 2 % 2
                        if tile_on(j, m):
                            xt = x_sb[:, bass.ds(b * NJ + j + (k - 7) // 4, 1), :]
                            dve.wait_ge(x_in[1], 16 * B)
                            dve.wait_ge(s["resid"], m + 1)
                            nc.vector.bn_stats(po_st[:, b, :], xt).then_inc(s["po_st"], 1)
                            dve.wait_ge(s["po_st"], m + 1)

                    def aggregate():
                        if k % 2 == 0 and tile_on(j, 2 * j + k // 2 + 2):
                            aggregate_in(s, k // 2)
                        if k % 2 == 1 and tile_on(j, 2 * j + (k - 7) // 2):
                            b = (k - 7) // 2 % 2
                            nc.vector.bn_aggr(po_mv[:, b, :], po_st[:, b, :]).then_inc(s["po_mv"], 1)

                    if not unit_on(j, k):
                        aggregate()
                    else:
                        c, b = k % 2, k // 2
                        sv = s_sb[:, k, 0:UK].rearrange("p (q h k) -> p q h k", q=2, h=QH)
                        pv = score_ps[:, :, 0:QK].rearrange("p q (h k) -> p q h k", h=QH)
                        dve.wait_ge(s["scored"], 4 * j + k + 1)
                        wait(dve, s["pt_done"], 4 * j + k - 3)
                        if l == 0:
                            dve.wait_ge(pen_done, 4 * j + k + 1)
                            nc.vector.tensor_tensor(
                                sv, pv, bias_heads(j, b, UH * c, UH).rearrange("p (q h) i k -> p q h (i k)", q=2),
                                ALU.add).then_inc(s["s_taken"], 1)
                            aggregate()
                            dve.wait_ge(s["s_taken"], 4 * j + k + 1)
                            wait(dve, subbed, 4 * j + k - 3)
                            nc.vector.tensor_reduce(mx_sb[:, k, :], s_sb[:, k, 0:UK].rearrange("p (h k) -> p h k", h=UH),
                                                    AX_X, ALU.max).then_inc(s["maxed"], 1)
                        else:
                            mq = mx_sb[:, k, :].rearrange("p (q h) -> p q h", q=2)
                            nc.vector.tensor_reduce(mq, pv, AX_X, ALU.max).then_inc(s["maxed"], 1)
                            aggregate()
                            dve.wait_ge(s["maxed"], 4 * j + k + 1)
                            nc.vector.tensor_tensor(
                                sv, pv, mq.unsqueeze(3).to_broadcast([P, 2, QH, KEYS]), ALU.subtract
                            ).then_inc(s["s_taken"], 1)
                    if k % 2 == 0:
                        m = 2 * j + k // 2 + 2
                        if tile_on(j, m):
                            norm_x(l, j + 1, k // 2, m)
                    else:
                        m, b = 2 * j + (k - 7) // 2, (k - 7) // 2 % 2
                        if tile_on(j, m):
                            t = b * NJ + j + (k - 7) // 4
                            dve.wait_ge(s["po_rs"], m + 1)
                            wait(dve, s["po_T"], m)
                            if l == 0:
                                wait(dve, kept, m)
                            if l == 0 and isinstance(j, int) and m == 0:
                                dve.wait_ge(zeroed, 16)
                            nc.vector.tensor_scalar(po_x.unsqueeze(1), x_sb[:, bass.ds(t, 1), :],
                                                    po_mv[:, b, 0:1], po_rs[:, b:b + 1],
                                                    ALU.subtract, ALU.mult).then_inc(s["po_xn"], 1)

                attention_steps(dve, step)

            attend(0)

            def te(i):
                return rt[:, i, :].rearrange("p (t e) -> p t e", e=NE)

            def et(i):
                return rt[:, i, :].rearrange("p (e t) -> p e t", e=NE)

            def c8(at):
                return cst[:, at:at + NE].unsqueeze(1).to_broadcast([P, NT, NE])

            dve.wait_ge(L[0]["po_read"], NT)
            dve.wait_ge(pen_done, UNITS)
            link(nc.vector.tensor_tensor(te(0), logit[:, :, :], gb[:, 1, :].unsqueeze(1).to_broadcast([P, NT, NE]),
                                         ALU.add))
            top = rt[:, 3, 0:NT]
            link(nc.vector.tensor_reduce(top, te(0), AX_X, ALU.max))
            link(nc.vector.tensor_tensor(te(1), te(0), top.unsqueeze(2).to_broadcast([P, NT, NE]), ALU.is_equal))
            link(nc.vector.tensor_tensor(te(1), te(1), c8(C_RANK), ALU.mult))
            link(nc.vector.tensor_tensor(te(1), te(1), c8(C_LAST), ALU.max))
            link(nc.vector.tensor_reduce(top, te(1), AX_X, ALU.max))
            nc.vector.tensor_tensor(te(2), te(1), top.unsqueeze(2).to_broadcast([P, NT, NE]),
                                    ALU.is_equal).then_inc(hot, 1)
            dve.wait_ge(ranked, 1)
            link(nc.vector.tensor_copy(et(4), o_ps[:, 1, P:2 * P].rearrange("p (t e) -> p e t", e=NE)))
            link(nc.vector.tensor_tensor_scan(rt[:, 5, :], cst[:, C_RESET:C_RESET + P], rt[:, 4, :], 0.0,
                                              ALU.mult, ALU.add))
            link(nc.vector.tensor_tensor(et(6), et(5)[:, :, NT - 1:NT].to_broadcast([P, NE, NT]),
                                         cst[:, C_THR:C_THR + NT].unsqueeze(1).to_broadcast([P, NE, NT]),
                                         ALU.is_gt))
            n_tiles, ends, start = rt[:, 7, 0:NE], rt[:, 7, 16:16 + NE], rt[:, 7, 32:32 + NE]
            link(nc.vector.tensor_reduce(n_tiles, et(6), AX_X, ALU.add))
            link(nc.vector.tensor_tensor_scan(ends, cst[:, C_ONE:C_ONE + NE], n_tiles, 0.0, ALU.mult, ALU.add))
            link(nc.vector.tensor_tensor(start, ends, n_tiles, ALU.subtract))
            link(nc.vector.tensor_scalar(start, start, float(P), None, ALU.mult))
            link(nc.vector.tensor_tensor(rt[:, 5, :], rt[:, 5, :], rt[:, 4, :], ALU.subtract))
            link(nc.vector.tensor_tensor(et(5), et(5), start.unsqueeze(2).to_broadcast([P, NE, NT]), ALU.add))
            link(nc.vector.tensor_tensor(te(8), o_ps[:, 1, 0:P].rearrange("p (t e) -> p t e", e=NE),
                                         rt[:, 5, :].rearrange("p (e t) -> p t e", e=NE), ALU.add))
            link(nc.vector.tensor_tensor(te(8), te(8), te(2), ALU.mult))
            link(nc.vector.tensor_reduce(top, te(8), AX_X, ALU.add))
            link(nc.vector.tensor_copy(slot_u[:, :], top))
            cmp_ = rt[:, 9:11, :].rearrange("p i n -> p (i n)")[:, 0:MT * (NE - 1)].rearrange("p (t e) -> p t e", t=MT)
            link(nc.vector.tensor_tensor(cmp_, cst[:, C_TILE:C_TILE + MT].unsqueeze(2).to_broadcast([P, MT, NE - 1]),
                                         ends[:, 0:NE - 1].unsqueeze(1).to_broadcast([P, MT, NE - 1]), ALU.is_ge))
            link(nc.vector.tensor_reduce(rt[:, 11, 0:MT], cmp_, AX_X, ALU.add))
            nc.vector.tensor_copy(tile_e[:, 0:MT], rt[:, 11, 0:MT]).then_inc(slots, 2)
            dve.wait_ge(kept, NT)
            for t in range(NT):
                nc.vector.tensor_scalar(xn_all[:, t, :], x_sb[:, t, :], mean_all[:, t:t + 1], rstd_all[:, t:t + 1],
                                        ALU.subtract, ALU.mult).then_inc(xna_done, 1)

            prepare(1)
            prepare_values(1)

            def keep_h(t):
                dve.wait_ge(h_done, t + 1)
                wait(dve, hT_done, t)
                nc.vector.tensor_copy(h_sb[:, 512:1024], score_ps[:, 1, :]).then_inc(h_ev_v, 1)

            def relu_h(t):
                e = dve.value_load(tile_e[0:1, bass.ds(t, 1)], min_val=0, max_val=NE - 1)
                dve.wait_ge(hT_done, t + 1)
                wait(dve, y_done, t)
                for f in range(4, FC):
                    i = nc.vector.tensor_scalar(hT_sb[:, f, :], pt_ps[:, 1, (f - 4) * P:(f - 3) * P],
                                                b1T[:, bass.ds(e * FC + f, 1)], 0.0, ALU.add, ALU.max)
                i.then_inc(hT_ev_v, 1)

            def keep_y(t):
                dve.wait_ge(y_done, t + 1)
                dve.wait_ge(b2_in, 16 * (t + 1))
                wait(dve, y_out, 16 * t)
                nc.vector.tensor_tensor(y_sb, o_ps[:, 0, 0:D], b2t_sb[:, :], ALU.add).then_inc(y_ev, 1)

            dve.wait_ge(dft_in, 16 * 5)
            dve.wait_ge(m_done, 1)
            dve.wait_ge(L[1]["ctx_T"], 1)
            keep_h(0)
            relu_h(0)
            keep_h(1)
            keep_y(0)
            with dve.Fori(1, MT - 2) as t:
                relu_h(t)
                keep_h(t + 1)
                keep_y(t)
            relu_h(MT - 2)
            keep_h(MT - 1)
            keep_y(MT - 2)
            relu_h(MT - 1)
            keep_y(MT - 1)
            for b in range(B):
                stats_in(1, 0, b, b)
                aggregate_in(L[1], b)
            norm_x(1, 0, 0, 0)
            norm_x(1, 0, 1, 1)
            attend(1)


_INS = ['x', 'ctx_1024', 'fside_Bx16xSxS2_0', 'mask_BxS2_bf0', 'g_xattn', 'g_ffn',
        'L0_xattn_wq', 'L0_xattn_bq', 'L0_xattn_wk', 'L0_xattn_bk', 'L0_xattn_wv', 'L0_xattn_bv',
        'L0_xattn_wo', 'L0_xattn_bo', 'L0_ffn_gate_w', 'L0_ffn_gate_b', 'L0_ffn_expert_bias',
        'L0_ffn_w1', 'L0_ffn_b1', 'L0_ffn_w2', 'L0_ffn_b2',
        'L1_xattn_Wq', 'L1_xattn_bq', 'L1_xattn_Wk', 'L1_xattn_bk', 'L1_xattn_Wv', 'L1_xattn_bv',
        'L1_xattn_Wo', 'L1_xattn_bo', 'L1_ffn_w_freq_real', 'L1_ffn_w_freq_imag', 'L1_ffn_bias']


def _constants():
    import numpy as np
    c = np.zeros((P, C_ALL), np.float32)
    p = np.arange(P)
    c[:, C_ID:C_ID + P] = np.eye(P)
    c[:, C_TRI:C_TRI + P] = p[:, None] < p[None, :]
    c[:, C_ONE:C_ONE + P] = 1.0
    c[:, C_KM:C_KM + QH] = (p[:, None] % 64) // HD == np.arange(QH)
    for w in range(NW):
        head = (w * TW + p[:TW, None]) // KEYS
        c[:TW, C_VM + w * WH:C_VM + (w + 1) * WH] = head == FIRST_HEAD[w] + np.arange(WH)
    c[:, C_RANK:C_RANK + NE] = NE - np.arange(NE)
    c[:, C_LAST + NE - 1] = 1.0
    c[:, C_RESET:C_RESET + P] = p % NT != 0
    c[:, C_THR:C_THR + NT] = P * np.arange(NT)
    c[:, C_TILE:C_TILE + MT] = np.arange(MT)
    query = p[:, None, None] * NJ + np.arange(NJ)[None, :, None]
    c[:, C_CAUSAL:C_ALL] = np.where(np.arange(KEYS)[None, None, :] > query, 1.0, 0.0).reshape(P, -1)
    angle = 2 * np.pi * (np.outer(np.arange(D), np.arange(D)) % D) / D
    dft = np.stack([np.cos(angle), np.sin(angle), -np.sin(angle)]).astype(np.float32)
    return c, dft


def kernel(**inputs):
    import numpy as _np
    import concourse.bacc as _bacc
    from concourse import mybir as _mybir
    from concourse.bass_utils import run_bass_kernel_spmd as _run

    nc = _bacc.Bacc("TRN2", target_bir_lowering=False, num_devices=1)
    arrays, args = {}, {}
    c_all, c_dft = _constants()
    for name, value in [(n, inputs[n]) for n in _INS] + [("c_all", c_all), ("c_dft", c_dft)]:
        v = _np.ascontiguousarray(value)
        arrays[f"in_{name}_dram"] = v
        args[name] = nc.dram_tensor(f"in_{name}_dram", v.shape, _mybir.dt.from_np(v.dtype), kind="ExternalInput").ap()
    out = nc.dram_tensor("out_0_dram", (B, S, D), F32, kind="ExternalOutput").ap()
    flamingo_kernel(nc, args, out)
    r = _run(nc, [arrays], core_ids=[0])
    return r.results[0]["out_0_dram"]
```

```python
from contextlib import ExitStack

import concourse.bass as bass
from concourse import mybir

ALU = mybir.AluOpType
ACT = mybir.ActivationFunctionType
AX_X = mybir.AxisListType.X
F32 = mybir.dt.float32
F32R = mybir.dt.float32r
U32 = mybir.dt.uint32
I32 = mybir.dt.int32
U8 = mybir.dt.uint8

P = 128
B, S, D = 2, 1024, 256
KEYS = 77
HEADS, HD = 16, 16
NJ = S // P
NT = B * NJ
DC = D // P
QH = 4
QK = QH * KEYS
HALF = P // 2
UH = 8
UK = UH * KEYS
NW = 5
TW = -(-UK // NW)
UP = NW * TW
WH = 3
HV = HD + 1
FIRST_HEAD = [min(w * TW // KEYS, UH - WH) for w in range(NW)]
NE, FF = 8, 1024
FC = FF // P
MT = NT + NE - 1
LAG_T, LAG_V = 2, 3
GATHERED_FIRST = 6
LAG_POST = 9
UNITS = 2 * NT
CTX_COPIES = 3
WIDE = B * HEADS * NJ * KEYS
EPS = 1e-5
MASKED = -1e38

C_ID, C_TRI, C_ONE, C_KM, C_VM = 0, P, 2 * P, 3 * P, 3 * P + QH
C_RANK = C_VM + NW * WH
C_LAST, C_RESET = C_RANK + NE, C_RANK + 2 * NE
C_THR = C_RESET + P
C_TILE = C_THR + NT
C_SMALL = C_TILE + MT
C_CAUSAL = C_SMALL
C_ALL = C_CAUSAL + NJ * KEYS


def flamingo_kernel(nc, a, out):
    with ExitStack() as ctx:
        def sb(name, shape, dt=F32):
            return ctx.enter_context(nc.sbuf_tensor(name, shape, dt))

        def sem(name):
            return ctx.enter_context(nc.semaphore(name))

        def dram(name, shape):
            return nc.dram_tensor(name, shape, F32, kind="Internal").ap()

        w1_sb = sb("w1_sb", [P, NE * DC * FF])
        with nc.sbuf_tensor("wide", [P, WIDE], F32) as wide:
            pass
        kparts_sb = sb("kparts_sb", [P, 2 * (HEADS // QH) * B * QK], F32R)
        qparts_sb = sb("qparts_sb", [P, B * (HEADS // QH) * P], F32R)
        sb("wide_rest", [P, WIDE - (HEADS // QH) * B * (2 * QK + P)])
        x_sb = sb("x_sb", [P, NT, D])
        s_sb = sb("s_sb", [P, 4, UP])
        pt_sb = sb("pt_sb", [P, 2, NW * P])
        xn_sb = sb("xn_sb", [P, B, D])
        xnT_sb = sb("xnT_sb", [P, DC, P])
        qT_sb = sb("qT_sb", [P, B, DC, P])
        on_sb = sb("on_sb", [P, B, D])
        oT_sb = sb("oT_sb", [P, B, DC, P])
        b2t_sb = sb("b2t_sb", [P, D])
        kbd = sb("kbd", [P, DC, B, QH, KEYS])
        vblk = sb("vblk", [P, B, NW, DC, WH, HV])
        wq_sb = sb("wq_sb", [P, DC, D])
        wo_sb = sb("wo_sb", [P, DC, D])
        m_sb = sb("m_sb", [P, DC, D])
        cst = sb("cst", [P, C_SMALL])
        rows = sb("rows", [P, 4, D])
        mx_sb = sb("mx_sb", [P, 4, 8])
        rs_sb = sb("rs_sb", [P, HEADS])
        no_key = sb("no_key", [P, NT])
        in_st, in_mv = sb("in_st", [P, B, 6]), sb("in_mv", [P, B, 2])
        in_ve, in_rs = sb("in_ve", [P, B]), sb("in_rs", [P, B])
        po_st, po_mv = sb("po_st", [P, B, 6]), sb("po_mv", [P, B, 2])
        po_ve, po_rs = sb("po_ve", [P, B]), sb("po_rs", [P, B])
        mean_all, rstd_all = sb("mean_all", [P, NT]), sb("rstd_all", [P, NT])
        logit = sb("logit", [P, NT, NE])
        power = sb("power", [P, 2])
        cols = sb("cols", [P, 8])
        tg = sb("tg", [P, 4])
        b1T = sb("b1T", [P, NE * FC])
        gwT = sb("gwT", [P, DC, NE])
        gb = sb("gb", [P, 2, NE])
        slot_u = sb("slot_u", [P, NT], U32)
        tile_e = sb("tile_e", [P, MT + 1], I32)

        last_w1 = (NE - 1) * DC * FF
        pen = w1_sb[:, last_w1:last_w1 + B * NJ * KEYS].rearrange("p (b j k) -> p b j k", b=B, j=NJ)
        st0 = 5 * DC * FF

        def mat(t, at):
            return t[:, at:at + DC * D].rearrange("p (c n) -> p c n", c=DC)

        def mat_ff(t, at):
            return t[:, at:at + DC * FF].rearrange("p (c n) -> p c n", c=DC)

        raw = [mat(w1_sb, st0 + 512 * i) for i in range(4)]
        wkT, wvT = mat(w1_sb, st0 + 2048), mat(w1_sb, st0 + 2560)
        causal = w1_sb[:, st0 + 3072:st0 + 3072 + NJ * KEYS].rearrange("p (j k) -> p j k", j=NJ)
        padraw = w1_sb[:, st0 + 3712:st0 + 3712 + 64].bitcast(U8)[:, 0:B * KEYS].rearrange("p (b k) -> p b k", b=B)
        padrow = w1_sb[:, st0 + 3776:st0 + 3776 + B * KEYS].rearrange("p (b k) -> p b k", b=B)
        PAIR = B * HEADS * 2 * KEYS
        w2_sb = wide[:, 0:NE * FC * D]
        XN0 = NJ // 2 * PAIR - NT * D
        xn_all = wide[:, XN0:XN0 + NT * D].rearrange("p (t d) -> p t d", d=D)
        NQ = HEADS // QH
        kb2 = kbd[:, :, :, :, :].rearrange("p c b h k -> p (c b h k)")[:, 0:NQ * B * KEYS].rearrange(
            "p (g b k) -> p g b k", g=NQ, b=B)
        kparts = kparts_sb[:, :].rearrange("p (i g b n) -> p i g b n", i=2, g=NQ, b=B)
        qparts = qparts_sb[:, :].rearrange("p (b g t) -> p b g t", b=B, g=NQ)
        W2_OVER = -(-(NE * FC * D - XN0) // D)
        y_all = xn_all
        wk1, wv1 = mat(wide, (NE - 1) * FC * D), mat(wide, (NE - 1) * FC * D + DC * D)
        sp0 = NJ // 2 * PAIR - 5 * DC * D
        wfr, wfi = mat(wide, sp0), mat(wide, sp0 + DC * D)
        dft = [mat(wide, sp0 + (2 + i) * DC * D) for i in range(3)]
        XN_CLEAR = (sp0 - XN0) // D
        flat = s_sb[:, :, :].rearrange("p a c -> p (a c)")
        ptf = pt_sb[:, :, :].rearrange("p a c -> p (a c)")
        ctx_at = 4 * UP - B * D
        ctx_sb = flat[0:KEYS, ctx_at:ctx_at + B * D].rearrange("p (b d) -> p b d", b=B)
        b1_raw = flat[0:NE * FC, ctx_at - 384:ctx_at - 256]
        gw_raw = flat[0:NE, ctx_at - 256:ctx_at]
        ctxT = ptf[:, 0:DC * B * CTX_COPIES * KEYS].rearrange("p (cb n) -> p cb n", cb=DC * B)
        kb_at = DC * B * CTX_COPIES * KEYS
        kb_sb = ptf[:, kb_at:kb_at + DC * B * KEYS].rearrange("p (c n) -> p c n", c=DC)
        arT = xn_sb[:, :, :]
        aiT = qT_sb[:, :, :, :].rearrange("p b c n -> p b (c n)")
        xs_sb, xsT_sb = xn_sb[:, 0, :], xnT_sb
        w1_tile = [mat_ff(flat, 0), mat_ff(wide, NE * FC * D)]
        hT_sb = [t.rearrange("p (c t) -> p c t", c=FC) for t in (
            ptf[:, 0:FF], wide[:, (NE + 1) * FC * D:(NE + 1) * FC * D + FF])]
        y_sb = flat[:, DC * FF:DC * FF + D]
        s_pad = s_sb[:, :, UK:UP]
        po_x = b2t_sb[:, :]
        po_xT = rows[:, 0, :].rearrange("p (c t) -> p c t", c=DC)
        rt = w1_sb[:, last_w1:last_w1 + 2048].rearrange("p (i n) -> p i n", n=P)

        score_ps = ctx.enter_context(nc.psum_tensor("score_ps", [P, 2, 512], F32))
        pt_ps = ctx.enter_context(nc.psum_tensor("pt_ps", [P, 2, 512], F32))
        o_ps = ctx.enter_context(nc.psum_tensor("o_ps", [P, B, 512], F32))
        in_ps = ctx.enter_context(nc.psum_tensor("in_ps", [P, 512], F32))
        out_ps = ctx.enter_context(nc.psum_tensor("out_ps", [P, 512], F32))


        xs_dram = dram("sorted_x", [MT * P, D])
        ys_dram = dram("sorted_y", [MT * P, D])
        zero_sb = b2t_sb[:, :]

        cst_in, ctx_in, col_in, row_in, small_in, pad_in = [
            sem(n) for n in ("cst_in", "ctx_in", "col_in", "row_in", "small_in", "pad_in")]
        x_in = [sem("x_in0"), sem("x_in1"), sem("x_in2")]
        raw_in = [sem(f"raw_in{i}") for i in range(4)]
        bias_in = [sem(f"bias_in{i}") for i in range(NJ // 2)]
        bias_ready = sem("bias_ready")
        zero_ready, zeroed = sem("zero_ready"), sem("zeroed")
        w1_in, w2_in, w_last_in = sem("w1_in"), sem("w2_in"), sem("w_last_in")
        l1w_in, l1q_in, dft_in, ctx1_in = [sem(n) for n in ("l1w_in", "l1q_in", "dft_in", "ctx1_in")]
        tg_ready, rows_ready = sem("tg_ready"), sem("rows_ready")
        flags_made = sem("flags_made")
        pads_ready, pen_made, pen_done = sem("pads_ready"), sem("pen_made"), sem("pen_done")
        wT_done, wT_ev = sem("wT_done"), sem("wT_ev")
        sm_done, sm_ev = sem("sm_done"), sem("sm_ev")
        col1_in, power_ready, pads_read = [sem(n) for n in ("col1_in", "power_ready", "pads_read")]
        dve_step = sem("dve_step")
        names = ("ctx_T ctx_ev k_done kbd_ready v_done v_ready in_st in_mv in_ve in_rs scored s_taken maxed "
                 "exp_done pt_done pt_ev pv_done rs_ready on_done oT_done oT_ev wo_done resid po_st po_mv "
                 "po_ve po_rs po_xn po_T po_ev po_done po_read xn_done xnT_done xnT_ev q_done q_ev xb_done").split()
        L = [{n: sem(f"{n}_{l}") for n in names} for l in range(2)]
        subbed, in_x, fb_done = sem("subbed"), sem("in_x"), sem("fb_done")
        kept, xna_done, hot, ranked, slots, scattered = [
            sem(n) for n in ("kept", "xna_done", "hot", "ranked", "slots", "scattered")]
        scattered_first = sem("scattered_first")
        ar_done, ar_ev, m_done, m_ready = sem("ar_done"), sem("ar_ev"), sem("m_done"), sem("m_ready")
        xs_in, b2_in, xsT_done, xsT_ev, h_done, hT_ev_a, hT_ev_v, y_done, y_ev, y_out = [
            sem(n) for n in ("xs_in", "b2_in", "xsT_done", "xsT_ev", "h_done", "hT_ev_a", "hT_ev_v",
                             "y_done", "y_ev", "y_out")]
        w1_tile_in = [sem("w1_tile_in0"), sem("w1_tile_in1")]
        gathered = [sem(f"gathered{i}") for i in range(NJ)]
        y_ready, x_out = sem("y_ready"), sem("x_out")
        kparts_ready, q_high, q_low = sem("kparts_ready"), sem("q_high"), sem("q_low")

        def wait(eng, s, value):
            if not isinstance(value, int) or value > 0:
                eng.wait_ge(s, value)

        def unit_on(j, k, back=0):
            return not isinstance(j, int) or 0 <= 4 * j + k - back < UNITS

        def tile_on(j, m):
            return not isinstance(j, int) or 0 <= m < NT

        def attention_steps(eng, body):
            for j in range(3):
                for k in range(4):
                    body(j, k)
            with eng.Fori(3, NJ - 2) as j:
                for k in range(4):
                    body(j, k)
            for step in range(4 * (NJ - 2), 2 * (NT - 1) + LAG_POST + 3):
                body(step // 4, step % 4)

        def expert_turns(eng, turn):
            for t in range(2):
                turn(t, t)
            with eng.Fori(1, (MT - 3) // 2) as i:
                for parity in range(2):
                    turn(2 * i + parity, parity)
            for t in range(MT - 3, MT - 1):
                turn(t, t % 2)

        ident = cst[:, C_ID:C_ID + P]
        W = dict(q=a["L0_xattn_wq"], k=a["L0_xattn_wk"], v=a["L0_xattn_wv"], o=a["L0_xattn_wo"])
        x_v = a["x"].rearrange("b (p j) d -> p b j d", j=NJ)
        out_v = out.rearrange("b (p j) d -> p b j d", j=NJ)
        bias_v = a["fside_Bx16xSxS2_0"].rearrange("b h (p j) k -> b p h (j k)", j=NJ)
        ctx_v = a["ctx_1024"].rearrange("b k d -> k b d")

        def bcast(row):
            return row.rearrange("(o n) -> o n", o=1).to_broadcast([P, row.shape[0]])

        def bias_heads(j, b, h0, n):
            at = (j // 2) * PAIR + b * HEADS * 2 * KEYS + h0 * 2 * KEYS
            v = wide[:, bass.ds(at, n * 2 * KEYS)].rearrange("p (h i k) -> p h i k", h=n, i=2)
            return v[:, :, bass.ds(j % 2, 1), :]

        def ptT(w):
            return pt_ps[0:TW, w // 4, w % 4 * P:(w % 4 + 1) * P]

        def at_most_tiles(j, count):
            return min(count, NT) if isinstance(j, int) else count

        def v_bank(l, b):
            return (o_ps[:, 1, :], out_ps[:, :])[b] if l == 0 else pt_ps[:, b, :]

        h_ps = (score_ps, pt_ps)
        w_banks = (in_ps[:, :], out_ps[:, :], o_ps[:, 0, :], o_ps[:, 1, :])

        block = ctx.enter_context(nc.Block())

        @block.sync
        def _(sp):
            sp.dma_start(cst[:, :], a["c_all"][:, 0:C_SMALL]).then_inc(cst_in, 16)
            sp.dma_start(ctx_sb, ctx_v).then_inc(ctx_in, 16)

            def load_raw(i):
                sp.dma_start(raw[i], W["kqvo"[i]].rearrange("(c p) n -> p c n", c=DC)).then_inc(raw_in[i], 16)

            def load_bias(i):
                for b in range(B):
                    at = i * PAIR + b * HEADS * 2 * KEYS
                    sp.dma_start(wide[:, at:at + HEADS * 2 * KEYS].rearrange("p (h n) -> p h n", h=HEADS),
                                 bias_v[b, :, :, 2 * i * KEYS:2 * (i + 1) * KEYS]).then_inc(bias_in[i], 16)

            load_raw(0)
            load_raw(1)

            def load_x(i, first, last):
                for b in range(B):
                    sp.dma_start(x_sb[:, b * NJ + first:b * NJ + last, :], x_v[:, b, first:last, :]
                                 ).then_inc(x_in[i], 16)

            load_x(0, 0, 2)
            sp.dma_start(b1_raw, a["L0_ffn_b1"].rearrange("e (c p) -> (e c) p", c=FC)).then_inc(small_in, 16)
            sp.dma_start(gw_raw, a["L0_ffn_gate_w"]).then_inc(small_in, 16)
            for i, n in enumerate(("L0_ffn_gate_b", "L0_ffn_expert_bias")):
                sp.dma_start(gb[:, i, :], bcast(a[n])).then_inc(small_in, 16)
            load_raw(2)
            load_bias(0)
            load_raw(3)
            load_x(1, 2, 4)
            load_bias(1)
            load_x(2, 4, NJ)
            for i, n in enumerate(("L1_xattn_bq", "L1_xattn_bk")):
                sp.dma_start(cols[:, 4 + 2 * i:6 + 2 * i], a[n].rearrange("(c p) -> p c", c=DC),
                             allow_slow_non_contiguous=True).then_inc(col1_in, 16)
            for i in range(2, NJ // 2):
                load_bias(i)

            def load_w1(e, s):
                sp.dma_start(w1_sb[:, e * DC * FF:(e + 1) * DC * FF].rearrange("p (c n) -> p c n", c=DC),
                             a["L0_ffn_w1"][e].rearrange("(c p) n -> p c n", c=DC)).then_inc(s, 16)

            def load_w2(e, s):
                sp.dma_start(w2_sb[:, e * FC * D:(e + 1) * FC * D].rearrange("p (c n) -> p c n", c=FC),
                             a["L0_ffn_w2"][e].rearrange("(c p) n -> p c n", c=FC)).then_inc(s, 16)

            sp.wait_ge(zero_ready, 1)
            sp.dma_start(xs_dram.rearrange("(r p) d -> p r d", p=P),
                         zero_sb.unsqueeze(1).to_broadcast([P, MT, D])).then_inc(zeroed, 16)
            for e in range(5):
                load_w1(e, w1_in)
            sp.wait_ge(wT_ev, 4)
            sp.wait_ge(L[0]["k_done"], 1)
            sp.wait_ge(L[0]["v_done"], B)
            sp.wait_ge(flags_made, 1)
            for e in (5, 6):
                load_w1(e, w1_in)
            for i in range(NJ // 2 - 2, NJ // 2):
                sp.wait_ge(bias_in[i], 16 * B)
                sp.sem_inc(bias_ready, i + 1 if i == NJ // 2 - 2 else 1)
            for e in range(NE - 1):
                last_pair = ((e + 1) * FC * D - 1) // PAIR
                sp.wait_ge(L[0]["s_taken"], 8 * (last_pair + 1))
                load_w2(e, w2_in)
            sp.wait_ge(L[0]["s_taken"], UNITS)
            for dst, src in ((dft[0], a["c_dft"][0]), (wfr, a["L1_ffn_w_freq_real"]), (dft[1], a["c_dft"][1]),
                             (wfi, a["L1_ffn_w_freq_imag"]), (dft[2], a["c_dft"][2])):
                sp.dma_start(dst, src.rearrange("(c p) n -> p c n", c=DC)).then_inc(dft_in, 16)
            sp.wait_ge(L[0]["pt_done"], UNITS)
            sp.dma_start(ctx_sb, ctx_v).then_inc(ctx1_in, 16)
            sp.dma_start(wk1, a["L1_xattn_Wk"].rearrange("(c p) n -> p c n", c=DC)).then_inc(l1w_in, 16)
            sp.dma_start(wv1, a["L1_xattn_Wv"].rearrange("(c p) n -> p c n", c=DC)).then_inc(l1w_in, 16)
            sp.wait_ge(L[0]["wo_done"], NT)
            sp.dma_start(wq_sb[:, :, :], a["L1_xattn_Wq"].rearrange("(c p) n -> p c n", c=DC)).then_inc(l1q_in, 16)
            sp.dma_start(wo_sb[:, :, :], a["L1_xattn_Wo"].rearrange("(c p) n -> p c n", c=DC)).then_inc(l1q_in, 16)
            sp.wait_ge(L[0]["po_done"], NT)
            sp.dma_start(rows[0:1, 0, :], bcast(a["L1_xattn_bv"])[0:1]).then_inc(l1w_in, 16)
            sp.wait_ge(slots, 2)
            load_w1(NE - 1, w_last_in)

            def load_xs(t):
                wait(sp, xsT_done, t)
                sp.dma_start(xs_sb, xs_dram[bass.ds(t * P, P), :]).then_inc(xs_in, 16)

            def load_w1_tile(t, parity):
                e = sp.value_load(tile_e[0:1, bass.ds(t, 1)], min_val=0, max_val=NE - 1)
                wait(sp, h_done, 2 * (t - 1))
                sp.dma_start(w1_tile[parity], w1_sb[:, bass.ds(e * (DC * FF), DC * FF)].rearrange(
                    "p (c n) -> p c n", c=DC)).then_inc(w1_tile_in[parity], 16)

            sp.wait_ge(L[1]["k_done"], 1)
            sp.wait_ge(w1_in, 16 * (NE - 1))
            sp.wait_ge(w_last_in, 16)
            load_w1_tile(0, 0)
            sp.wait_ge(L[1]["v_done"], B)
            sp.wait_ge(scattered_first, 16 * W2_OVER)
            load_w2(NE - 1, w_last_in)
            sp.wait_ge(scattered, 16 * (NT - W2_OVER))
            sp.wait_ge(m_done, 1)
            load_xs(0)
            load_w1_tile(1, 1)
            load_xs(1)

            def turn(t, parity):
                load_w1_tile(t + 2, parity)
                load_xs(t + 2)

            for t in range(2):
                turn(t, t)
            with sp.Fori(1, (MT - 3) // 2) as i:
                for parity in range(2):
                    turn(2 * i + parity, parity)
            turn(MT - 3, (MT - 3) % 2)
            for i in range(NJ):
                sp.wait_ge(gathered[i], 16 * B)
                sp.sem_inc(y_ready, B)
            with sp.Fori(0, NJ) as j:
                for b in range(B):
                    sp.wait_ge(L[1]["po_read"], 2 * j + b + 1)
                    sp.dma_start(out_v[:, b, bass.ds(j, 1), :], x_sb[:, bass.ds(b * NJ + j, 1), :]).then_inc(x_out, 16)
            sp.wait_ge(x_out, 16 * NT)

        @block.tensor
        def _(pe):
            def prepare(l):
                s = L[l]
                wk = wkT if l == 0 else wk1
                pe.wait_ge(ctx_in if l == 0 else ctx1_in, 16)
                if l == 1:
                    pe.wait_ge(ar_ev, 2)
                for c in range(DC):
                    for b in range(B):
                        at = (c * B + b) * KEYS
                        t = nc.tensor.transpose(score_ps[:, 1, at:at + KEYS], ctx_sb[:, b, c * P:(c + 1) * P],
                                                ident[0:KEYS, 0:KEYS])
                t.then_inc(s["ctx_T"], 1)
                pe.wait_ge(s["ctx_ev"], 1)
                if l == 0:
                    pe.wait_ge(wT_ev, 1)
                else:
                    pe.wait_ge(l1w_in, 16 * 3)
                for oc in range(DC):
                    for ic in range(DC):
                        t = nc.tensor.matmul(score_ps[:, 0, oc * B * KEYS:(oc + 1) * B * KEYS],
                                             wk[:, ic, oc * P:(oc + 1) * P], ctxT[:, ic * B:(ic + 1) * B, 0:KEYS],
                                             start=(ic == 0), stop=(ic == DC - 1))
                t.then_inc(s["k_done"], 1)

            def prepare_values(l, b):
                s = L[l]
                wv = wvT if l == 0 else wv1
                for w in range(NW):
                    f, key = FIRST_HEAD[w] * HD, w * TW % KEYS
                    out_ = v_bank(l, b)[0:TW, w * DC * WH * HD:(w + 1) * DC * WH * HD].rearrange(
                        "p (c n) -> p c n", c=DC)
                    for ic in range(DC):
                        nc.tensor.matmul(out_, ctxT[:, ic * B + b, key:key + TW],
                                         wv[:, ic, :].rearrange("p (c n) -> p c n", c=DC)[:, :, f:f + WH * HD],
                                         start=(ic == 0), stop=False)
                    t = nc.tensor.matmul(out_, cst[0:1, C_ONE:C_ONE + TW],
                                         rows[0:1, 0, :].rearrange("p (c n) -> p c n", c=DC)[:, :, f:f + WH * HD],
                                         start=False, stop=True)
                t.then_inc(s["v_done"], 1)

            def spectral(part, oc):
                pe.wait_ge(dft_in, 16 * 5)
                one, two = (((wfr, dft[0]), (wfi, dft[1])), ((wfi, dft[0]), (wfr, dft[2])))[part]
                n = 0
                for w, f in (one, two):
                    for ic in range(DC):
                        i = nc.tensor.matmul(score_ps[:, part, oc * D:(oc + 1) * D], w[:, ic, oc * P:(oc + 1) * P],
                                             f[:, ic, :], start=(n == 0), stop=(n == 2 * DC - 1))
                        n += 1
                i.then_inc(ar_done, 1)

            def attend(l):
                s = L[l]

                def transpose_x(m, b):
                    pe.wait_ge(s["xn_done"], m + 1)
                    wait(pe, s["q_ev"], m)
                    for c in range(DC):
                        t = nc.tensor.transpose(in_ps[:, c * P:(c + 1) * P], xn_sb[:, b, c * P:(c + 1) * P], ident)
                    t.then_inc(s["xnT_done"], 1)

                def project_q(m):
                    pe.wait_ge(s["xnT_ev"], m + 1)
                    for oc in range(DC):
                        for ic in range(DC):
                            t = nc.tensor.matmul(in_ps[:, oc * P:(oc + 1) * P], wq_sb[:, ic, oc * P:(oc + 1) * P],
                                                 xnT_sb[:, ic, :], start=(ic == 0), stop=(ic == DC - 1))
                    t.then_inc(s["q_done"], 1)

                if l == 0:
                    pe.wait_ge(wT_ev, 2)
                else:
                    pe.wait_ge(l1q_in, 32)
                    pe.wait_ge(kparts_ready, 2 * QH)
                transpose_x(0, 0)
                project_q(0)
                transpose_x(1, 1)
                if l == 0:
                    turn_weights(2, 4)
                    pe.wait_ge(small_in, 16 * 4)
                    for c in range(DC):
                        nc.tensor.transpose(out_ps[:, c * NE:(c + 1) * NE], gw_raw[:, c * P:(c + 1) * P],
                                            ident[0:NE, 0:NE])
                    nc.tensor.transpose(out_ps[:, DC * NE:DC * NE + NE * FC], b1_raw,
                                        ident[0:NE * FC, 0:NE * FC]).then_inc(sm_done, 1)
                    pe.wait_ge(s["kbd_ready"], QH)

                def step(j, k):
                    if l == 0 and isinstance(j, int) and 0 <= 4 * j + k - UNITS - 3 < 2 * DC:
                        spectral((4 * j + k - UNITS - 3) // DC, (4 * j + k - UNITS - 3) % DC)
                    if l == 0 and isinstance(j, int) and 4 * j + k in (1, 2):
                        if k == 1:
                            pe.wait_ge(wT_ev, 4)
                            pe.wait_ge(col_in, 16 * 3)
                        else:
                            pe.wait_ge(sm_ev, 2)
                        prepare_values(0, k - 1)
                    if unit_on(j, k):
                        c, b = k % 2, k // 2
                        if c == 0:
                            pe.wait_ge(s["q_ev"] if l == 0 else q_low, 2 * j + b + 1)
                        wait(pe, s["s_taken"], 4 * j + k)
                        for h in range(2 if l == 1 else 0):
                            for part in range(2):
                                t = nc.tensor.matmul(
                                    score_ps[:, h, 0:QK], qparts[:, b, 2 * c + h, :], kparts[:, part, 2 * c + h, b, :],
                                    start=(part == 0), stop=(part == 1))
                        for h in range(2 if l == 0 else 0):
                            t = nc.tensor.matmul(
                                score_ps[:, h, 0:QK], qT_sb[64 * h:64 * h + 64, b, c, :],
                                kbd[64 * h:64 * h + 64, c, b, :, :].rearrange("p h k -> p (h k)"),
                                start=True, stop=True)
                        t.then_inc(s["scored"], 1)
                    if k % 2 == 0:
                        m, b = 2 * j + k // 2 - 3, (k // 2 + 1) % 2
                        if tile_on(j, m):
                            pe.wait_ge(s["on_done"], m + 1)
                            wait(pe, s["resid"], m)
                            if tile_on(j, m - 2):
                                pe.wait_ge(s["po_ev"], m - 1)
                            for c in range(DC):
                                t = nc.tensor.transpose(out_ps[:, c * P:(c + 1) * P],
                                                        on_sb[:, b, c * P:(c + 1) * P], ident)
                            t.then_inc(s["oT_done"], 1)
                        m = 2 * j + k // 2 + 1
                        if tile_on(j, m):
                            project_q(m)
                    if unit_on(j, k, LAG_T):
                        k2 = (k - LAG_T) % 4
                        pe.wait_ge(s["exp_done"], 4 * j + k - LAG_T + 1)
                        wait(pe, s["pt_ev"], 4 * j + k - LAG_T)
                        for w in range(NW):
                            t = nc.tensor.transpose(ptT(w), s_sb[:, k2, w * TW:(w + 1) * TW], ident)
                        t.then_inc(s["pt_done"], 1)
                    if k % 2 == 0:
                        m = 2 * j + (k - LAG_POST - 1) // 2
                        if tile_on(j, m):
                            rhs, n = (gwT, NE) if l == 0 else (m_sb, D)
                            pe.wait_ge(s["po_ev"], m + 1)
                            if tile_on(j, 2 * j + k // 2 - 3):
                                pe.wait_ge(s["oT_ev"], 2 * j + k // 2 - 2)
                            for c in range(DC):
                                t = nc.tensor.matmul(out_ps[:, D:D + n], po_xT[:, c, :], rhs[:, c, :],
                                                     start=(c == 0), stop=(c == DC - 1))
                            t.then_inc(s["po_done"], 1)
                        m = 2 * j + k // 2 - 3
                        if tile_on(j, m):
                            b = (k // 2 + 1) % 2
                            pe.wait_ge(s["oT_ev"], m + 1)
                            for ic in range(DC):
                                t = nc.tensor.matmul(out_ps[:, 0:D], oT_sb[:, b, ic, :], wo_sb[:, ic, :],
                                                     start=(ic == 0), stop=(ic == DC - 1))
                            t.then_inc(s["wo_done"], 1)
                    if unit_on(j, k, LAG_V):
                        kv = (k - LAG_V) % 4
                        c, b = kv % 2, kv // 2
                        u = 4 * j + k - LAG_V
                        pe.wait_ge(s["pt_ev"], u + 1)
                        if c == 0:
                            wait(pe, s["on_done"], 2 * j + (k - LAG_V) // 2 - 1)
                        if l == 0 and isinstance(j, int) and u in (0, 2):
                            pe.wait_ge(s["v_ready"], (u // 2 + 1) * (DC + 1))
                        for w in range(NW):
                            at = (c * UH + FIRST_HEAD[w]) * HV
                            t = nc.tensor.matmul(
                                o_ps[:, b, at:at + WH * HV], pt_sb[0:TW, kv % 2, w * P:(w + 1) * P],
                                vblk[0:TW, b, w, c, :, :].rearrange("p h e -> p (h e)"),
                                start=(w == 0), stop=(w == NW - 1), skip_group_check=True)
                        t.then_inc(s["pv_done"], 1)
                    if k % 2 == 1:
                        m = 2 * j + (k - LAG_POST) // 2
                        if tile_on(j, m):
                            pe.wait_ge(s["po_xn"], m + 1)
                            wait(pe, s["po_read"], m)
                            pe.wait_ge(s["resid"], at_most_tiles(j, m + 2))
                            for c in range(DC):
                                t = nc.tensor.transpose(out_ps[:, c * P:(c + 1) * P], po_x[:, c * P:(c + 1) * P],
                                                        ident)
                            t.then_inc(s["po_T"], 1)
                        m, b = 2 * j + (k - 1) // 2 + 2, (k - 1) // 2
                        if tile_on(j, m):
                            transpose_x(m, b)

                attention_steps(pe, step)

            def turn_weights(first, last):
                for i in range(first, last):
                    pe.wait_ge(raw_in[i], 16)
                    bank = w_banks[i]
                    for ic in range(DC):
                        for oc in range(DC):
                            at = (ic * DC + oc) * P
                            t = nc.tensor.transpose(bank[:, at:at + P], raw[i][:, oc, ic * P:(ic + 1) * P], ident)
                    t.then_inc(wT_done, 1)

            pe.wait_ge(cst_in, 16)
            turn_weights(0, 2)
            prepare(0)
            attend(0)

            pe.wait_ge(L[0]["pt_ev"], UNITS)
            pe.wait_ge(ar_ev, 2)
            for oc in range(DC):
                n = 0
                for w, f in ((arT, dft[0]), (aiT, dft[2])):
                    for ic in range(DC):
                        i = nc.tensor.matmul(pt_ps[:, 0, oc * D:(oc + 1) * D], w[:, ic, oc * P:(oc + 1) * P],
                                             f[:, ic, :], start=(n == 0), stop=(n == 2 * DC - 1))
                        n += 1
            i.then_inc(m_done, 1)
            pe.wait_ge(hot, 1)
            nc.tensor.matmul(o_ps[:, 1, 0:P], cst[:, C_TRI:C_TRI + P], rt[:, 2, :], start=True, stop=True)
            nc.tensor.matmul(o_ps[:, 1, P:2 * P], cst[:, C_ONE:C_ONE + P], rt[:, 2, :],
                             start=True, stop=True).then_inc(ranked, 1)
            prepare(1)
            pe.wait_ge(m_ready, 1)
            for b in range(B):
                prepare_values(1, b)

            for s_, v in ((w1_in, 16 * 7), (w2_in, 16 * 7), (w_last_in, 16 * 2)):
                pe.wait_ge(s_, v)
            pe.wait_ge(L[1]["kbd_ready"], QH)
            pe.wait_ge(L[1]["v_ready"], B * DC)

            def turn_xs(t):
                pe.wait_ge(xs_in, 16 * (t + 1))
                wait(pe, xsT_ev, t)
                for c in range(DC):
                    i = nc.tensor.transpose(in_ps[:, c * P:(c + 1) * P], xs_sb[:, c * P:(c + 1) * P], ident)
                i.then_inc(xsT_done, 1)

            def expert(t):
                return pe.value_load(tile_e[0:1, bass.ds(t, 1)], min_val=0, max_val=NE - 1)

            def hidden(t, parity):
                pe.wait_ge(xsT_ev, t + 1)
                pe.wait_ge(w1_tile_in[parity], 16 * (t // 2 + 1))
                wait(pe, hT_ev_a, t - 1)
                wait(pe, hT_ev_v, t - 1)
                for f in range(FC):
                    for c in range(DC):
                        i = nc.tensor.matmul(h_ps[parity][:, f // 4, f % 4 * P:(f % 4 + 1) * P],
                                             w1_tile[parity][:, c, f * P:(f + 1) * P], xsT_sb[:, c, :],
                                             start=(c == 0), stop=(c == DC - 1))
                    if f % 4 == 3:
                        i.then_inc(h_done, 1)

            def outputs(t, parity, e):
                pe.wait_ge(hT_ev_a, t + 1)
                pe.wait_ge(hT_ev_v, t + 1)
                wait(pe, y_ev, t)
                for f in range(FC):
                    i = nc.tensor.matmul(o_ps[:, 0, 0:D], hT_sb[parity][:, f, :],
                                         w2_sb[:, bass.ds(e * (FC * D) + f * D, D)],
                                         start=(f == 0), stop=(f == FC - 1))
                i.then_inc(y_done, 1)

            turn_xs(0)
            hidden(0, 0)
            turn_xs(1)

            def turn(t, parity):
                e = expert(t)
                hidden(t + 1, 1 - parity)
                if not isinstance(t, int) or t + 2 < MT:
                    turn_xs(t + 2)
                outputs(t, parity, e)

            expert_turns(pe, turn)
            outputs(MT - 1, (MT - 1) % 2, expert(MT - 1))
            attend(1)

        @block.scalar
        def _(act):
            def copy(out_, in_, s):
                nc.scalar.activation(out_, in_, ACT.Copy).then_inc(s, 1)

            def attend(l):
                s = L[l]

                def keep_xT(m):
                    act.wait_ge(s["xnT_done"], m + 1)
                    wait(act, s["q_done"], m)
                    copy(xnT_sb[:, :, :].rearrange("p c t -> p (c t)"), in_ps[:, 0:D], s["xnT_ev"])

                def keep_q(m, b):
                    act.wait_ge(s["q_done"], m + 1)
                    wait(act, s["scored"], 2 * m - 2)
                    nc.scalar.activation(qT_sb[:, b, 0, :], in_ps[:, 0:P], ACT.Identity, bias=cols[:, 4 * l:4 * l + 1])
                    nc.scalar.activation(qT_sb[:, b, 1, :], in_ps[:, P:2 * P], ACT.Identity,
                                         bias=cols[:, 4 * l + 1:4 * l + 2]).then_inc(s["q_ev"], 1)
                    if l == 1:
                        act.wait_ge(s["q_ev"], m + 1)
                        for h in range(2):
                            rows_ = slice(h * HALF, (h + 1) * HALF)
                            i = nc.scalar.activation(qparts[rows_, b, h:NQ:2, :], qT_sb[rows_, b, :, :], ACT.Copy)
                        i.then_inc(q_high, 1)

                keep_xT(0)
                keep_q(0, 0)
                if l == 0:
                    keep_weights(2, 4)
                    act.wait_ge(row_in, 16 * 5)
                    nc.scalar.activation(tg[:, :], tg[:, :], ACT.Tanh).then_inc(tg_ready, 1)
                    act.wait_ge(sm_done, 1)
                    copy(gwT[:, :, :].rearrange("p c e -> p (c e)"), out_ps[:, 0:DC * NE], sm_ev)
                    copy(b1T[:, :], out_ps[:, DC * NE:DC * NE + NE * FC], sm_ev)

                def step(j, k):
                    if l == 0 and isinstance(j, int) and 4 * j + k == UNITS + 8:
                        act.wait_ge(ar_done, 2 * DC)
                        copy(arT.rearrange("p b n -> p (b n)"), score_ps[:, 0, :], ar_ev)
                        copy(aiT.rearrange("p b n -> p (b n)"), score_ps[:, 1, :], ar_ev)
                    if k % 2 == 0:
                        m = 2 * j + k // 2 + 1
                        if tile_on(j, m):
                            keep_xT(m)
                        m, b = 2 * j + k // 2 - 3, (k // 2 + 1) % 2
                        if tile_on(j, m):
                            act.wait_ge(s["oT_done"], m + 1)
                            copy(oT_sb[:, b, :, :].rearrange("p c t -> p (c t)"), out_ps[:, 0:D], s["oT_ev"])
                    elif l == 0:
                        m = 2 * j + (k - 1) // 2 + 1
                        if tile_on(j, m):
                            keep_q(m, ((k - 1) // 2 + 1) % 2)
                    if unit_on(j, k, 1):
                        kk = (k - 1) % 4
                        act.wait_ge(subbed if l == 0 else s["s_taken"], 4 * j + k)
                        nc.scalar.activation(s_sb[:, kk, 0:UK], s_sb[:, kk, 0:UK], ACT.Exp).then_inc(s["exp_done"], 1)
                    if l == 1 and k % 2 == 0 and tile_on(j, 2 * j + k // 2 + 1):
                        keep_q(2 * j + k // 2 + 1, (k // 2 + 1) % 2)
                    if unit_on(j, k, 2):
                        act.wait_ge(s["pt_done"], 4 * j + k - 1)
                        wait(act, s["pv_done"], 4 * j + k - 3)
                        copy(pt_sb[0:TW, k % 2, :], pt_ps[0:TW, :, :].rearrange("p a n -> p (a n)")[:, 0:NW * P],
                             s["pt_ev"])
                    if k % 2 == 1:
                        m = 2 * j + (k - LAG_POST) // 2
                        if tile_on(j, m):
                            act.wait_ge(s["po_T"], m + 1)
                            wait(act, s["po_done"], m)
                            copy(po_xT.rearrange("p c t -> p (c t)"), out_ps[:, 0:D], s["po_ev"])

                attention_steps(act, step)

            act.dma_start(cols[:, 2:4], a["L0_xattn_bk"].rearrange("(c p) -> p c", c=DC),
                          allow_slow_non_contiguous=True).then_inc(col_in, 16)
            act.dma_start(cols[:, 0:2], a["L0_xattn_bq"].rearrange("(c p) -> p c", c=DC),
                          allow_slow_non_contiguous=True).then_inc(col_in, 16)
            act.dma_start(causal, a["c_all"][:, C_CAUSAL:C_ALL].rearrange("p (j k) -> p j k", j=NJ)
                          ).then_inc(pad_in, 16)
            act.dma_start(padraw.rearrange("p b k -> p (b k)"),
                          bcast(a["mask_BxS2_bf0"].rearrange("b k -> (b k)"))).then_inc(pad_in, 16)
            act.dma_start(rows[0:1, 0, :], bcast(a["L0_xattn_bv"])[0:1]).then_inc(col_in, 16)

            def keep_weights(first, last):
                for i in range(first, last):
                    act.wait_ge(wT_done, i + 1)
                    dst = (wkT, wq_sb[:, :, :], wvT, wo_sb[:, :, :])[i]
                    copy(dst.rearrange("p c n -> p (c n)"), w_banks[i], wT_ev)

            def keep_context(l):
                s = L[l]
                act.wait_ge(s["ctx_T"], 1)
                for r in range(CTX_COPIES):
                    i = nc.scalar.activation(ctxT[:, :, r * KEYS:(r + 1) * KEYS],
                                             score_ps[:, 1, 0:DC * B * KEYS].rearrange("p (c k) -> p c k", c=DC * B),
                                             ACT.Copy)
                i.then_inc(s["ctx_ev"], 1)

            keep_weights(0, 2)
            keep_context(0)
            act.wait_ge(col_in, 16 * 3)
            attend(0)

            act.wait_ge(m_done, 1)
            nc.scalar.activation(m_sb[:, :, :].rearrange("p c n -> p (c n)"), pt_ps[:, 0, :], ACT.Copy,
                                 scale=1.0 / D).then_inc(m_ready, 1)
            keep_context(1)

            def keep_xs(t):
                act.wait_ge(xsT_done, t + 1)
                wait(act, h_done, 2 * t)
                copy(xsT_sb[:, :, :].rearrange("p c t -> p (c t)"), in_ps[:, 0:D], xsT_ev)

            def relu(t, parity):
                e = act.value_load(tile_e[0:1, bass.ds(t, 1)], min_val=0, max_val=NE - 1)
                act.wait_ge(h_done, 2 * t + 1)
                wait(act, y_done, t - 1)
                for f in range(4):
                    i = nc.scalar.activation(hT_sb[parity][:, f, :], h_ps[parity][:, 0, f * P:(f + 1) * P], ACT.Relu,
                                             bias=b1T[:, bass.ds(e * FC + f, 1)])
                i.then_inc(hT_ev_a, 1)

            act.wait_ge(slots, 2)
            act.wait_ge(L[1]["kbd_ready"], QH)
            act.wait_ge(L[1]["v_ready"], B * DC)
            act.wait_ge(col1_in, 16 * 2)
            keep_xs(0)
            relu(0, 0)
            keep_xs(1)

            def turn(t, parity):
                relu(t + 1, 1 - parity)
                if not isinstance(t, int) or t + 2 < MT:
                    keep_xs(t + 2)

            expert_turns(act, turn)
            attend(1)

        @block.gpsimd
        def _(pool):
            def scatter(t):
                pool.wait_ge(xna_done, t + 1)
                nc.gpsimd.indirect_dma_start(out=xs_dram, out_offset=bass.IndirectOffsetOnAxis(slot_u[:, t:t + 1], 0),
                                             in_=xn_all[:, t, :], in_offset=None
                                             ).then_inc(scattered_first if t < W2_OVER else scattered, 16)

            def gather(m):
                t = m % B * NJ + m // B
                nc.gpsimd.indirect_dma_start(out=y_all[:, t, :], out_offset=None, in_=ys_dram,
                                             in_offset=bass.IndirectOffsetOnAxis(slot_u[:, t:t + 1], 0)
                                             ).then_inc(gathered[m // B], 16)

            def make_rstd(s, m, b, mv_, ve, rs, done, name):
                pool.wait_ge(s[name + "_mv"], m + 1)
                wait(pool, s[done], m - 1)
                nc.gpsimd.tensor_tensor(ve[:, b:b + 1], mv_[:, b, 1:2], power[:, 1:2], ALU.add
                                        ).then_inc(s[name + "_ve"], 1)
                pool.wait_ge(s[name + "_ve"], m + 1)
                nc.gpsimd.tensor_tensor(rs[:, b:b + 1], ve[:, b:b + 1], power[:, 0:1], ALU.pow
                                        ).then_inc(s[name + "_rs"], 1)

            def rstd_in(s, m, b):
                make_rstd(s, m, b, in_mv, in_ve, in_rs, "xn_done", "in")

            nc.gpsimd.memset(power[:, 0:1], -0.5)
            nc.gpsimd.memset(power[:, 1:2], EPS).then_inc(power_ready, 1)
            nc.gpsimd.memset(zero_sb, 0.0).then_inc(zero_ready, 1)
            pool.dma_start(tg[:, 0:4:2], bcast(a["g_xattn"]), allow_slow_non_contiguous=True).then_inc(row_in, 16)
            pool.dma_start(tg[:, 1:4:2], bcast(a["g_ffn"]), allow_slow_non_contiguous=True).then_inc(row_in, 16)
            for i, n in enumerate(("L0_xattn_bo", "L1_xattn_bo", "L1_ffn_bias")):
                pool.dma_start(rows[:, i + 1, :], bcast(a[n])).then_inc(row_in, 16)
            pool.wait_ge(pad_in, 16 * 2)
            nc.gpsimd.tensor_copy(padrow, padraw).then_inc(pads_read, 1)
            pool.wait_ge(pads_read, 1)
            for b in range(B):
                i = nc.gpsimd.tensor_tensor(pen[:, b, :, :], causal,
                                            padrow[:, b, :].unsqueeze(1).to_broadcast([P, NJ, KEYS]), ALU.add)
            i.then_inc(flags_made, 1)
            pool.wait_ge(power_ready, 1)
            for m in range(3):
                rstd_in(L[0], m, m % B)

            def penalize(j, b, c):
                if c == 0 and isinstance(j, int) and j < 4:
                    pool.wait_ge(bias_in[j // 2], 16 * B)
                elif c == 0:
                    pool.wait_ge(bias_ready, j // 2 + 1)
                v = bias_heads(j, b, c * UH, UH)[:, :, 0, :]
                nc.gpsimd.tensor_tensor(v, v, pen[:, b, bass.ds(j, 1), :].to_broadcast([P, UH, KEYS]),
                                        ALU.add).then_inc(pen_done, 1)

            def attend(l):
                s = L[l]

                def add_bo(j, b, m):
                    pool.wait_ge(s["xn_done"], m + 1)
                    xt = x_sb[:, bass.ds(b * NJ + j, 1), :]
                    nc.gpsimd.tensor_tensor(xt, xt, rows[:, 1 + l:2 + l, :], ALU.add).then_inc(s["xb_done"], 1)

                def step(j, k):
                    if l == 1 and isinstance(j, int):
                        if GATHERED_FIRST + 4 * j + k < NT:
                            gather(GATHERED_FIRST + 4 * j + k)
                    if k % 2 == 1:
                        m, b = 2 * j + (k - 7) // 2, (k - 7) // 2 % 2
                        if tile_on(j, m):
                            make_rstd(s, m, b, po_mv, po_ve, po_rs, "po_xn", "po")
                            if l == 0:
                                jm = j + (k - 7) // 4
                                pool.wait_ge(s["po_rs"], m + 1)
                                nc.gpsimd.tensor_copy(mean_all[:, bass.ds(b * NJ + jm, 1)], po_mv[:, b, 0:1])
                                nc.gpsimd.tensor_copy(rstd_all[:, bass.ds(b * NJ + jm, 1)],
                                                      po_rs[:, b:b + 1]).then_inc(kept, 1)
                    if l == 0 and unit_on(j, k):
                        pool.wait_ge(s["maxed"], 4 * j + k + 1)
                        v = s_sb[:, k, 0:UK].rearrange("p (h k) -> p h k", h=UH)
                        nc.gpsimd.tensor_tensor(v, v, mx_sb[:, k, :].unsqueeze(2).to_broadcast([P, UH, KEYS]),
                                                ALU.subtract).then_inc(subbed, 1)
                    if k % 2 == 0:
                        m = 2 * j + k // 2 + 3
                        if tile_on(j, m):
                            rstd_in(s, m, (k // 2 + 1) % 2)
                    if k % 2 == 1:
                        m, b = 2 * j + (k - 1) // 2 + 2, k // 2
                        if tile_on(j, m):
                            add_bo(j + 1, b, m)
                        m, b = 2 * j + (k - LAG_POST) // 2, (k - LAG_POST) // 2 % 2
                        if l == 1 and tile_on(j, m):
                            pool.wait_ge(s["po_xn"], m + 1)
                            xt = x_sb[:, bass.ds(b * NJ + j + (k - LAG_POST) // 4, 1), :]
                            nc.gpsimd.tensor_tensor(xt, xt, rows[:, 3:4, :], ALU.add).then_inc(fb_done, 1)
                    if l == 0 and tile_on(j, 2 * j + k // 2 + 2):
                        penalize(j + 1, k // 2, k % 2)

                if l == 0:
                    pool.wait_ge(pen_made, 1)
                    for b in range(B):
                        for c in range(2):
                            penalize(0, b, c)
                    pool.wait_ge(L[0]["ctx_T"], 1)
                    pool.wait_ge(sm_done, 1)
                pool.wait_ge(y_out, 16 * MT) if l == 1 else None
                nc.gpsimd.memset(s_pad, 0.0).then_inc(pads_ready, 1)
                pool.wait_ge(rows_ready, 3)
                add_bo(0, 0, 0)
                add_bo(0, 1, 1)
                attention_steps(pool, step)

            attend(0)
            pool.wait_ge(slots, 2)
            pool.wait_ge(zeroed, 16)
            for t in range(NT):
                scatter(t)

            def store_y(t):
                pool.wait_ge(y_ev, t + 1)
                pool.dma_start(ys_dram[bass.ds(t * P, P), :], y_sb).then_inc(y_out, 16)

            def load_b2(t):
                e = pool.value_load(tile_e[0:1, bass.ds(t, 1)], min_val=0, max_val=NE - 1)
                pool.dma_start(b2t_sb[:, :], a["L0_ffn_b2"][bass.ds(e, 1), :].to_broadcast([P, D])).then_inc(b2_in, 16)

            pool.wait_ge(L[0]["po_done"], NT)
            load_b2(0)
            with pool.Fori(0, MT - 1) as t:
                store_y(t)
                load_b2(t + 1)
            store_y(MT - 1)
            pool.wait_ge(y_out, 16 * MT)
            for m in range(GATHERED_FIRST):
                gather(m)
                if m >= GATHERED_FIRST - 3:
                    rstd_in(L[1], m - GATHERED_FIRST + 3, (m - GATHERED_FIRST + 3) % B)
            attend(1)

        @block.vector
        def _(dve):
            steps = [0]

            def link(i):
                steps[0] += 1
                i.then_inc(dve_step, 1)
                dve.wait_ge(dve_step, steps[0])

            def add_y(j, b, m):
                xt = x_sb[:, bass.ds(b * NJ + j, 1), :]
                dve.wait_ge(y_ready, m + 1)
                nc.vector.scalar_tensor_tensor(out=xt, in0=y_all[:, bass.ds(b * NJ + j, 1), :], scalar=tg[:, 1:2],
                                               in1=xt, op0=ALU.mult, op1=ALU.add).then_inc(in_x, 1)
                dve.wait_ge(in_x, m + 1)

            def stats_in(s, j, b, m):
                nc.vector.bn_stats(in_st[:, b, :], x_sb[:, bass.ds(b * NJ + j, 1), :]).then_inc(s["in_st"], 1)
                dve.wait_ge(s["in_st"], m + 1)

            def aggregate_in(s, b):
                nc.vector.bn_aggr(in_mv[:, b, :], in_st[:, b, :]).then_inc(s["in_mv"], 1)

            def first_stats(l):
                for m in range(3):
                    if m == 2:
                        norm_x(l, 0, 0, 0)
                        norm_x(l, 0, 1, 1)
                        dve.wait_ge(L[l]["xn_done"], 1)
                    if l == 1:
                        add_y(m // B, m % B, m)
                    stats_in(L[l], m // B, m % B, m)
                    aggregate_in(L[l], m % B)

            def norm_x(l, j, b, m):
                s = L[l]
                dve.wait_ge(s["in_rs"], m + 1)
                wait(dve, s["xnT_done"], m - 1)
                nc.vector.tensor_scalar(xn_sb[:, b:b + 1, :], x_sb[:, bass.ds(b * NJ + j, 1), :],
                                        in_mv[:, b, 0:1], in_rs[:, b:b + 1],
                                        ALU.subtract, ALU.mult).then_inc(s["xn_done"], 1)

            def prepare(l):
                s = L[l]
                dve.wait_ge(s["k_done"], 1)
                if l == 0:
                    dve.wait_ge(cst_in, 16)
                    dve.wait_ge(col_in, 16 * 3)
                else:
                    dve.wait_ge(col1_in, 16 * 2)
                for c in range(DC):
                    i = nc.vector.tensor_scalar(kb_sb[:, c, :], score_ps[:, 0, c * B * KEYS:(c + 1) * B * KEYS],
                                                cols[:, 4 * l + 2 + c:4 * l + 3 + c], HD ** -0.5, ALU.add, ALU.mult)
                link(i)
                if l == 1:
                    for h in range(2):
                        for half in range(2):
                            nc.vector.tensor_copy(
                                kb2[half * HALF:(half + 1) * HALF, h:NQ:2, :, :].rearrange("p g b k -> p g (b k)"),
                                kb_sb[h * HALF:(h + 1) * HALF, :, :]).then_inc(s["kbd_ready"], 1)
                    return
                for h in range(QH):
                    nc.vector.tensor_scalar(kbd[:, :, :, h, :].rearrange("p c b k -> p (c b) k"),
                                            kb_sb.rearrange("p c (b k) -> p (c b) k", b=B),
                                            cst[:, C_KM + h:C_KM + h + 1], None, ALU.mult).then_inc(s["kbd_ready"], 1)

            def prepare_values(l, b):
                s = L[l]
                vmask = cst[0:TW, C_VM:C_VM + NW * WH].rearrange("p (w h) -> p w h", w=NW)
                dve.wait_ge(s["v_done"], b + 1)
                for c in range(DC):
                    if l == 0 and c == 0:
                        nc.vector.tensor_copy(vblk[0:TW, b, :, :, :, HD],
                                              vmask.unsqueeze(2).to_broadcast([TW, NW, DC, WH])
                                              ).then_inc(s["v_ready"], 1)
                    pv = v_bank(l, b)[0:TW, 0:NW * DC * WH * HD].rearrange("p (w c h d) -> p w c h d", w=NW, c=DC, h=WH)
                    nc.vector.tensor_tensor(vblk[0:TW, b, :, c, :, 0:HD], pv[:, :, c, :, :],
                                            vmask.unsqueeze(3).to_broadcast([TW, NW, WH, HD]),
                                            ALU.mult).then_inc(s["v_ready"], 1)

            dve.wait_ge(x_in[0], 16 * B)
            first_stats(0)
            prepare(0)
            dve.wait_ge(flags_made, 1)
            link(nc.vector.tensor_reduce(no_key[:, :], pen.rearrange("p b j k -> p (b j) k"), AX_X, ALU.min))
            nc.vector.tensor_scalar(pen.rearrange("p b j k -> p (b j k)"), pen.rearrange("p b j k -> p (b j k)"),
                                    MASKED, None, ALU.mult).then_inc(pen_made, 1)
            dve.wait_ge(tg_ready, 1)
            for i, g in ((1, 0), (2, 2), (3, 3)):
                nc.vector.tensor_scalar(rows[:, i, :], rows[:, i, :], tg[:, g:g + 1], None, ALU.mult
                                        ).then_inc(rows_ready, 1)
            link(nc.vector.tensor_scalar(no_key[:, :], no_key[:, :], 3e38, 10.0, ALU.mult, ALU.mult))
            link(nc.vector.tensor_scalar(no_key[:, :], no_key[:, :], 0.0, None, ALU.mult))
            dve.wait_ge(small_in, 16 * 4)

            def attend(l):
                s = L[l]
                dve.wait_ge(pads_ready, l + 1)

                def leave(j, k):
                    m, b = 2 * j + (k - 7) // 2, (k - 7) // 2 % 2
                    if tile_on(j, m):
                        xt = x_sb[:, bass.ds(b * NJ + j + (k - 7) // 4, 1), :]
                        dve.wait_ge(s["wo_done"], m + 1)
                        dve.wait_ge(s["xb_done"], m + 1)
                        nc.vector.scalar_tensor_tensor(
                            out=xt, in0=out_ps[:, 0:D].unsqueeze(1), scalar=tg[:, 2 * l:2 * l + 1], in1=xt,
                            op0=ALU.mult, op1=ALU.add).then_inc(s["resid"], 1)
                    m, b = 2 * j + (k - 11) // 2, (k - 11) // 2 % 2
                    if tile_on(j, m):
                        t = b * NJ + j + (k - 11) // 4
                        dve.wait_ge(s["po_done"], m + 1)
                        if l == 0:
                            nc.vector.tensor_tensor(logit[:, bass.ds(t, 1), :], out_ps[:, D:D + NE].unsqueeze(1),
                                                    gb[:, 0:1, :], ALU.add).then_inc(s["po_read"], 1)
                        else:
                            xt = x_sb[:, bass.ds(t, 1), :]
                            dve.wait_ge(fb_done, m + 1)
                            nc.vector.scalar_tensor_tensor(
                                out=xt, in0=out_ps[:, D:2 * D].unsqueeze(1), scalar=tg[:, 3:4], in1=xt,
                                op0=ALU.mult, op1=ALU.add).then_inc(s["po_read"], 1)
                    if tile_on(j, 2 * j + (k - 7) // 2):
                        dve.wait_ge(s["resid"], 2 * j + (k - 7) // 2 + 1)

                def divide(j, k):
                    m, b = 2 * j + (k - 1) // 2 - 2, (k - 1) // 2
                    if tile_on(j, m):
                        ov = o_ps[:, b, 0:HEADS * HV].rearrange("p (h e) -> p h e", e=HV)
                        dve.wait_ge(s["pv_done"], 2 * m + 2)
                        nc.vector.reciprocal(rs_sb[:, :], ov[:, :, HD]).then_inc(s["rs_ready"], 1)
                        dve.wait_ge(s["rs_ready"], m + 1)
                        wait(dve, s["oT_done"], m - 1)
                        onv = on_sb[:, b, :].rearrange("p (h d) -> p h d", d=HD)
                        rsv = rs_sb[:, :].unsqueeze(2).to_broadcast([P, HEADS, HD])
                        if l == 0:
                            nc.vector.scalar_tensor_tensor(
                                out=onv, in0=ov[:, :, 0:HD], scalar=no_key[:, bass.ds(b * NJ + j - 1, 1)],
                                in1=rsv, op0=ALU.add, op1=ALU.mult).then_inc(s["on_done"], 1)
                        else:
                            nc.vector.tensor_tensor(onv, ov[:, :, 0:HD], rsv, ALU.mult).then_inc(s["on_done"], 1)

                def softmax(j, k, part):
                    c, b = k % 2, k // 2
                    sv = s_sb[:, k, 0:UK].rearrange("p (q h k) -> p q h k", q=2, h=QH)
                    pv = score_ps[:, :, 0:QK].rearrange("p q (h k) -> p q h k", h=QH)
                    mq = mx_sb[:, k, :].rearrange("p (q h) -> p q h", q=2)
                    if part == 0:
                        dve.wait_ge(s["scored"], 4 * j + k + 1)
                    if part == 0 and l == 0:
                        wait(dve, s["pt_done"], 4 * j + k - 3)
                        dve.wait_ge(pen_done, 4 * j + k + 1)
                        nc.vector.tensor_tensor(
                            sv, pv, bias_heads(j, b, UH * c, UH).rearrange("p (q h) i k -> p q h (i k)", q=2),
                            ALU.add).then_inc(s["s_taken"], 1)
                    elif part == 0:
                        nc.vector.tensor_reduce(mq, pv, AX_X, ALU.max).then_inc(s["maxed"], 1)
                    elif l == 0:
                        dve.wait_ge(s["s_taken"], 4 * j + k + 1)
                        wait(dve, subbed, 4 * j + k - 3)
                        nc.vector.tensor_reduce(mx_sb[:, k, :], s_sb[:, k, 0:UK].rearrange("p (h k) -> p h k", h=UH),
                                                AX_X, ALU.max).then_inc(s["maxed"], 1)
                    else:
                        dve.wait_ge(s["maxed"], 4 * j + k + 1)
                        wait(dve, s["pt_done"], 4 * j + k - 3)
                        nc.vector.tensor_tensor(
                            sv, pv, mq.unsqueeze(3).to_broadcast([P, 2, QH, KEYS]), ALU.subtract
                        ).then_inc(s["s_taken"], 1)

                def lower(m, b):
                    dve.wait_ge(q_high, m + 1)
                    for h in range(2):
                        rows_, other = slice(h * HALF, (h + 1) * HALF), slice((1 - h) * HALF, (2 - h) * HALF)
                        i = nc.vector.tensor_tensor(qparts[other, b, h:NQ:2, :], qT_sb[rows_, b, :, :],
                                                    qparts[rows_, b, h:NQ:2, :].bitcast(F32), ALU.subtract)
                    i.then_inc(q_low, 1)

                if l == 1:
                    lower(0, 0)

                def step(j, k):
                    if l == 1 and k % 2 == 1 and tile_on(j, 2 * j + (k - 1) // 2 + 1):
                        lower(2 * j + (k - 1) // 2 + 1, ((k - 1) // 2 + 1) % 2)
                    ahead, ahead_b = 2 * j + k // 2 + 3, (k // 2 + 1) % 2
                    ahead_j = j + 1 + (k // 2 + 1) // 2
                    normed = 2 * j + k // 2 + 2
                    after, after_b = 2 * j + (k - 7) // 2, (k - 7) // 2 % 2

                    def statistics():
                        if k % 2 == 0 and tile_on(j, ahead):
                            if l == 0 and isinstance(j, int) and ahead in (4, 8):
                                dve.wait_ge(x_in[ahead // 4], 16 * B)
                            stats_in(s, ahead_j, ahead_b, ahead)
                        if k % 2 == 1 and tile_on(j, after):
                            t = after_b * NJ + j + (k - 7) // 4
                            nc.vector.bn_stats(po_st[:, after_b, :], x_sb[:, bass.ds(t, 1), :]).then_inc(s["po_st"], 1)
                            dve.wait_ge(s["po_st"], after + 1)

                    if l == 0 and isinstance(j, int) and 4 * j + k in (2, 3):
                        prepare_values(0, k - 2)
                    if k % 2 == 0 and l == 1 and tile_on(j, ahead):
                        add_y(ahead_j, ahead_b, ahead)
                    if k % 2 == 0 and l == 1 and tile_on(j, normed):
                        norm_x(l, j + 1, k // 2, normed)
                    if k % 2 == 1:
                        leave(j, k)
                    if k % 2 == 1 and l == 0:
                        divide(j, k)
                    if k % 2 == 0 and l == 1:
                        statistics()
                    if unit_on(j, k):
                        softmax(j, k, 0)
                    if l == 0:
                        statistics()
                    if unit_on(j, k):
                        softmax(j, k, 1)
                    if k % 2 == 1 and l == 1:
                        statistics()
                        divide(j, k)
                    if k % 2 == 0 and tile_on(j, ahead):
                        aggregate_in(s, ahead_b)
                    if k % 2 == 1 and tile_on(j, after):
                        nc.vector.bn_aggr(po_mv[:, after_b, :], po_st[:, after_b, :]).then_inc(s["po_mv"], 1)
                    if k % 2 == 0:
                        if l == 0 and tile_on(j, normed):
                            norm_x(l, j + 1, k // 2, normed)
                        m, b = 2 * j + (k - 8) // 2, (k - 8) // 2 % 2
                        if tile_on(j, m):
                            t = b * NJ + j + (k - 8) // 4
                            dve.wait_ge(s["po_rs"], m + 1)
                            wait(dve, s["po_T"], m)
                            if l == 0:
                                wait(dve, kept, m)
                            if l == 0 and isinstance(j, int) and m == 0:
                                dve.wait_ge(zeroed, 16)
                            nc.vector.tensor_scalar(po_x.unsqueeze(1), x_sb[:, bass.ds(t, 1), :],
                                                    po_mv[:, b, 0:1], po_rs[:, b:b + 1],
                                                    ALU.subtract, ALU.mult).then_inc(s["po_xn"], 1)

                attention_steps(dve, step)

            attend(0)

            def te(i):
                return rt[:, i, :].rearrange("p (t e) -> p t e", e=NE)

            def et(i):
                return rt[:, i, :].rearrange("p (e t) -> p e t", e=NE)

            def c8(at):
                return cst[:, at:at + NE].unsqueeze(1).to_broadcast([P, NT, NE])

            dve.wait_ge(L[0]["po_read"], NT)
            dve.wait_ge(pen_done, UNITS)
            link(nc.vector.tensor_tensor(te(0), logit[:, :, :], gb[:, 1, :].unsqueeze(1).to_broadcast([P, NT, NE]),
                                         ALU.add))
            top = rt[:, 3, 0:NT]
            link(nc.vector.tensor_reduce(top, te(0), AX_X, ALU.max))
            link(nc.vector.tensor_tensor(te(1), te(0), top.unsqueeze(2).to_broadcast([P, NT, NE]), ALU.is_equal))
            link(nc.vector.tensor_tensor(te(1), te(1), c8(C_RANK), ALU.mult))
            link(nc.vector.tensor_tensor(te(1), te(1), c8(C_LAST), ALU.max))
            link(nc.vector.tensor_reduce(top, te(1), AX_X, ALU.max))
            nc.vector.tensor_tensor(te(2), te(1), top.unsqueeze(2).to_broadcast([P, NT, NE]),
                                    ALU.is_equal).then_inc(hot, 1)
            dve.wait_ge(ranked, 1)
            link(nc.vector.tensor_copy(et(4), o_ps[:, 1, P:2 * P].rearrange("p (t e) -> p e t", e=NE)))
            link(nc.vector.tensor_tensor_scan(rt[:, 5, :], cst[:, C_RESET:C_RESET + P], rt[:, 4, :], 0.0,
                                              ALU.mult, ALU.add))
            link(nc.vector.tensor_tensor(et(6), et(5)[:, :, NT - 1:NT].to_broadcast([P, NE, NT]),
                                         cst[:, C_THR:C_THR + NT].unsqueeze(1).to_broadcast([P, NE, NT]),
                                         ALU.is_gt))
            n_tiles, ends, start = rt[:, 7, 0:NE], rt[:, 7, 16:16 + NE], rt[:, 7, 32:32 + NE]
            link(nc.vector.tensor_reduce(n_tiles, et(6), AX_X, ALU.add))
            link(nc.vector.tensor_tensor_scan(ends, cst[:, C_ONE:C_ONE + NE], n_tiles, 0.0, ALU.mult, ALU.add))
            link(nc.vector.tensor_tensor(start, ends, n_tiles, ALU.subtract))
            link(nc.vector.tensor_scalar(start, start, float(P), None, ALU.mult))
            link(nc.vector.tensor_tensor(rt[:, 5, :], rt[:, 5, :], rt[:, 4, :], ALU.subtract))
            link(nc.vector.tensor_tensor(et(5), et(5), start.unsqueeze(2).to_broadcast([P, NE, NT]), ALU.add))
            link(nc.vector.tensor_tensor(te(8), o_ps[:, 1, 0:P].rearrange("p (t e) -> p t e", e=NE),
                                         rt[:, 5, :].rearrange("p (e t) -> p t e", e=NE), ALU.add))
            link(nc.vector.tensor_tensor(te(8), te(8), te(2), ALU.mult))
            link(nc.vector.tensor_reduce(top, te(8), AX_X, ALU.add))
            link(nc.vector.tensor_copy(slot_u[:, :], top))
            cmp_ = rt[:, 9:11, :].rearrange("p i n -> p (i n)")[:, 0:MT * (NE - 1)].rearrange("p (t e) -> p t e", t=MT)
            link(nc.vector.tensor_tensor(cmp_, cst[:, C_TILE:C_TILE + MT].unsqueeze(2).to_broadcast([P, MT, NE - 1]),
                                         ends[:, 0:NE - 1].unsqueeze(1).to_broadcast([P, MT, NE - 1]), ALU.is_ge))
            link(nc.vector.tensor_reduce(rt[:, 11, 0:MT], cmp_, AX_X, ALU.add))
            nc.vector.tensor_copy(tile_e[:, 0:MT], rt[:, 11, 0:MT]).then_inc(slots, 2)
            dve.wait_ge(kept, NT)
            for t in range(NT):
                if t == XN_CLEAR:
                    dve.wait_ge(m_done, 1)
                nc.vector.tensor_scalar(xn_all[:, t, :], x_sb[:, t, :], mean_all[:, t:t + 1], rstd_all[:, t:t + 1],
                                        ALU.subtract, ALU.mult).then_inc(xna_done, 1)

            prepare(1)
            for b in range(B):
                prepare_values(1, b)

            def relu(t, parity):
                e = dve.value_load(tile_e[0:1, bass.ds(t, 1)], min_val=0, max_val=NE - 1)
                dve.wait_ge(h_done, 2 * t + 2)
                wait(dve, y_done, t - 1)
                for f in range(4, FC):
                    i = nc.vector.tensor_scalar(hT_sb[parity][:, f, :], h_ps[parity][:, 1, (f - 4) * P:(f - 3) * P],
                                                b1T[:, bass.ds(e * FC + f, 1)], 0.0, ALU.add, ALU.max)
                i.then_inc(hT_ev_v, 1)

            def keep_y(t):
                dve.wait_ge(y_done, t + 1)
                dve.wait_ge(b2_in, 16 * (t + 1))
                wait(dve, y_out, 16 * t)
                nc.vector.tensor_tensor(y_sb, o_ps[:, 0, 0:D], b2t_sb[:, :], ALU.add).then_inc(y_ev, 1)

            dve.wait_ge(dft_in, 16 * 5)
            dve.wait_ge(m_done, 1)
            dve.wait_ge(L[1]["ctx_T"], 1)
            relu(0, 0)

            def turn(t, parity):
                relu(t + 1, 1 - parity)
                keep_y(t)

            expert_turns(dve, turn)
            keep_y(MT - 1)
            for part in range(2):
                for h in range(QH):
                    mask = cst[:, C_KM + h:C_KM + h + 1]
                    high, low = [kparts[:, i, :, :, h * KEYS:(h + 1) * KEYS] for i in range(2)]
                    if part == 0:
                        nc.vector.tensor_scalar(high, kb2, mask, None, ALU.mult).then_inc(kparts_ready, 1)
                    else:
                        dve.wait_ge(kparts_ready, QH + h)
                        nc.vector.scalar_tensor_tensor(out=low, in0=kb2, scalar=mask, in1=high.bitcast(F32),
                                                       op0=ALU.mult, op1=ALU.subtract).then_inc(kparts_ready, 1)
            first_stats(1)
            attend(1)


_INS = ['x', 'ctx_1024', 'fside_Bx16xSxS2_0', 'mask_BxS2_bf0', 'g_xattn', 'g_ffn',
        'L0_xattn_wq', 'L0_xattn_bq', 'L0_xattn_wk', 'L0_xattn_bk', 'L0_xattn_wv', 'L0_xattn_bv',
        'L0_xattn_wo', 'L0_xattn_bo', 'L0_ffn_gate_w', 'L0_ffn_gate_b', 'L0_ffn_expert_bias',
        'L0_ffn_w1', 'L0_ffn_b1', 'L0_ffn_w2', 'L0_ffn_b2',
        'L1_xattn_Wq', 'L1_xattn_bq', 'L1_xattn_Wk', 'L1_xattn_bk', 'L1_xattn_Wv', 'L1_xattn_bv',
        'L1_xattn_Wo', 'L1_xattn_bo', 'L1_ffn_w_freq_real', 'L1_ffn_w_freq_imag', 'L1_ffn_bias']


def _constants():
    import numpy as np
    c = np.zeros((P, C_ALL), np.float32)
    p = np.arange(P)
    c[:, C_ID:C_ID + P] = np.eye(P)
    c[:, C_TRI:C_TRI + P] = p[:, None] < p[None, :]
    c[:, C_ONE:C_ONE + P] = 1.0
    c[:, C_KM:C_KM + QH] = (p[:, None] % 64) // HD == np.arange(QH)
    for w in range(NW):
        head = (w * TW + p[:TW, None]) // KEYS
        c[:TW, C_VM + w * WH:C_VM + (w + 1) * WH] = head == FIRST_HEAD[w] + np.arange(WH)
    c[:, C_RANK:C_RANK + NE] = NE - np.arange(NE)
    c[:, C_LAST + NE - 1] = 1.0
    c[:, C_RESET:C_RESET + P] = p % NT != 0
    c[:, C_THR:C_THR + NT] = P * np.arange(NT)
    c[:, C_TILE:C_TILE + MT] = np.arange(MT)
    query = p[:, None, None] * NJ + np.arange(NJ)[None, :, None]
    c[:, C_CAUSAL:C_ALL] = np.where(np.arange(KEYS)[None, None, :] > query, 1.0, 0.0).reshape(P, -1)
    angle = 2 * np.pi * (np.outer(np.arange(D), np.arange(D)) % D) / D
    dft = np.stack([np.cos(angle), np.sin(angle), -np.sin(angle)]).astype(np.float32)
    return c, dft


def kernel(**inputs):
    import numpy as _np
    import concourse.bacc as _bacc
    from concourse import mybir as _mybir
    from concourse.bass_utils import run_bass_kernel_spmd as _run

    nc = _bacc.Bacc("TRN2", target_bir_lowering=False, num_devices=1)
    arrays, args = {}, {}
    c_all, c_dft = _constants()
    for name, value in [(n, inputs[n]) for n in _INS] + [("c_all", c_all), ("c_dft", c_dft)]:
        v = _np.ascontiguousarray(value)
        arrays[f"in_{name}_dram"] = v
        args[name] = nc.dram_tensor(f"in_{name}_dram", v.shape, _mybir.dt.from_np(v.dtype), kind="ExternalInput").ap()
    out = nc.dram_tensor("out_0_dram", (B, S, D), F32, kind="ExternalOutput").ap()
    flamingo_kernel(nc, args, out)
    r = _run(nc, [arrays], core_ids=[0])
    return r.results[0]["out_0_dram"]
```
